# Optimizing a Trainium2 kernel written in Bass

```python
import numpy as np
import jax
import jax.numpy as jnp

def _softmax(x, axis=-1):
    return jax.nn.softmax(x, axis=axis)

def _gelu(x):
    return jax.nn.gelu(x, approximate=True)

def _silu(x):
    return jax.nn.silu(x)

def _sigmoid(x):
    return jax.nn.sigmoid(x)

def _layernorm(x, axis=-1, eps=1e-05):
    m = jnp.mean(x, axis=axis, keepdims=True)
    v = jnp.var(x, axis=axis, keepdims=True)
    return (x - m) / jnp.sqrt(v + eps)

def _scatter_add(tgt, idx, src, axis=0):
    return tgt.at[idx].add(src)

def _segment_sum(src, seg, n):
    return jax.ops.segment_sum(src, seg, n)
kernel_name = 'mk_gnn_ffn_d2_gnn_r8_e4cc66'

def setup_inputs(seed: int=0):
    np.random.seed(seed)
    _w = jnp.asarray

    def _rec_inputs():
        import jax
        import jax.numpy as jnp
        _gk = jax.random.key(seed)
        x = -0.0003713 + 1 * jax.random.normal(jax.random.fold_in(_gk, 1), (6250, 256), jnp.float32)
        src = jax.random.randint(jax.random.fold_in(_gk, 2), (200000,), 0, 6250, jnp.int32)
        dst = jax.random.randint(jax.random.fold_in(_gk, 3), (200000,), 0, 6250, jnp.int32)
        _o = jnp.argsort(dst, stable=True)
        src = src[_o]
        dst = dst[_o]
        return (x, src, dst)
    x, src, dst = _rec_inputs()

    def _L0_gnn_setup():
        import jax, jax.numpy as jnp
        import numpy as np
        N_NODES = 6250
        N_EDGES = 200000
        IN_FEATS = 256
        HIDDEN = 512
        OUT_FEATS = 256
        EPS = 0.0
        key = jax.random.key(seed)
        ks = jax.random.split(key, 6)
        x = jax.random.normal(ks[0], (N_NODES, IN_FEATS), dtype=jnp.float32)
        edge_row = jax.random.randint(ks[1], (N_EDGES,), 0, N_NODES, dtype=jnp.int32)
        edge_col = jax.random.randint(ks[2], (N_EDGES,), 0, N_NODES, dtype=jnp.int32)
        W1 = jax.random.uniform(ks[3], (IN_FEATS, HIDDEN), dtype=jnp.float32, minval=-1.0 / np.sqrt(IN_FEATS), maxval=1.0 / np.sqrt(IN_FEATS))
        b1 = jnp.zeros((HIDDEN,), dtype=jnp.float32)
        W2 = jax.random.uniform(ks[4], (HIDDEN, OUT_FEATS), dtype=jnp.float32, minval=-1.0 / np.sqrt(HIDDEN), maxval=1.0 / np.sqrt(HIDDEN))
        b2 = jnp.zeros((OUT_FEATS,), dtype=jnp.float32)
        return {'x': x, 'edge_row': edge_row, 'edge_col': edge_col, 'W1': W1, 'b1': b1, 'W2': W2, 'b2': b2}
    _L0_gnn_all = _L0_gnn_setup()
    _L0_gnn_in = {k: v for k, v in _L0_gnn_all.items() if k in ('W1', 'b1', 'W2', 'b2')}
    del _L0_gnn_all

    def _L0_ffn_setup():
        import jax, jax.numpy as jnp
        import numpy as np
        BN_EPS = 0.001

        def _bn(h, g, b, m, v):
            return g * (h - m) * jax.lax.rsqrt(v + BN_EPS) + b
        key = jax.random.key(seed)
        ks = jax.random.split(key, 8)
        B, F, Df = (256, 64, 256)
        E, H, D = (8, 256, 256)
        s1 = 1.0 / np.sqrt(Df)
        s2 = 1.0 / np.sqrt(H)
        return {'x': jax.random.normal(ks[0], (B, F, Df), jnp.float32), 'Wr': jax.random.normal(ks[1], (Df, E), jnp.float32) * s1, 'br': jnp.zeros((E,), jnp.float32), 'W1': jax.random.normal(ks[2], (E, Df, H), jnp.float32) * s1, 'b1': jnp.zeros((E, H), jnp.float32), 'g1': jnp.ones((E, H), jnp.float32), 'be1': jnp.zeros((E, H), jnp.float32), 'm1': jnp.zeros((E, H), jnp.float32), 'v1': jnp.ones((E, H), jnp.float32), 'W2': jax.random.normal(ks[3], (E, H, H), jnp.float32) * s2, 'b2': jnp.zeros((E, H), jnp.float32), 'g2': jnp.ones((E, H), jnp.float32), 'be2': jnp.zeros((E, H), jnp.float32), 'm2': jnp.zeros((E, H), jnp.float32), 'v2': jnp.ones((E, H), jnp.float32), 'Wo': jax.random.normal(ks[4], (E, H, D), jnp.float32) * s2, 'bo': jnp.zeros((E, D), jnp.float32)}
    _L0_ffn_all = _L0_ffn_setup()
    _L0_ffn_in = {k: v for k, v in _L0_ffn_all.items() if k in ('Wr', 'br', 'W1', 'b1', 'g1', 'be1', 'm1', 'v1', 'W2', 'b2', 'g2', 'be2', 'm2', 'v2', 'Wo', 'bo')}
    del _L0_ffn_all

    def _L1_gnn_setup():
        import jax, jax.numpy as jnp
        import numpy as np
        N, E = (6250, 100000)
        D_IN, D_OUT, H = (256, 64, 4)
        NEG_SLOPE = 0.01

        def _segment_softmax(z, seg, n):
            m = jax.ops.segment_max(z, seg, num_segments=n)
            ez = jnp.exp(z - m[seg])
            denom = jax.ops.segment_sum(ez, seg, num_segments=n)
            return ez / jnp.maximum(denom[seg], 1e-09)
        key = jax.random.key(seed)
        ks = jax.random.split(key, 7)
        s = 0.1
        return {'features': jax.random.normal(ks[0], (N, D_IN), jnp.float32), 'src': jax.random.randint(ks[1], (E,), 0, N), 'dst': jax.random.randint(ks[2], (E,), 0, N), 'W_fc': jax.random.normal(ks[3], (H, D_IN, D_OUT), jnp.float32) * s, 'W_al': jax.random.normal(ks[4], (H, D_OUT, 1), jnp.float32) * s, 'W_ar': jax.random.normal(ks[5], (H, D_OUT, 1), jnp.float32) * s, 'W_res': jax.random.normal(ks[6], (H, D_IN, D_OUT), jnp.float32) * s}
    _L1_gnn_all = _L1_gnn_setup()
    _L1_gnn_in = {k: v for k, v in _L1_gnn_all.items() if k in ('W_fc', 'W_al', 'W_ar', 'W_res')}
    del _L1_gnn_all

    def _L1_ffn_setup():
        import math
        import jax, jax.numpy as jnp
        import numpy as np
        CAPACITY_FACTOR = 1.25
        TOP_K = 2
        LN_EPS = 1e-05

        def _layer_norm(x, gamma, beta):
            mu = jnp.mean(x, axis=-1, keepdims=True)
            var = jnp.var(x, axis=-1, keepdims=True)
            return (x - mu) * jax.lax.rsqrt(var + LN_EPS) * gamma + beta
        key = jax.random.key(seed)
        ks = jax.random.split(key, 4)
        B, S, D, F, E = (8, 512, 256, 512, 8)
        x = jax.random.normal(ks[0], (B, S, D), dtype=jnp.float32)
        Wr = jax.random.normal(ks[1], (D, E), dtype=jnp.float32) / np.sqrt(D)
        br = jnp.zeros((E,), jnp.float32)
        W1 = jax.random.normal(ks[2], (E, D, F), dtype=jnp.float32) / np.sqrt(D)
        b1 = jnp.zeros((E, F), jnp.float32)
        W2 = jax.random.normal(ks[3], (E, F, D), dtype=jnp.float32) / np.sqrt(F)
        b2 = jnp.zeros((E, D), jnp.float32)
        gamma = jnp.ones((D,), jnp.float32)
        beta = jnp.zeros((D,), jnp.float32)
        return {'x': x, 'Wr': Wr, 'br': br, 'W1': W1, 'b1': b1, 'W2': W2, 'b2': b2, 'gamma': gamma, 'beta': beta}
    _L1_ffn_all = _L1_ffn_setup()
    _L1_ffn_in = {k: v for k, v in _L1_ffn_all.items() if k in ('Wr', 'br', 'W1', 'b1', 'W2', 'b2', 'gamma', 'beta')}
    del _L1_ffn_all
    return {'x': x, 'src': src, 'dst': dst, 'L0_gnn_W1': _L0_gnn_in['W1'], 'L0_gnn_b1': _L0_gnn_in['b1'], 'L0_gnn_W2': _L0_gnn_in['W2'], 'L0_gnn_b2': _L0_gnn_in['b2'], 'L0_ffn_Wr': _L0_ffn_in['Wr'], 'L0_ffn_br': _L0_ffn_in['br'], 'L0_ffn_W1': _L0_ffn_in['W1'], 'L0_ffn_b1': _L0_ffn_in['b1'], 'L0_ffn_g1': _L0_ffn_in['g1'], 'L0_ffn_be1': _L0_ffn_in['be1'], 'L0_ffn_m1': _L0_ffn_in['m1'], 'L0_ffn_v1': _L0_ffn_in['v1'], 'L0_ffn_W2': _L0_ffn_in['W2'], 'L0_ffn_b2': _L0_ffn_in['b2'], 'L0_ffn_g2': _L0_ffn_in['g2'], 'L0_ffn_be2': _L0_ffn_in['be2'], 'L0_ffn_m2': _L0_ffn_in['m2'], 'L0_ffn_v2': _L0_ffn_in['v2'], 'L0_ffn_Wo': _L0_ffn_in['Wo'], 'L0_ffn_bo': _L0_ffn_in['bo'], 'L1_gnn_W_fc': _L1_gnn_in['W_fc'], 'L1_gnn_W_al': _L1_gnn_in['W_al'], 'L1_gnn_W_ar': _L1_gnn_in['W_ar'], 'L1_gnn_W_res': _L1_gnn_in['W_res'], 'L1_ffn_Wr': _L1_ffn_in['Wr'], 'L1_ffn_br': _L1_ffn_in['br'], 'L1_ffn_W1': _L1_ffn_in['W1'], 'L1_ffn_b1': _L1_ffn_in['b1'], 'L1_ffn_W2': _L1_ffn_in['W2'], 'L1_ffn_b2': _L1_ffn_in['b2'], 'L1_ffn_gamma': _L1_ffn_in['gamma'], 'L1_ffn_beta': _L1_ffn_in['beta']}

def reference(x, src, dst, L0_gnn_W1, L0_gnn_b1, L0_gnn_W2, L0_gnn_b2, L0_ffn_Wr, L0_ffn_br, L0_ffn_W1, L0_ffn_b1, L0_ffn_g1, L0_ffn_be1, L0_ffn_m1, L0_ffn_v1, L0_ffn_W2, L0_ffn_b2, L0_ffn_g2, L0_ffn_be2, L0_ffn_m2, L0_ffn_v2, L0_ffn_Wo, L0_ffn_bo, L1_gnn_W_fc, L1_gnn_W_al, L1_gnn_W_ar, L1_gnn_W_res, L1_ffn_Wr, L1_ffn_br, L1_ffn_W1, L1_ffn_b1, L1_ffn_W2, L1_ffn_b2, L1_ffn_gamma, L1_ffn_beta):
    import jax
    import jax.numpy as jnp

    def _L0_gnn_ref(x, edge_row, edge_col, W1, b1, W2, b2):
        import jax, jax.numpy as jnp
        import numpy as np
        N_NODES = 6250
        N_EDGES = 200000
        IN_FEATS = 256
        HIDDEN = 512
        OUT_FEATS = 256
        EPS = 0.0
        agg = jax.ops.segment_sum(x[edge_col], edge_row, num_segments=N_NODES)
        h = agg + (1.0 + EPS) * x
        h = h @ W1 + b1
        out = h @ W2 + b2
        return out

    def _L0_ffn_ref(x, Wr, br, W1, b1, g1, be1, m1, v1, W2, b2, g2, be2, m2, v2, Wo, bo):
        import jax, jax.numpy as jnp
        import numpy as np
        BN_EPS = 0.001

        def _bn(h, g, b, m, v):
            return g * (h - m) * jax.lax.rsqrt(v + BN_EPS) + b
        feat = jnp.mean(x, axis=0)
        w = jax.nn.softmax(feat @ Wr + br, axis=-1)
        h = jnp.einsum('bfd,edh->bfeh', x, W1) + b1
        h = jax.nn.relu(_bn(h, g1, be1, m1, v1))
        h = jnp.einsum('bfeh,ehk->bfek', h, W2) + b2
        h = jax.nn.relu(_bn(h, g2, be2, m2, v2))
        y = jnp.einsum('bfeh,ehd->bfed', h, Wo) + bo
        return jnp.einsum('bfed,fe->bfd', y, w)

    def _L1_gnn_ref(features, src, dst, W_fc, W_al, W_ar, W_res):
        import jax, jax.numpy as jnp
        import numpy as np
        N, E = (6250, 100000)
        D_IN, D_OUT, H = (256, 64, 4)
        NEG_SLOPE = 0.01

        def _segment_softmax(z, seg, n):
            m = jax.ops.segment_max(z, seg, num_segments=n)
            ez = jnp.exp(z - m[seg])
            denom = jax.ops.segment_sum(ez, seg, num_segments=n)
            return ez / jnp.maximum(denom[seg], 1e-09)
        ft = jnp.einsum('nd,hdo->hno', features, W_fc)
        a1 = jnp.einsum('hno,hoa->hna', ft, W_al)
        a2 = jnp.einsum('hno,hoa->hna', ft, W_ar)

        def head(ft_h, a1_h, a2_h, Wr_h):
            z = jax.nn.leaky_relu(a1_h[dst, 0] + a2_h[src, 0], NEG_SLOPE)
            e = _segment_softmax(z, dst, N)[:, None]
            accum = jax.ops.segment_sum(e * ft_h[src], dst, num_segments=N)
            return jax.nn.relu(accum + features @ Wr_h)
        outs = jax.vmap(head)(ft, a1, a2, W_res)
        return jnp.transpose(outs, (1, 0, 2)).reshape(N, H * D_OUT)

    def _L1_ffn_ref(x, Wr, br, W1, b1, W2, b2, gamma, beta):
        import math
        import jax, jax.numpy as jnp
        import numpy as np
        CAPACITY_FACTOR = 1.25
        TOP_K = 2
        LN_EPS = 1e-05

        def _layer_norm(x, gamma, beta):
            mu = jnp.mean(x, axis=-1, keepdims=True)
            var = jnp.var(x, axis=-1, keepdims=True)
            return (x - mu) * jax.lax.rsqrt(var + LN_EPS) * gamma + beta
        B, S, D = x.shape
        E = Wr.shape[1]
        N = B * S
        K = TOP_K
        logits = jnp.mean(x, axis=1) @ Wr + br
        routing_weights = jax.nn.softmax(logits, axis=-1)
        capacity = float(math.ceil(N * CAPACITY_FACTOR / E))
        expected_loads = routing_weights.sum(axis=0) * (N / B)
        scale = jnp.where(expected_loads > capacity, capacity / expected_loads, 1.0)
        routing_weights = jax.nn.softmax(routing_weights * scale, axis=-1)
        rw_tok = jnp.broadcast_to(routing_weights[:, None, :], (B, S, E)).reshape(N, E)
        top_w, top_i = jax.lax.top_k(rw_tok, K)
        top_w = jax.nn.softmax(top_w, axis=-1)
        xf = x.reshape(N, D)
        h = jax.nn.gelu(jnp.einsum('nd,edf->enf', xf, W1) + b1[:, None, :], approximate=False)
        y = jnp.einsum('enf,efd->end', h, W2) + b2[:, None, :]
        w_dense = jnp.zeros((N, E), x.dtype).at[jnp.arange(N)[:, None], top_i].add(top_w)
        out = jnp.einsum('ne,end->nd', w_dense, y).reshape(B, S, D)
        out = _layer_norm(out + x, gamma, beta)
        return out
    x = x + _L0_gnn_ref(_layernorm(x, axis=-1), src, dst, L0_gnn_W1, L0_gnn_b1, L0_gnn_W2, L0_gnn_b2)
    x = x + _L0_ffn_ref(_layernorm(x, axis=-1)[None], L0_ffn_Wr, L0_ffn_br, L0_ffn_W1, L0_ffn_b1, L0_ffn_g1, L0_ffn_be1, L0_ffn_m1, L0_ffn_v1, L0_ffn_W2, L0_ffn_b2, L0_ffn_g2, L0_ffn_be2, L0_ffn_m2, L0_ffn_v2, L0_ffn_Wo, L0_ffn_bo)[0]
    x = x + _L1_gnn_ref(_layernorm(x, axis=-1), src, dst, L1_gnn_W_fc, L1_gnn_W_al, L1_gnn_W_ar, L1_gnn_W_res)
    x = x + _L1_ffn_ref(_layernorm(x, axis=-1)[None], L1_ffn_Wr, L1_ffn_br, L1_ffn_W1, L1_ffn_b1, L1_ffn_W2, L1_ffn_b2, L1_ffn_gamma, L1_ffn_beta)[0]
    return x

_drawn_inputs = setup_inputs


def setup_inputs(seed=0):
    import zlib

    import numpy as np

    out = dict(_drawn_inputs(seed))
    spreads = {'L0_gnn_b1': (0.0, 0.271),
     'L0_gnn_b2': (0.0, 0.1),
     'L0_ffn_br': (0.0, 0.471),
     'L0_ffn_b1': (0.0, 0.641),
     'L0_ffn_g1': (1.0, 0.6),
     'L0_ffn_be1': (0.0, 0.655),
     'L0_ffn_m1': (0.0, 0.63),
     'L0_ffn_v1': (1.0, 0.6),
     'L0_ffn_b2': (0.0, 0.411),
     'L0_ffn_g2': (1.0, 0.2),
     'L0_ffn_be2': (0.0, 0.48),
     'L0_ffn_m2': (0.0, 0.422),
     'L0_ffn_v2': (1.0, 0.6),
     'L0_ffn_bo': (0.0, 0.335),
     'L1_ffn_br': (0.0, 0.1),
     'L1_ffn_b1': (0.0, 0.582),
     'L1_ffn_b2': (0.0, 0.432),
     'L1_ffn_gamma': (1.0, 0.2),
     'L1_ffn_beta': (0.0, 0.288)}
    factors = {}
    for name, (base, spread) in spreads.items():
        noise = np.random.default_rng([zlib.crc32(name.encode()), seed]).standard_normal(out[name].shape)
        drawn = base * np.exp(spread * noise) if base else spread * noise
        out[name] = jnp.asarray(drawn.astype(out[name].dtype))
    for name, factor in factors.items():
        out[name] = (out[name] * factor).astype(out[name].dtype)
    return out
```

```python
from contextlib import ExitStack

import concourse.bass as bass
from concourse import mybir

F32 = mybir.dt.float32
BF16 = mybir.dt.bfloat16
I32 = mybir.dt.int32
U32 = mybir.dt.uint32
ALU = mybir.AluOpType
ACT = mybir.ActivationFunctionType
AX = mybir.AxisListType

P = 128
N = 6250
E = 200000
D = 256
KD = D // P
NB = -(-N // P)
LAST = N - (NB - 1) * P
NP = NB * P
G = 2
STEP = G * P
STEPS = (E + NB * (STEP - 1)) // STEP
TABLE = -(-STEPS // P)
SLOTS = 8
ROUNDS = -(-STEPS // SLOTS)
LOTS = SLOTS * G
SUMS = 4
LAG = SUMS // G
NOWHERE = 1 << 14
ER = 125
EC = E // ER
H0 = 512
X0 = 8
HEADS, DO = 4, 64
SLOPE = 0.01
ROW = D + HEADS
GROW = D + 2 * HEADS
PROJ = GROW + ROW
TINY = 1e-30
SB = 7
NSB = NB // SB
TOK = SB * P
HALF = TOK // 2
X1, F1 = 8, 512
TOP = 2
CAPACITY = float(-(-N * 5 // (4 * X1)))
DVE_MIX = 21


class Tally:

    def __init__(self, sem):
        self.sem, self.base, self.n, self.outer = sem, 0, 0, []

    def done(self, instruction, by=1):
        instruction.then_inc(self.sem, by)
        self.n += by

    def enter(self, i, per_round):
        self.outer.append((self.base, self.n, per_round))
        self.base, self.n = self.base + self.n + i * per_round, 0

    def leave(self, rounds):
        base, n, per_round = self.outer.pop()
        assert self.n == per_round, (self.sem, self.n, per_round)
        self.base, self.n = base, n + rounds * per_round

    @property
    def now(self):
        return self.base + self.n


class Kept:
    pass


class Scope:

    def __init__(self, nc, ctx, stage):
        self.nc, self.ctx, self.stage, self.used = nc, ctx, stage, []
        ctx.callback(self.free_semaphores)

    def sb(self, name, shape, dtype=F32):
        return self.ctx.enter_context(self.nc.sbuf_tensor(f"{self.stage}_{name}", shape, dtype))

    def ps(self, name, shape, dtype=F32):
        return self.ctx.enter_context(self.nc.psum_tensor(f"{self.stage}_{name}", shape, dtype))

    def sem(self, name):
        self.used.append(self.nc.alloc_semaphore(name=f"{self.stage}_{name}"))
        return self.used[-1]

    def sems(self, name, n):
        return [self.sem(f"{name}{i}") for i in range(n)]

    def free_semaphores(self):
        if self.used:
            self.nc.clear_and_free_semaphores(self.used)
            self.nc.all_engine_barrier()


def spread(ap, shape):
    return ap.to_broadcast(shape)


def registers(eng, name, n):
    return [eng.alloc_register(f"{name}{u}") for u in range(n)]


def step_values(eng, regs, row, i, most):
    eng.load(regs, row[:, bass.ds(i * len(regs), len(regs))])
    return [eng.snap(r, min_val=0, max_val=most) for r in regs]


def load_and_index(nc, io, keep):
    with ExitStack() as ctx:
        s = Scope(nc, ctx, "prep")
        edges = s.sb("edges", [ER, 2, EC], I32)
        pairs = s.sb("pairs", [ER, EC, 2], I32)
        junk = s.sb("junk", [ER, EC], BF16)
        padding = s.sb("padding", [1, 4, STEP], I32)
        bounds = s.sb("bounds", [P, NB + 1])
        bounds_i = s.sb("bounds_i", [P, NB + 1], I32)
        signs = s.sb("signs", [P, NB + 1])
        starts = s.sb("starts", [P, NB + 1])
        count = s.sb("count", [P, NB])
        nsteps_i = s.sb("nsteps_i", [P, NB], I32)
        nsteps = s.sb("nsteps", [P, NB])
        until = s.sb("until", [P, NB])
        zeros = s.sb("zeros", [P, 512])
        step_i = s.sb("step_i", [P, TABLE], I32)
        step_id = s.sb("step_id", [P, TABLE])
        past = s.sb("past", [P, TABLE, NB])
        part = s.sb("part", [P, TABLE, NB])
        block_of = s.sb("block_of", [P, TABLE])
        before = s.sb("before", [P, TABLE])
        edge0 = s.sb("edge0", [P, TABLE])
        inside = s.sb("inside", [P, TABLE])
        table = s.sb("table", [P, 2, TABLE], I32)
        ints = s.sb("ints", [P, P], I32)
        small_i = s.sb("small_i", [P, 2 * NB + 1], I32)
        stats = s.sb("stats", [P, NB, 6])
        aggr = s.sb("aggr", [P, NB, 2])
        std = s.sb("std", [P, NB])
        rstd = s.sb("rstd", [P, NB])
        eps = s.sb("eps", [P, 1])
        total = s.ps("total", [P, NB + 1])

        x_in = s.sem("x_in")
        x_last = s.sem("x_last")
        edges_in = s.sem("edges_in")
        x_pad = s.sem("x_pad")
        made = s.sem("made")
        consts = s.sem("consts")
        counted = s.sem("counted")
        summed = s.sem("summed")
        stats_done = s.sem("stats_done")
        std_done = s.sem("std_done")
        edges_out = s.sem("edges_out")
        table_ready = s.sem("table_ready")
        table_io = s.sem("table_io")
        pairs_ready = s.sem("pairs_ready")
        pads_ready = s.sem("pads_ready")
        order = s.sem("order")
        warm = s.sem("warm")

        with nc.Block() as block:

            @block.sync
            def _(sp):
                sp.dma_start(edges[:, 0, :], io["src"].rearrange("(p c) -> p c", p=ER)).then_inc(edges_in, 16)
                sp.dma_start(edges[:, 1, :], io["dst"].rearrange("(p c) -> p c", p=ER)).then_inc(edges_in, 16)
                blocks = io["x"][0:(NB - 1) * P, :].rearrange("(b p) d -> p b d", p=P)
                for b in range(0, NB - 1, 12):
                    sp.dma_start(keep.x[:, b:b + 12, :], blocks[:, b:b + 12, :]).then_inc(x_in, 16)
                sp.wait_ge(x_pad, 1)
                sp.dma_start(keep.x[0:LAST, NB - 1, :], io["x"][(NB - 1) * P:N, :]).then_inc(x_last, 16)
                sp.wait_ge(edges_in, 32)
                sp.dma_start(keep.src_list[0:E].rearrange("(p c) -> p c", p=ER), edges[:, 0, :]).then_inc(edges_out, 16)
                sp.dma_start(keep.dst_list[0:E].rearrange("(p c) -> p c", p=ER), edges[:, 1, :]).then_inc(edges_out, 16)
                sp.wait_ge(pads_ready, 3)
                one = lambda ap: ap.rearrange("(a c) -> a c", a=1)
                sp.dma_start(one(keep.src_list[E:E + STEP]), padding[:, 0, :]).then_inc(edges_out, 16)
                sp.dma_start(one(keep.dst_list[E:E + STEP]), padding[:, 1, :]).then_inc(edges_out, 16)
                sp.dma_start(keep.pair_list[E:E + STEP, :].rearrange("(a c) t -> a (c t)", a=1),
                             padding[:, 2:4, :].rearrange("p a b -> p (a b)")).then_inc(edges_out, 16)
                sp.wait_ge(pairs_ready, 2)
                sp.dma_start(keep.pair_list[0:E, :].rearrange("(p c) t -> p (c t)", p=ER),
                             pairs[:, :, :].rearrange("p c t -> p (c t)")).then_inc(edges_out, 16)
                sp.wait_ge(table_ready, 1)
                for t in range(2):
                    sp.dma_start(keep.table_dram[t:t + 1, :].rearrange("t (p j) -> p (t j)", p=P), table[:, t, :]).then_inc(table_io, 16)
                sp.wait_ge(table_io, 32)
                sp.dma_start(keep.step_edge[:, :], keep.table_dram[0:1, :]).then_inc(table_io, 16)
                sp.dma_start(keep.step_block[:, :], keep.table_dram[1:2, :]).then_inc(table_io, 16)
                sp.wait_ge(table_io, 64)
                sp.wait_ge(edges_out, 96)

            @block.gpsimd
            def _(pool):
                made_n = Tally(made)
                made_n.done(pool.memset(zeros[:, :], 0.0))
                made_n.done(pool.memset(keep.ident[:, :], 0.0))
                made_n.done(pool.memset(keep.below[:, :], 1.0))
                pool.memset(keep.ones[:, :], 1.0).then_inc(consts, 1)
                pool.wait_ge(made, 3)
                pool.affine_select(out=keep.ident[:, :], in_=keep.ident[:, :], compare_op=ALU.not_equal, fill=1.0,
                                   base=0, pattern=[[-1, P]], channel_multiplier=1).then_inc(consts, 1)
                pool.affine_select(out=keep.below[:, :], in_=keep.below[:, :], compare_op=ALU.is_gt, fill=0.0,
                                   base=0, pattern=[[-1, P]], channel_multiplier=1).then_inc(consts, 1)
                made_n.done(pool.iota(ints[:, :], pattern=[[1, P]], base=0, channel_multiplier=0))
                made_n.done(pool.iota(bounds_i[:, :], pattern=[[P, NB + 1]], base=0, channel_multiplier=0))
                made_n.done(pool.iota(small_i[:, 0:NB], pattern=[[P, NB]], base=0, channel_multiplier=1))
                made_n.done(pool.iota(small_i[:, NB:2 * NB], pattern=[[P, NB]], base=0, channel_multiplier=0))
                made_n.done(pool.iota(small_i[:, 2 * NB:2 * NB + 1], pattern=[[0, 1]], base=NP, channel_multiplier=1))
                made_n.done(pool.iota(step_i[:, :], pattern=[[1, TABLE]], base=0, channel_multiplier=TABLE))
                part_rows = (NP + P) * SUMS // LOTS
                for k in range(LOTS):
                    rows = keep.partial[k % SUMS][k // SUMS * part_rows:(k // SUMS + 1) * part_rows, :]
                    pool.dma_start(rows.rearrange("(p a) d -> p a d", p=64),
                                   spread(zeros[0:64, 0:D].rearrange("p (a d) -> p a d", a=1), [64, part_rows // 64, D]),
                                   ).then_inc(keep.added[k], 16)
                for k in range(LOTS):
                    pool.wait_ge(keep.added[k], 16)

            @block.scalar
            def _(act):
                act.wait_ge(edges_in, 32)
                act.wait_ge(consts, 4)
                act.activation(std[:, 0:1], bounds[:, 0:1], ACT.Sign).then_inc(warm, 1)
                act.wait_ge(warm, 1)
                with act.Fori(0, NB + 1) as b:
                    act.activation(junk[:, :], edges[:, 1, :], ACT.Sign, bias=bounds[0:ER, bass.ds(b, 1)], scale=-1.0,
                                   accum_out=signs[0:ER, bass.ds(b, 1)]).then_inc(counted, 1)
                    act.wait_ge(counted, b + 1)
                act.wait_ge(stats_done, 1)
                act.activation(std[:, :], aggr[:, :, 1], ACT.Sqrt, bias=eps[:, 0:1]).then_inc(std_done, 1)

            @block.tensor
            def _(pe):
                pe.wait_ge(counted, NB + 1)
                pe.wait_ge(consts, 1)
                pe.matmul(total[:, :], keep.ones[0:ER, :], signs[0:ER, :], start=True, stop=True).then_inc(summed, 1)

            @block.vector
            def _(dve):
                seq = Tally(order)

                def then(instruction):
                    seq.done(instruction)
                    dve.wait_ge(order, seq.now)

                dve.memset(keep.x[:, NB - 1, :], 0.0).then_inc(x_pad, 1)
                seq.done(dve.memset(eps[:, :], 1e-5))
                dve.memset(padding[:, 0, :], 0).then_inc(pads_ready, 1)
                dve.memset(padding[:, 1, :], NOWHERE).then_inc(pads_ready, 1)
                then(dve.memset(padding[:, 2:4, :], 0))
                dve.memset(padding[:, 2:4, :].rearrange("p a (b t) -> p (a b) t", t=2)[:, :, 1], NOWHERE).then_inc(pads_ready, 1)
                dve.wait_ge(made, 9)
                then(dve.tensor_copy(keep.lane[:, :], ints[:, :]))
                then(dve.tensor_scalar(bounds[:, :], bounds_i[:, :], 0.5, None, ALU.subtract))
                then(dve.tensor_copy(keep.node_id[:, :], small_i[:, 0:NB]))
                then(dve.tensor_copy(keep.block_base[:, :], small_i[:, NB:2 * NB]))
                then(dve.tensor_copy(keep.spare_row[:, :], small_i[:, 2 * NB:2 * NB + 1]))
                dve.tensor_copy(step_id[:, :], step_i[:, :]).then_inc(consts, 1)
                dve.wait_ge(edges_in, 32)
                dve.tensor_copy(pairs[:, :, 0], edges[:, 0, :]).then_inc(pairs_ready, 1)
                dve.tensor_copy(pairs[:, :, 1], edges[:, 1, :]).then_inc(pairs_ready, 1)
                dve.wait_ge(x_in, 64)
                dve.wait_ge(x_last, 16)
                dve.wait_ge(x_pad, 1)
                dve.wait_ge(order, seq.now)
                with dve.Fori(0, NB) as b:
                    seq.enter(b, 1)
                    seq.done(dve.bn_stats(stats[:, bass.ds(b, 1), :], keep.x[:, bass.ds(b, 1), :]))
                    seq.leave(NB)
                dve.wait_ge(order, seq.now)
                for b in range(NB):
                    last = dve.bn_aggr(aggr[:, b, :], stats[:, b, :])
                last.then_inc(stats_done, 1)
                dve.wait_ge(std_done, 1)
                then(dve.reciprocal(rstd[:, :], std[:, :]))
                with dve.Fori(0, NB) as b:
                    seq.enter(b, 1)
                    seq.done(dve.tensor_scalar(keep.xn[:, bass.ds(b, 1), 0:D], keep.x[:, bass.ds(b, 1), :],
                                               aggr[:, bass.ds(b, 1), 0], rstd[:, bass.ds(b, 1)],
                                               ALU.subtract, ALU.mult))
                    seq.leave(NB)
                dve.wait_ge(summed, 1)
                then(dve.tensor_scalar(starts[:, :], total[:, :], float(E), 0.5, ALU.add, ALU.mult))
                then(dve.tensor_tensor(count[:, :], starts[:, 1:NB + 1], starts[:, 0:NB], ALU.subtract))
                then(dve.tensor_scalar(nsteps_i[:, :], count[:, :], float(STEP - 1), None, ALU.add))
                then(dve.tensor_scalar(nsteps_i[:, :], nsteps_i[:, :], STEP.bit_length() - 1, None, ALU.logical_shift_right))
                then(dve.tensor_copy(nsteps[:, :], nsteps_i[:, :]))
                dve.wait_ge(made, 1)
                then(dve.tensor_tensor_scan(until[:, :], nsteps[:, :], zeros[:, 0:NB], 0.0, ALU.add, ALU.add))
                every = [P, TABLE, NB]
                row = lambda ap: spread(ap.rearrange("p (j b) -> p j b", j=1), every)
                dve.wait_ge(consts, 4)
                then(dve.tensor_tensor(past[:, :, :], row(until[:, :]),
                                       spread(step_id[:, :].rearrange("p (j b) -> p j b", b=1), every), ALU.is_le))
                then(dve.tensor_reduce(block_of[:, :], past[:, :, :], AX.X, ALU.add))
                then(dve.tensor_tensor(part[:, :, :], past[:, :, :], row(count[:, :]), ALU.mult))
                then(dve.tensor_reduce(edge0[:, :], part[:, :, :], AX.X, ALU.add))
                then(dve.tensor_tensor(part[:, :, :], past[:, :, :], row(until[:, :]), ALU.mult))
                then(dve.tensor_reduce(before[:, :], part[:, :, :], AX.X, ALU.max))
                then(dve.tensor_tensor(inside[:, :], step_id[:, :], before[:, :], ALU.subtract))
                then(dve.scalar_tensor_tensor(edge0[:, :], inside[:, :], float(STEP), edge0[:, :], ALU.mult, ALU.add))
                then(dve.tensor_scalar(table[:, 0, :], edge0[:, :], float(E), None, ALU.min))
                dve.tensor_scalar(table[:, 1, :], block_of[:, :], float(NB - 1), None, ALU.min).then_inc(table_ready, 1)
                dve.wait_ge(order, seq.now)


def scatter_sums(nc, io, keep):
    with ExitStack() as ctx:
        s = Scope(nc, ctx, "scat")
        cols = s.sb("cols", [P, SLOTS, G, 2], I32)
        rows = s.sb("rows", [P, SLOTS, STEP], I32)
        dst_in = s.sb("dst_in", [P, SLOTS, G])
        is_dst = s.sb("is_dst", [P, SLOTS, G, P], BF16)
        same = s.sb("same", [P, SLOTS, G, P], BF16)
        junk = s.sb("junk", [P, 2, G, P], BF16)
        repeated = s.sb("repeated", [P, SLOTS, G])
        to_spare = s.sb("to_spare", [P, SLOTS, G])
        index = s.sb("index", [P, SLOTS, G], I32)
        merge = s.sb("merge", [P, SLOTS, G, P])
        values = s.sb("values", [P, SLOTS, G, D])
        merge_ps = [s.ps(f"merge_ps{u}", [P, G, P]) for u in range(2)]
        values_ps = [s.ps(f"values_ps{u}", [P, G, D]) for u in range(2)]

        cols_in = s.sems("cols_in", SLOTS)
        rows_in = s.sems("rows_in", SLOTS)
        masks_ready = s.sem("masks_ready")
        index_ready = s.sem("index_ready")
        merged = s.sem("merged")
        merge_ready = s.sem("merge_ready")
        summed = s.sem("summed")
        values_ready = s.sem("values_ready")
        lists_free = s.sem("lists_free")
        order = s.sem("order")
        turn = s.sem("turn")

        with nc.Block() as block:

            @block.sync
            def _(sp):
                regs = registers(sp, "scat_first", SLOTS)
                with sp.Fori(0, ROUNDS) as i:
                    firsts = step_values(sp, regs, keep.step_edge, i, E)
                    for u, first in enumerate(firsts):
                        sp.wait_ge(lists_free, i * SLOTS + u + 1)
                        sp.sem_inc(turn, 1)
                        sp.dma_start(cols[:, u, :, :].rearrange("p g t -> p (g t)"),
                                     keep.pair_list[bass.ds(first, STEP), :].rearrange("(p g) t -> p (g t)", g=G)
                                     ).then_inc(cols_in[u], 16)
                        sp.dma_start(rows[:, u, :], keep.src_list[bass.ds(first, STEP)].partition_broadcast(P)
                                     ).then_inc(rows_in[u], 16)

            @block.vector
            def _(dve):
                seq = Tally(order)

                def then(instruction):
                    seq.done(instruction)
                    dve.wait_ge(order, seq.now)

                every = [P, G, P]
                dve.sem_inc(lists_free, SLOTS)
                regs = registers(dve, "scat_dve", SLOTS)
                with dve.Fori(0, ROUNDS) as i:
                    in_block = step_values(dve, regs, keep.step_block, i, NB - 1)
                    seq.enter(i, SLOTS * (2 + G))

                    def write_index(u):
                        for g in range(G):
                            dve.wait_ge(keep.added[u * G + g], i * 16 + 16)
                        dve.wait_ge(order, ready[u])
                        for g in range(G):
                            last = dve.scalar_tensor_tensor(index[:, u, g:g + 1], to_spare[:, u, g:g + 1],
                                                            repeated[:, u, g:g + 1], cols[:, u, g:g + 1, 0],
                                                            ALU.mult, ALU.add)
                        last.then_inc(index_ready, 1)

                    ready = {}
                    for u in range(SLOTS):
                        src = cols[:, u, :, 0]
                        dve.wait_ge(cols_in[u], i * 16 + 16)
                        seq.done(dve.tensor_scalar(dst_in[:, u, :], cols[:, u, :, 1], keep.block_base[:, bass.ds(in_block[u], 1)],
                                                   None, ALU.subtract))
                        dst_done = seq.now
                        dve.wait_ge(merged, i * SLOTS + u + 1)
                        dve.wait_ge(rows_in[u], i * 16 + 16)
                        dve.tensor_tensor(same[:, u, :, :], rows[:, u, :].rearrange("p (q g) -> p g q", g=G),
                                          spread(src.rearrange("p (g n) -> p g n", n=1), every),
                                          ALU.is_equal).then_inc(masks_ready, 1)
                        seq.done(dve.tensor_scalar(to_spare[:, u, :], src, -1.0, keep.spare_row[:, 0:1], ALU.mult, ALU.add))
                        if u:
                            write_index(u - 1)
                        dve.wait_ge(order, dst_done)
                        dve.tensor_tensor(is_dst[:, u, :, :], spread(keep.lane[:, :].rearrange("p (g n) -> p g n", g=1), every),
                                          spread(dst_in[:, u, :].rearrange("p (g n) -> p g n", n=1), every),
                                          ALU.is_equal).then_inc(masks_ready, 1)
                        dve.wait_ge(masks_ready, (i * SLOTS + u) * 2 + 1)
                        dve.sem_inc(turn, 1)
                        for g in range(G):
                            seq.done(dve.tensor_tensor_reduce(out=junk[:, u % 2, g, :], in0=same[:, u, g, :], in1=keep.below[:, :],
                                                              scale=1.0, scalar=0.0, op0=ALU.mult, op1=ALU.max,
                                                              accum_out=repeated[:, u, g:g + 1]))
                        ready[u] = seq.now
                        if u:
                            dve.wait_ge(index_ready, i * SLOTS + u)
                            dve.sem_inc(lists_free, 1)
                    write_index(SLOTS - 1)
                    dve.wait_ge(index_ready, i * SLOTS + SLOTS)
                    dve.sem_inc(lists_free, 1)
                    seq.leave(ROUNDS)

            @block.tensor
            def _(pe):
                pe.sem_inc(merged, SLOTS)
                regs = registers(pe, "scat_pe", SLOTS)
                with pe.Fori(0, ROUNDS) as i:
                    in_block = step_values(pe, regs, keep.step_block, i, NB - 1)

                    def merge_edges(u):
                        pe.wait_ge(masks_ready, (i * SLOTS + u) * 2 + 2)
                        for g in range(G):
                            last = pe.matmul(merge_ps[u % 2][:, g, :], is_dst[:, u, g, :], same[:, u, g, :], start=True, stop=True)
                        last.then_inc(merged, 1)

                    def sum_values(u):
                        pe.wait_ge(merge_ready, i * SLOTS + u + 1)
                        for g in range(G):
                            last = pe.matmul(values_ps[u % 2][:, g, :], merge[:, u, g, :], keep.xn[:, bass.ds(in_block[u], 1), 0:D],
                                             start=True, stop=True)
                        last.then_inc(summed, 1)

                    merge_edges(0)
                    for u in range(1, SLOTS):
                        merge_edges(u)
                        sum_values(u - 1)
                    sum_values(SLOTS - 1)

            @block.scalar
            def _(act):
                with act.Fori(0, ROUNDS) as i:

                    def copy_merge(u):
                        act.wait_ge(merged, i * SLOTS + u + 1 + SLOTS)
                        act.copy(merge[:, u, :, :], merge_ps[u % 2][:, :, :]).then_inc(merge_ready, 1)

                    def copy_values(u):
                        act.wait_ge(summed, i * SLOTS + u + 1)
                        for g in range(G):
                            act.wait_ge(keep.added[u * G + g], i * 16 + 16)
                        act.copy(values[:, u, :, :], values_ps[u % 2][:, :, :]).then_inc(values_ready, 1)

                    copy_merge(0)
                    for u in range(1, SLOTS):
                        copy_merge(u)
                        copy_values(u - 1)
                    copy_values(SLOTS - 1)

            @block.gpsimd
            def _(pool):
                with pool.Fori(0, ROUNDS) as i:
                    for u in range(SLOTS):
                        pool.wait_ge(index_ready, i * SLOTS + u + 1)
                        pool.wait_ge(values_ready, i * SLOTS + u + 1)
                        pool.sem_inc(turn, 1)
                        for g in range(G):
                            k = u * G + g
                            pool.wait_ge(keep.added[(k - SUMS) % LOTS], i * 16 + (16 if u < LAG else 32))
                            pool.sem_inc(turn, 1)
                            pool.indirect_dma_start(
                                out=keep.partial[k % SUMS], out_offset=bass.IndirectOffsetOnAxis(ap=index[:, u, g:g + 1], axis=0),
                                in_=values[:, u, g, :], in_offset=None, compute_op=ALU.add).then_inc(keep.added[k], 16)
                for k in range(LOTS):
                    pool.wait_ge(keep.added[k], 16 * (ROUNDS + 1))


def fold_weights(nc, io, keep):
    with ExitStack() as ctx:
        s = Scope(nc, ctx, "fold")
        w1 = s.sb("w1", [P, KD, H0])
        w2 = s.sb("w2", [P, H0 // P, D])
        w1t = s.sb("w1t", [P, H0 // P, D])
        b1 = s.sb("b1", [P, H0 // P])
        b1_wide = s.sb("b1_wide", [P, H0 // P, P])
        b2 = s.sb("b2", [P, D])
        norms = s.sb("norms", [2 * X0, 2, 5, P])
        root = s.sb("root", [2 * X0, 2, P])
        eps = s.sb("eps", [P, 1])
        lines = s.sb("lines", [2 * X0, 4, P])
        al = s.sb("al", [P, 2, D])
        prod = s.sb("prod", [P, KD, 2, HEADS, DO])
        w1t_ps = [s.ps(f"w1t_ps{k}", [P, H0 // P, P]) for k in range(KD)]
        w12_ps = s.ps("w12_ps", [P, KD, D])
        b12_ps = s.ps("b12_ps", [P, D])
        norm_ps = s.ps("norm_ps", [P, 4, 2 * X0])

        w_in = s.sem("w_in")
        b_in = s.sem("b_in")
        norms_in = s.sem("norms_in")
        heads_in = s.sem("heads_in")
        others_in = s.sem("others_in")
        w1_turned = s.sem("w1_turned")
        w1t_ready = s.sem("w1t_ready")
        wide_ready = s.sem("wide_ready")
        w12_done = s.sem("w12_done")
        b12_done = s.sem("b12_done")
        var_ready = s.sem("var_ready")
        root_ready = s.sem("root_ready")
        lines_ready = s.sem("lines_ready")
        norm_done = s.sem("norm_done")
        order = s.sem("order")

        with nc.Block() as block:

            @block.sync
            def _(sp):
                sp.dma_start(w1[:, :, :], io["L0_gnn_W1"].rearrange("(k p) h -> p k h", p=P)).then_inc(w_in, 16)
                sp.dma_start(w2[:, :, :], io["L0_gnn_W2"].rearrange("(c p) d -> p c d", p=P)).then_inc(w_in, 16)
                with nc.allow_non_contiguous_dma(reason="512 words"):
                    sp.dma_start(b1[:, :], io["L0_gnn_b1"].rearrange("(c p) -> p c", p=P)).then_inc(b_in, 16)
                sp.dma_start(b2[:, :], io["L0_gnn_b2"].partition_broadcast(P)).then_inc(b_in, 16)
                for layer, names in enumerate((("g1", "be1", "m1", "v1", "b1"), ("g2", "be2", "m2", "v2", "b2"))):
                    vectors = (io["L0_ffn_g1"], io["L0_ffn_be1"], io["L0_ffn_m1"], io["L0_ffn_v1"], io["L0_ffn_b1"]) if layer == 0 else \
                              (io["L0_ffn_g2"], io["L0_ffn_be2"], io["L0_ffn_m2"], io["L0_ffn_v2"], io["L0_ffn_b2"])
                    for n, v in enumerate(vectors):
                        sp.dma_start(norms[:, layer, n, :], v.rearrange("e (c p) -> (e c) p", p=P)).then_inc(norms_in, 16)
                for k in range(KD):
                    rows = slice(k * P, (k + 1) * P)
                    sp.dma_start(keep.proj[:, k, 0:D].rearrange("p (h o) -> p h o", h=HEADS),
                                 io["L1_gnn_W_fc"][:, rows, :].rearrange("h p o -> p h o")).then_inc(heads_in, 16)
                    sp.dma_start(keep.proj[:, k, GROW + HEADS:PROJ].rearrange("p (h o) -> p h o", h=HEADS),
                                 io["L1_gnn_W_res"][:, rows, :].rearrange("h p o -> p h o")).then_inc(others_in, 16)
                sp.dma_start(al[:, 0, :], io["L1_gnn_W_ar"].rearrange("h o a -> (h o a)").partition_broadcast(P)).then_inc(heads_in, 16)
                sp.dma_start(al[:, 1, :], io["L1_gnn_W_al"].rearrange("h o a -> (h o a)").partition_broadcast(P)).then_inc(heads_in, 16)
                sp.dma_start(keep.wr[:, :, :], io["L0_ffn_Wr"].rearrange("(k p) e -> p k e", p=P)).then_inc(others_in, 16)
                sp.dma_start(keep.br[:, :], io["L0_ffn_br"].partition_broadcast(P)).then_inc(others_in, 16)
                sp.dma_start(keep.bo[:, :], io["L0_ffn_bo"]).then_inc(others_in, 16)
                sp.wait_ge(others_in, 16 * (KD + 3))

            @block.tensor
            def _(pe):
                pe.wait_ge(w_in, 32)
                for k in range(KD):
                    for c in range(H0 // P):
                        last = pe.transpose(w1t_ps[k][:, c, :], w1[:, k, c * P:(c + 1) * P], keep.ident[:, :])
                last.then_inc(w1_turned, 1)
                pe.wait_ge(b_in, 32)
                pe.wait_ge(wide_ready, 1)
                for c in range(H0 // P):
                    last = pe.matmul(b12_ps[:, :], b1_wide[:, c, :], w2[:, c, :], start=(c == 0), stop=(c == H0 // P - 1))
                last.then_inc(b12_done, 1)
                pe.wait_ge(w1t_ready, KD)
                for k in range(KD):
                    for c in range(H0 // P):
                        last = pe.matmul(w12_ps[:, k, :], w1t[:, c, k * P:(k + 1) * P], w2[:, c, :],
                                         start=(c == 0), stop=(c == H0 // P - 1))
                last.then_inc(w12_done, 1)
                pe.wait_ge(lines_ready, 4)
                for n in range(4):
                    last = pe.transpose(norm_ps[:, n, :], lines[:, n, :], keep.ident[0:2 * X0, 0:2 * X0])
                last.then_inc(norm_done, 1)

            @block.scalar
            def _(act):
                act.wait_ge(w1_turned, 1)
                for k in range(KD):
                    act.copy(w1t[:, :, k * P:(k + 1) * P], w1t_ps[k][:, :, :]).then_inc(w1t_ready, 1)
                act.wait_ge(var_ready, 1)
                act.wait_ge(norms_in, 160)
                act.activation(root[:, :, :], norms[:, :, 3, :], ACT.Sqrt, bias=eps[0:2 * X0, 0:1]).then_inc(root_ready, 1)

            @block.vector
            def _(dve):
                seq = Tally(order)

                def then(instruction):
                    seq.done(instruction)
                    dve.wait_ge(order, seq.now)

                dve.memset(eps[:, :], 1e-3).then_inc(var_ready, 1)
                dve.wait_ge(b_in, 32)
                dve.tensor_copy(b1_wide[:, :, :], spread(b1[:, :].rearrange("p (c n) -> p c n", n=1), [P, H0 // P, P]))\
                   .then_inc(wide_ready, 1)
                dve.wait_ge(root_ready, 1)
                then(dve.reciprocal(root[:, :, :], root[:, :, :]))
                for layer in range(2):
                    g, be, m, v, b = (norms[:, layer, n, :] for n in range(5))
                    scale, shift = lines[:, 2 * layer, :], lines[:, 2 * layer + 1, :]
                    dve.tensor_tensor(scale, g, root[:, layer, :], ALU.mult).then_inc(lines_ready, 1)
                    then(dve.tensor_tensor(b, b, m, ALU.subtract))
                    dve.wait_ge(lines_ready, 2 * layer + 1)
                    then(dve.tensor_tensor(b, b, scale, ALU.mult))
                    dve.tensor_tensor(shift, b, be, ALU.add).then_inc(lines_ready, 1)
                dve.wait_ge(heads_in, 16 * (KD + 2))
                for k in range(KD):
                    for n in range(2):
                        then(dve.tensor_tensor(prod[:, k, n, :, :], keep.proj[:, k, 0:D].rearrange("p (h o) -> p h o", h=HEADS),
                                               al[:, n, :].rearrange("p (h o) -> p h o", h=HEADS), ALU.mult))
                        at = D + 2 * n * HEADS
                        seq.done(dve.tensor_reduce(keep.proj[:, k, at:at + HEADS], prod[:, k, n, :, :], AX.X, ALU.add))
                dve.wait_ge(order, seq.now)
                seq.done(dve.tensor_scalar(keep.proj[:, :, D + HEADS:GROW], keep.proj[:, :, D:ROW], SLOPE, None, ALU.mult))
                dve.wait_ge(b12_done, 1)
                seq.done(dve.tensor_tensor(keep.b12[:, :], b12_ps[:, :], b2[:, :], ALU.add))
                dve.wait_ge(w12_done, 1)
                seq.done(dve.tensor_copy(keep.w12[:, :, :], w12_ps[:, :, :]))
                dve.wait_ge(norm_done, 1)
                seq.done(dve.tensor_copy(keep.bn[:, :, :], norm_ps[:, :, :]))
                dve.wait_ge(order, seq.now)


T_H, T_X, T_R, T_W, T_Z, TURNS = 0, 4, 8, 10, 12, 16
WIDES = X0 * 8
C_E, C_BO, C_P = SB, SB + X0 * SB, 2 * SB + X0 * SB
SUMS_C = C_P + 2 * SB


def turn_blocks(j):
    return range(2 * j, min(2 * j + 2, SB))


def mixture(nc, io, keep):
    with ExitStack() as ctx:
        s = Scope(nc, ctx, "mix")
        parts = s.sb("parts", [P, 2, SB, D])
        h = s.sb("h", [P, SB, D])
        normed = s.sb("normed", [P, SB, D])
        at = s.sb("at", [P, KD, TOK])
        xt = s.sb("xt", [P, KD, TOK])
        h1 = s.sb("h1", [P, KD, TOK])
        h2 = s.sb("h2", [P, KD, TOK])
        weights = s.sb("weights", [P, 2, 3, KD, D])
        rows = s.sb("rows", [P, SB, GROW])
        residual = s.sb("residual", [P, SB, ROW])
        stats = s.sb("stats", [P, SB, 6])
        aggr = s.sb("aggr", [P, SB, 2])
        std = s.sb("std", [P, SB])
        rstd = s.sb("rstd", [P, SB])
        eps = s.sb("eps", [P, 1])
        logits = s.sb("logits", [P, SB, X0])
        gate = s.sb("gate", [P, SB, X0])
        top = s.sb("top", [P, SB])
        gate_t = s.sb("gate_t", [X0, SB, P])
        a2_top = s.sb("a2_top", [P, HEADS])
        a2_new = s.sb("a2_new", [P, HEADS])
        shift = s.sb("shift", [P, NB, HEADS])
        turn = [s.ps(f"turn{n}", [P, 512]) for n in range(2)]
        wide = [s.ps(f"wide{n}", [P, 512]) for n in range(4)]
        sums = [s.ps(f"sums{n}", [P, 512]) for n in range(2)]

        parts_in = s.sems("parts_in", 2)
        parts_used = s.sem("parts_used")
        biased = s.sem("biased")
        weights_in = s.sems("weights_in", 2)
        turn_full = s.sem("turn_full")
        turn_free = s.sems("turn_free", 2)
        wide_full = s.sem("wide_full")
        wide_free = s.sems("wide_free", 4)
        sums_full = s.sem("sums_full")
        sums_free = s.sems("sums_free", 2)
        std_ready = s.sem("std_ready")
        aggr_ready = s.sem("aggr_ready")
        normed_ready = s.sem("normed_ready")
        exp_in = s.sem("exp_in")
        exp_out = s.sem("exp_out")
        gate_ready = s.sem("gate_ready")
        rows_ready = s.sem("rows_ready")
        rows_out = s.sem("rows_out")
        node_ready = s.sem("node_ready")
        at_ready = s.sem("at_ready")
        xt_ready = s.sem("xt_ready")
        h1_ready = s.sem("h1_ready")
        h2_ready = s.sem("h2_ready")
        gate_t_ready = s.sem("gate_t_ready")
        a1_taken = s.sem("a1_taken")
        order = s.sem("order")
        pause = s.sem("pause")

        def turn_used(i, t):
            return i * (TURNS // 2) + t // 2 + 2

        def sums_used(i, t):
            return i * (SUMS_C // 2) + t // 2 + 2

        with nc.Block() as block:

            @block.sync
            def _(sp):
                sp.sem_inc(rows_out, 32)
                with sp.Fori(0, NSB) as i:
                    for k in range(SUMS):
                        sp.wait_ge(parts_used, i * SUMS + k + 1)
                        sp.sem_inc(pause, 1)
                        sp.dma_start(parts[:, k % 2, :, :],
                                     keep.partial[k][bass.ds(i * TOK, TOK), :].rearrange("(b p) d -> p b d", p=P)
                                     ).then_inc(parts_in[k % 2], 16)
                    with sp.Fori(0, X0 // 2) as j:
                        for e in range(2):
                            sp.wait_ge(sums_full, i * SUMS_C + j * 2 * SB + e * SB + 1)
                            sp.sem_inc(pause, 1)
                            for n, w in enumerate((io["L0_ffn_W1"], io["L0_ffn_W2"], io["L0_ffn_Wo"])):
                                sp.dma_start(weights[:, e, n, :, :],
                                             w[bass.ds(j * 2 + e, 1), :, :].rearrange("e (k p) h -> p (e k) h", p=P)
                                             ).then_inc(weights_in[e], 16)
                    sp.wait_ge(rows_ready, (i + 1) * 2 * SB)
                    sp.sem_inc(pause, 1)
                    sp.dma_start(keep.rows_dram[bass.ds(i * TOK, TOK), :].rearrange("(b p) d -> p b d", p=P),
                                 rows[:, :, :]).then_inc(rows_out, 16)
                    sp.dma_start(keep.residual_dram[bass.ds(i * TOK, TOK), :].rearrange("(b p) d -> p b d", p=P),
                                 residual[:, :, HEADS:ROW]).then_inc(rows_out, 16)
                sp.wait_ge(rows_out, 32 * (NSB + 1))

            @block.gpsimd
            def _(pool):
                pool.sem_inc(parts_used, 2)
                with pool.Fori(0, NSB) as i:
                    here = bass.ds(i * SB, SB)
                    for k in range(SUMS):
                        pool.wait_ge(parts_in[k % 2], (i * (SUMS // 2) + k // 2 + 1) * 16)
                        if k == 0:
                            pool.wait_ge(turn_full, i * TURNS + 1)
                            pool.sem_inc(pause, 1)
                            pool.tensor_tensor(h[:, :, :], keep.xn[:, here, 0:D], parts[:, 0, :, :], ALU.add).then_inc(parts_used, 1)
                        else:
                            pool.wait_ge(parts_used, i * SUMS + k + 2)
                            pool.tensor_tensor(h[:, :, :], h[:, :, :], parts[:, k % 2, :, :], ALU.add).then_inc(parts_used, 1)
                    pool.tensor_tensor(keep.x[:, here, :], keep.x[:, here, :],
                                       spread(keep.b12[:, :].rearrange("p (b d) -> p b d", b=1), [P, SB, D]),
                                       ALU.add).then_inc(biased, 1)
                pool.wait_ge(order, NSB * DVE_MIX + 2)
                pool.partition_all_reduce(keep.a2_bound[:, :], a2_top[:, :], P, bass.bass_isa.ReduceOp.max).then_inc(node_ready, 1)
                pool.wait_ge(node_ready, 1)

            @block.tensor
            def _(pe):
                pe.sem_inc(turn_full, 1)
                pe.sem_inc(sums_full, 1)
                with pe.Fori(0, NSB) as i:

                    def turn_over(tile, t0, ready, first):
                        for j in range(4):
                            t = t0 + j
                            for b in turn_blocks(j):
                                if ready is not None:
                                    pe.wait_ge(ready, first + b + 1)
                                if b == 2 * j:
                                    pe.wait_ge(turn_free[t % 2], turn_used(i, t) - 1)
                                for k in range(KD):
                                    at0 = (k * 2 + b - 2 * j) * P
                                    last = pe.transpose(turn[t % 2][:, at0:at0 + P], tile[:, b, k * P:(k + 1) * P], keep.ident[:, :])
                            last.then_inc(turn_full, 1)

                    def sum_tile(t, left, right, width=D, at0=0):
                        pe.wait_ge(sums_free[t % 2], sums_used(i, t) - 1)
                        for k in range(KD):
                            last = pe.matmul(sums[t % 2][:, 0:width], left(k), right(k), start=(k == 0), stop=(k == KD - 1))
                        last.then_inc(sums_full, 1)

                    pe.wait_ge(parts_used, i * SUMS + SUMS + 2)
                    turn_over(h, T_H, None, 0)
                    for b in range(SB):
                        pe.wait_ge(at_ready, i * 8 + b // 2 + 1)
                        sum_tile(b, lambda k: at[:, k, b * P:(b + 1) * P], lambda k: keep.w12[:, k, :])
                    turn_over(normed, T_X, normed_ready, i * 2 * SB)
                    for half in range(2):
                        blocks = range(0, 4) if half == 0 else range(4, SB)
                        t = T_R + half
                        pe.wait_ge(turn_free[t % 2], turn_used(i, t) - 1)
                        for b in blocks:
                            pe.wait_ge(xt_ready, i * 4 + b // 2 + 1)
                            for k in range(KD):
                                last = pe.matmul(turn[t % 2][:, b * X0:(b + 1) * X0], xt[:, k, b * P:(b + 1) * P], keep.wr[:, k, :],
                                                 start=(k == 0), stop=(k == KD - 1))
                        last.then_inc(turn_full, 1)
                    with pe.Fori(0, X0 // 2) as j:
                        for e in range(2):
                            pe.wait_ge(weights_in[e], (i * (X0 // 2) + j + 1) * 48)
                            w0 = i * WIDES + j * 16 + e * 8
                            for layer, (source, ready) in enumerate(((xt, None), (h1, h1_ready))):
                                for half in range(2):
                                    if ready is not None:
                                        pe.wait_ge(ready, i * X0 * 4 + j * 8 + e * 4 + 2 * half + 2)
                                    for m in range(KD):
                                        t = layer * 4 + half * 2 + m
                                        pe.wait_ge(wide_free[t % 4], i * (WIDES // 4) + j * 4 + e * 2 + t // 4 + 1)
                                        for k in range(KD):
                                            last = pe.matmul(wide[t % 4][:, 0:HALF], weights[:, e, layer, k, m * P:(m + 1) * P],
                                                             source[:, k, half * HALF:(half + 1) * HALF],
                                                             start=(k == 0), stop=(k == KD - 1))
                                        last.then_inc(wide_full, 1)
                            for b in range(SB):
                                pe.wait_ge(h2_ready, i * X0 * 4 + j * 8 + e * 4 + (2 if (b + 1) * P <= HALF else 4))
                                t = C_E + e * SB + b
                                pe.wait_ge(sums_free[t % 2], i * (SUMS_C // 2) + j * SB + t // 2 + 1)
                                for k in range(KD):
                                    last = pe.matmul(sums[t % 2][:, 0:D], h2[:, k, b * P:(b + 1) * P], weights[:, e, 2, k, :],
                                                     start=(k == 0), stop=(k == KD - 1))
                                last.then_inc(sums_full, 1)
                    for half in range(2):
                        blocks = range(0, 4) if half == 0 else range(4, SB)
                        t = T_W + half
                        pe.wait_ge(gate_ready, i + 1)
                        pe.wait_ge(turn_free[t % 2], turn_used(i, t) - 1)
                        for n, b in enumerate(blocks):
                            last = pe.transpose(turn[t % 2][0:X0, n * P:(n + 1) * P], gate[:, b, :], keep.ident[:, :])
                        last.then_inc(turn_full, 1)
                    for b in range(SB):
                        t = C_BO + b
                        pe.wait_ge(gate_t_ready, i * 2 + b // 4 + 1)
                        pe.wait_ge(sums_free[t % 2], sums_used(i, t) - 1)
                        pe.matmul(sums[t % 2][:, 0:D], gate_t[:, b, :], keep.bo[:, :], start=True, stop=True).then_inc(sums_full, 1)
                    turn_over(normed, T_Z, normed_ready, i * 2 * SB + SB)
                    for b in range(SB):
                        pe.wait_ge(at_ready, i * 8 + 4 + b // 2 + 1)
                        for n in range(2):
                            c0, c1 = (0, GROW) if n == 0 else (GROW, PROJ)
                            sum_tile(C_P + 2 * b + n, lambda k: at[:, k, b * P:(b + 1) * P],
                                     lambda k: keep.proj[:, k, c0:c1], width=c1 - c0)

            @block.scalar
            def _(act):
                act.sem_inc(a1_taken, 1)
                for n in range(4):
                    act.sem_inc(wide_free[n], 1)
                with act.Fori(0, NSB) as i:

                    def copy_turn(t0, j, tile, ready):
                        t = t0 + j
                        act.wait_ge(turn_full, i * TURNS + t + 2)
                        width = len(turn_blocks(j)) * P
                        act.copy(tile[:, :, 2 * j * P:2 * j * P + width],
                                 turn[t % 2][:, :].rearrange("p (k n) -> p k n", k=KD)[:, :, 0:width]).then_inc(ready, 1)
                        act.wait_ge(ready, i * (8 if ready is at_ready else 4) + (4 if t0 == T_Z else 0) + j + 1)
                        act.sem_inc(turn_free[t % 2], 1)

                    for j in range(4):
                        copy_turn(T_H, j, at, at_ready)
                    act.wait_ge(aggr_ready, 2 * i + 1)
                    act.activation(std[:, :], aggr[:, :, 1], ACT.Sqrt, bias=eps[:, 0:1]).then_inc(std_ready, 1)
                    for j in range(4):
                        copy_turn(T_X, j, xt, xt_ready)
                    act.wait_ge(exp_in, i + 1)
                    act.activation(gate[:, :, :], logits[:, :, :], ACT.Exp).then_inc(exp_out, 1)
                    with act.Fori(0, X0 // 2) as j:
                        for e in range(2):
                            for layer, (tile, ready) in enumerate(((h1, h1_ready), (h2, h2_ready))):
                                for half in range(2):
                                    for m in range(KD):
                                        t = layer * 4 + half * 2 + m
                                        col = bass.ds(j * 4 + e * 2 + m, 1)
                                        act.wait_ge(wide_full, i * WIDES + j * 16 + e * 8 + t + 1)
                                        act.sem_inc(pause, 1)
                                        act.activation(tile[:, m, half * HALF:(half + 1) * HALF], wide[t % 4][:, 0:HALF], ACT.Relu,
                                                       bias=keep.bn[:, 2 * layer + 1, col], scale=keep.bn[:, 2 * layer, col]
                                                       ).then_inc(ready, 1)
                                        act.wait_ge(ready, i * X0 * 4 + j * 8 + e * 4 + half * 2 + m + 1)
                                        act.sem_inc(wide_free[t % 4], 1)
                    for half in range(2):
                        t = T_W + half
                        n = 4 if half == 0 else SB - 4
                        act.wait_ge(turn_full, i * TURNS + t + 2)
                        act.copy(gate_t[:, 4 * half:4 * half + n, :], turn[t % 2][0:X0, 0:n * P].rearrange("p (b n) -> p b n", n=P))\
                           .then_inc(gate_t_ready, 1)
                        act.wait_ge(gate_t_ready, i * 2 + half + 1)
                        act.sem_inc(turn_free[t % 2], 1)
                    act.wait_ge(aggr_ready, 2 * i + 2)
                    act.activation(std[:, :], aggr[:, :, 1], ACT.Sqrt, bias=eps[:, 0:1]).then_inc(std_ready, 1)
                    for j in range(4):
                        copy_turn(T_Z, j, at, at_ready)
                    act.wait_ge(rows_out, (i + 1) * 32)
                    act.wait_ge(a1_taken, i + 1)
                    for b in range(SB):
                        for n in range(2):
                            t = C_P + 2 * b + n
                            act.wait_ge(sums_full, i * SUMS_C + t + 2)
                            if n == 0:
                                act.copy(rows[:, b, :], sums[t % 2][:, 0:GROW]).then_inc(rows_ready, 1)
                            else:
                                act.copy(residual[:, b, :], sums[t % 2][:, 0:ROW]).then_inc(rows_ready, 1)
                            act.wait_ge(rows_ready, i * 2 * SB + 2 * b + n + 1)
                            act.sem_inc(sums_free[t % 2], 1)

            @block.vector
            def _(dve):
                seq = Tally(order)

                def then(instruction):
                    seq.done(instruction)
                    dve.wait_ge(order, seq.now)

                for n in range(2):
                    dve.sem_inc(turn_free[n], 1)
                    dve.sem_inc(sums_free[n], 1)
                then(dve.memset(eps[:, :], 1e-5))
                then(dve.memset(a2_top[:, :], -3e38))
                with dve.Fori(0, NSB) as i:
                    seq.enter(i, DVE_MIX)

                    def node(b):
                        return bass.ds(i * SB + b, 1)

                    def layer_norm(nth, after):
                        for b in range(SB):
                            after(b)
                            seq.done(dve.bn_stats(stats[:, b, :], keep.x[:, node(b), :]))
                        dve.wait_ge(order, seq.now)
                        dve.sem_inc(pause, 1)
                        for b in range(SB):
                            last = dve.bn_aggr(aggr[:, b, :], stats[:, b, :])
                        last.then_inc(aggr_ready, 1)
                        dve.wait_ge(std_ready, 2 * i + nth + 1)
                        then(dve.reciprocal(rstd[:, :], std[:, :]))
                        for b in range(SB):
                            dve.tensor_scalar(normed[:, b, :], keep.x[:, node(b), :], aggr[:, b, 0:1], rstd[:, b:b + 1],
                                              ALU.subtract, ALU.mult).then_inc(normed_ready, 1)

                    dve.wait_ge(biased, i + 1)
                    for b in range(SB):
                        dve.wait_ge(sums_full, i * SUMS_C + b + 2)
                        dve.tensor_tensor(keep.x[:, node(b), :], sums[b % 2][:, 0:D].rearrange("p (b d) -> p b d", b=1),
                                          keep.x[:, node(b), :], ALU.add).then_inc(sums_free[b % 2], 1)

                    def after_gin(b):
                        dve.wait_ge(sums_free[b % 2], sums_used(i, b))
                        dve.sem_inc(pause, 1)

                    layer_norm(0, after_gin)
                    for half in range(2):
                        b0, b1 = (0, 4) if half == 0 else (4, SB)
                        t = T_R + half
                        dve.wait_ge(turn_full, i * TURNS + t + 2)
                        dve.tensor_tensor(logits[:, b0:b1, :], turn[t % 2][:, b0 * X0:b1 * X0].rearrange("p (b e) -> p b e", e=X0),
                                          spread(keep.br[:, :].rearrange("p (b e) -> p b e", b=1), [P, b1 - b0, X0]),
                                          ALU.add).then_inc(turn_free[t % 2], 1)
                    for half in range(2):
                        dve.wait_ge(turn_free[half], turn_used(i, T_R + half))
                    every = [P, SB, X0]
                    wide_col = lambda ap: spread(ap.rearrange("p (b e) -> p b e", e=1), every)
                    then(dve.tensor_reduce(top[:, :], logits[:, :, :], AX.X, ALU.max))
                    dve.tensor_tensor(logits[:, :, :], logits[:, :, :], wide_col(top[:, :]), ALU.subtract).then_inc(exp_in, 1)
                    dve.wait_ge(exp_out, i + 1)
                    then(dve.tensor_reduce(top[:, :], gate[:, :, :], AX.X, ALU.add))
                    then(dve.reciprocal(top[:, :], top[:, :]))
                    dve.tensor_tensor(gate[:, :, :], gate[:, :, :], wide_col(top[:, :]), ALU.mult).then_inc(gate_ready, 1)
                    dve.wait_ge(gate_ready, i + 1)
                    dve.sem_inc(pause, 1)
                    with dve.Fori(0, X0 // 2) as j:
                        for e in range(2):
                            for b in range(SB):
                                t = C_E + e * SB + b
                                dve.wait_ge(sums_full, i * SUMS_C + j * 2 * SB + t + 2)
                                dve.wait_ge(sums_free[(t - SB) % 2], i * (SUMS_C // 2) + j * SB + (t - SB) // 2 + 2)
                                dve.scalar_tensor_tensor(keep.x[:, node(b), :], sums[t % 2][:, 0:D].rearrange("p (b d) -> p b d", b=1),
                                                         gate[:, b, bass.ds(j * 2 + e, 1)], keep.x[:, node(b), :],
                                                         ALU.mult, ALU.add).then_inc(sums_free[t % 2], 1)
                    for b in range(SB):
                        t = C_BO + b
                        dve.wait_ge(sums_full, i * SUMS_C + t + 2)
                        dve.wait_ge(sums_free[(t - SB) % 2], sums_used(i, t - SB))
                        dve.tensor_tensor(keep.x[:, node(b), :], sums[t % 2][:, 0:D].rearrange("p (b d) -> p b d", b=1),
                                          keep.x[:, node(b), :], ALU.add).then_inc(sums_free[t % 2], 1)

                    def after_bias(b):
                        dve.wait_ge(sums_free[(C_BO + b) % 2], sums_used(i, C_BO + b))
                        dve.sem_inc(pause, 1)

                    layer_norm(1, after_bias)
                    dve.wait_ge(rows_ready, (i + 1) * 2 * SB)
                    then(dve.tensor_reduce(a2_new[:, :], rows[:, :, D:ROW].rearrange("p b h -> p h b"), AX.X, ALU.max))
                    then(dve.tensor_tensor(a2_top[:, :], a2_top[:, :], a2_new[:, :], ALU.max))
                    dve.tensor_copy(keep.node[:, bass.ds(i * SB, SB), 0:HEADS], residual[:, :, 0:HEADS]).then_inc(a1_taken, 1)
                    seq.leave(NSB)
                dve.wait_ge(a1_taken, NSB + 1)
                dve.wait_ge(node_ready, 1)
                a1, low = keep.node[:, :, 0:HEADS], keep.node[:, :, HEADS:2 * HEADS]
                then(dve.tensor_tensor(shift[:, :, :], a1, spread(keep.a2_bound[:, :].rearrange("p (b h) -> p b h", b=1), [P, NB, HEADS]), ALU.add))
                then(dve.scalar_tensor_tensor(shift[:, :, :], shift[:, :, :], SLOPE, shift[:, :, :], ALU.mult, ALU.max))
                then(dve.scalar_tensor_tensor(low, a1, SLOPE, shift[:, :, :], ALU.mult, ALU.subtract))
                then(dve.tensor_tensor(a1, a1, shift[:, :, :], ALU.subtract))


def attend(nc, io, keep):
    with ExitStack() as ctx:
        s = Scope(nc, ctx, "att")
        cols = s.sb("cols", [P, SLOTS, G, 2], I32)
        rows = s.sb("rows", [P, SLOTS, STEP], I32)
        dst_in = s.sb("dst_in", [P, SLOTS, G])
        is_dst = s.sb("is_dst", [P, SLOTS, G, P])
        to_edge = s.sb("to_edge", [P, SLOTS, G, P])
        gathered = s.sb("gathered", [P, SLOTS, G, GROW])
        terms = s.sb("terms", [P, SLOTS, G, 2, HEADS])
        scores = s.sb("scores", [P, SLOTS, G, HEADS])
        warmed = s.sb("warmed", [P, 1])
        node_ps = [s.ps(f"node_ps{u}", [P, G, 2, HEADS]) for u in range(2)]
        sums_ps = [s.ps(f"sums_ps{u}", [P, ROW]) for u in range(2)]
        acc = keep.xn

        cols_in = s.sems("cols_in", SLOTS)
        rows_in = s.sems("rows_in", SLOTS)
        row_in = s.sems("row_in", LOTS)
        masks_ready = s.sem("masks_ready")
        node_ready = s.sem("node_ready")
        terms_ready = s.sem("terms_ready")
        scores_ready = s.sem("scores_ready")
        p_ready = s.sem("p_ready")
        lot0_ready = s.sem("lot0_ready")
        lot1_ready = s.sem("lot1_ready")
        summed = s.sem("summed")
        added = s.sem("added")
        zeroed = s.sem("zeroed")
        order = s.sem("order")
        turn = s.sem("turn")

        with nc.Block() as block:

            @block.sync
            def _(sp):
                regs = registers(sp, "att_first", SLOTS)
                with sp.Fori(0, ROUNDS) as i:
                    firsts = step_values(sp, regs, keep.step_edge, i, E)
                    for u, first in enumerate(firsts):
                        sp.wait_ge(terms_ready, i * SLOTS + u + 1)
                        sp.sem_inc(turn, 1)
                        sp.dma_start(cols[:, u, :, :].rearrange("p g t -> p (g t)"),
                                     keep.pair_list[bass.ds(first, STEP), :].rearrange("(p g) t -> p (g t)", g=G)
                                     ).then_inc(cols_in[u], 16)
                        sp.dma_start(rows[:, u, :], keep.dst_list[bass.ds(first, STEP)].partition_broadcast(P)
                                     ).then_inc(rows_in[u], 16)

            @block.gpsimd
            def _(pool):
                with pool.Fori(0, ROUNDS) as i:
                    for u in range(SLOTS):
                        pool.wait_ge(cols_in[u], i * 16 + 16)
                        pool.wait_ge(summed, i * SLOTS + u + 1)
                        pool.sem_inc(turn, 1)
                        for g in range(G):
                            pool.indirect_dma_start(
                                out=gathered[:, u, g, :], out_offset=None, in_=keep.rows_dram[:, :],
                                in_offset=bass.IndirectOffsetOnAxis(ap=cols[:, u, g, 0:1], axis=0)).then_inc(row_in[u * G + g], 16)
                for k in range(LOTS):
                    pool.wait_ge(row_in[k], 16 * ROUNDS)

            @block.vector
            def _(dve):
                seq = Tally(order)
                every = [P, G, P]
                dve.sem_inc(added, 2)
                dve.memset(acc[:, :, :], 0.0).then_inc(zeroed, 1)
                dve.wait_ge(zeroed, 1)
                regs = registers(dve, "att_dve", SLOTS)
                with dve.Fori(0, ROUNDS) as i:
                    in_block = step_values(dve, regs, keep.step_block, i, NB - 1)
                    seq.enter(i, SLOTS)

                    def make_masks(u):
                        block_of = bass.ds(in_block[u], 1)
                        dve.wait_ge(cols_in[u], i * 16 + 16)
                        seq.done(dve.tensor_scalar(dst_in[:, u, :], cols[:, u, :, 1], keep.block_base[:, block_of],
                                                   None, ALU.subtract))
                        dve.wait_ge(rows_in[u], i * 16 + 16)
                        dve.wait_ge(summed, i * SLOTS + u + 1)
                        dve.tensor_scalar(to_edge[:, u, :, :], rows[:, u, :].rearrange("p (q g) -> p g q", g=G),
                                          keep.node_id[:, block_of], None, ALU.is_equal).then_inc(masks_ready, 1)
                        dve.wait_ge(order, seq.now)
                        dve.tensor_tensor(is_dst[:, u, :, :], spread(keep.lane[:, :].rearrange("p (g n) -> p g n", g=1), every),
                                          spread(dst_in[:, u, :].rearrange("p (g n) -> p g n", n=1), every),
                                          ALU.is_equal).then_inc(masks_ready, 1)

                    def make_scores(u):
                        dve.wait_ge(node_ready, i * SLOTS + u + 1)
                        for g in range(G):
                            dve.wait_ge(row_in[u * G + g], i * 16 + 16)
                        dve.tensor_tensor(terms[:, u, :, :, :].rearrange("p g t h -> p g (t h)"),
                                          node_ps[u % 2][:, :, :, :].rearrange("p g t h -> p g (t h)"),
                                          gathered[:, u, :, D:GROW], ALU.add).then_inc(terms_ready, 1)
                        dve.wait_ge(terms_ready, i * SLOTS + u + 1 + SLOTS)
                        dve.scalar_tensor_tensor(scores[:, u, :, :], terms[:, u, :, 0, :], 0.0, terms[:, u, :, 1, :],
                                                 ALU.min, ALU.max).then_inc(scores_ready, 1)

                    def weigh(u):
                        dve.wait_ge(p_ready, i * SLOTS + u + 1)
                        row = gathered[:, u, 0, 0:D].rearrange("p (h o) -> p h o", h=HEADS)
                        dve.tensor_tensor(row, row, spread(gathered[:, u, 0, D:ROW].rearrange("p (h o) -> p h o", o=1), [P, HEADS, DO]),
                                          ALU.mult).then_inc(lot0_ready, 1)

                    def add(u):
                        dve.wait_ge(summed, i * SLOTS + u + 1 + SLOTS)
                        dve.wait_ge(added, i * SLOTS + u + 2)
                        here = acc[:, bass.ds(in_block[u], 1), :]
                        dve.tensor_tensor(here, sums_ps[u % 2][:, :].rearrange("p (b d) -> p b d", b=1), here, ALU.add).then_inc(added, 1)

                    for u in range(SLOTS + 3):
                        if u < SLOTS:
                            make_masks(u)
                        if 0 <= u - 1 < SLOTS:
                            make_scores(u - 1)
                        if 0 <= u - 2 < SLOTS:
                            weigh(u - 2)
                        if u >= 3:
                            add(u - 3)
                    seq.leave(ROUNDS)
                dve.wait_ge(added, ROUNDS * SLOTS + 2)

            @block.scalar
            def _(act):
                act.activation(warmed[:, :], keep.ones[:, 0:1], ACT.Exp).then_inc(turn, 1)
                with act.Fori(0, ROUNDS) as i:

                    def exponentials(u):
                        act.wait_ge(scores_ready, i * SLOTS + u + 1)
                        act.activation(gathered[:, u, :, D:ROW], scores[:, u, :, :], ACT.Exp).then_inc(p_ready, 1)

                    def weigh(u):
                        act.wait_ge(p_ready, i * SLOTS + u + 1)
                        for h in range(HEADS):
                            row = gathered[:, u, 1, h * DO:(h + 1) * DO]
                            last = act.activation(row, row, ACT.Copy, scale=gathered[:, u, 1, D + h:D + h + 1])
                        last.then_inc(lot1_ready, 1)

                    exponentials(0)
                    for u in range(1, SLOTS):
                        exponentials(u)
                        weigh(u - 1)
                    weigh(SLOTS - 1)

            @block.tensor
            def _(pe):
                pe.sem_inc(summed, SLOTS)
                pe.sem_inc(terms_ready, SLOTS)
                regs = registers(pe, "att_pe", SLOTS)
                with pe.Fori(0, ROUNDS) as i:
                    in_block = step_values(pe, regs, keep.step_block, i, NB - 1)

                    def expand(u):
                        pe.wait_ge(masks_ready, (i * SLOTS + u) * 2 + 1)
                        pe.wait_ge(terms_ready, i * SLOTS + u - 1 + SLOTS)
                        for g in range(G):
                            last = pe.matmul(node_ps[u % 2][:, g, :, :].rearrange("p t h -> p (t h)"), to_edge[:, u, g, :],
                                             keep.node[:, bass.ds(in_block[u], 1), :].rearrange("p b c -> p (b c)"), start=True, stop=True)
                        last.then_inc(node_ready, 1)

                    def total(u):
                        pe.wait_ge(masks_ready, (i * SLOTS + u) * 2 + 2)
                        pe.wait_ge(lot0_ready, i * SLOTS + u + 1)
                        pe.wait_ge(lot1_ready, i * SLOTS + u + 1)
                        pe.wait_ge(added, i * SLOTS + u + 1)
                        for g in range(G):
                            last = pe.matmul(sums_ps[u % 2][:, :], is_dst[:, u, g, :], gathered[:, u, g, 0:ROW],
                                             start=(g == 0), stop=(g == G - 1))
                        last.then_inc(summed, 1)

                    for u in range(SLOTS + 2):
                        if u < SLOTS:
                            expand(u)
                        if u >= 2:
                            total(u - 2)


def finish_attention(nc, io, keep):
    with ExitStack() as ctx:
        s = Scope(nc, ctx, "fin")
        residual = s.sb("residual", [P, 2, SB, D])
        den = s.sb("den", [P, NB, HEADS])
        stats = s.sb("stats", [P, NB, 6])
        aggr = s.sb("aggr", [P, NB, 2])
        std = s.sb("std", [P, NB])
        rstd = s.sb("rstd", [P, NB])
        eps = s.sb("eps", [P, 1])
        acc, xn = keep.xn, keep.xn
        total = s.ps("total", [P, D])

        residual_in = s.sems("residual_in", 2)
        divided = s.sem("divided")
        outs_ready = s.sem("outs_ready")
        aggr_ready = s.sem("aggr_ready")
        std_ready = s.sem("std_ready")
        normed = s.sem("normed")
        summed = s.sem("summed")
        order = s.sem("order")
        pause = s.sem("pause")

        with nc.Block() as block:

            @block.sync
            def _(sp):
                for i in range(NSB):
                    if i >= 2:
                        sp.wait_ge(outs_ready, i - 1)
                    sp.dma_start(residual[:, i % 2, :, :], keep.residual_dram[i * TOK:(i + 1) * TOK, :].rearrange("(b p) d -> p b d", p=P)
                                 ).then_inc(residual_in[i % 2], 16)

            @block.gpsimd
            def _(pool):
                for i in range(NSB):
                    pool.wait_ge(divided, i + 1)
                    pool.wait_ge(residual_in[i % 2], i // 2 * 16 + 16)
                    here = slice(i * SB, (i + 1) * SB)
                    pool.tensor_tensor(acc[:, here, 0:D], acc[:, here, 0:D], residual[:, i % 2, :, :], ALU.add).then_inc(outs_ready, 1)

            @block.vector
            def _(dve):
                seq = Tally(order)

                def then(instruction):
                    seq.done(instruction)
                    dve.wait_ge(order, seq.now)

                seq.done(dve.memset(eps[:, :], 1e-5))
                then(dve.tensor_scalar(den[:, :, :], acc[:, :, D:ROW], TINY, None, ALU.max))
                then(dve.reciprocal(den[:, :, :], den[:, :, :]))
                heads = lambda ap: ap.rearrange("p b (h o) -> p (b h) o", h=HEADS)

                def divide(i):
                    here = slice(i * SB, (i + 1) * SB)
                    for b in range(i * SB, (i + 1) * SB):
                        row = acc[:, b, 0:D].rearrange("p (h o) -> p h o", h=HEADS)
                        last = dve.tensor_tensor(row, row, spread(den[:, b, :].rearrange("p (h o) -> p h o", o=1), [P, HEADS, DO]), ALU.mult)
                    last.then_inc(divided, 1)

                divide(0)
                for i in range(NSB):
                    if i + 1 < NSB:
                        divide(i + 1)
                    dve.wait_ge(outs_ready, i + 1)
                    here = slice(i * SB, (i + 1) * SB)
                    then(dve.scalar_tensor_tensor(keep.x[:, here, :], acc[:, here, 0:D], 0.0, keep.x[:, here, :], ALU.max, ALU.add))
                    for b in range(i * SB, (i + 1) * SB):
                        last = dve.bn_stats(stats[:, b, :], keep.x[:, b, :])
                    then(last)
                    for b in range(i * SB, (i + 1) * SB):
                        last = dve.bn_aggr(aggr[:, b, :], stats[:, b, :])
                    last.then_inc(aggr_ready, 1)
                    dve.wait_ge(std_ready, i + 1)
                    then(dve.reciprocal(rstd[:, here], std[:, here]))
                    for b in range(i * SB, (i + 1) * SB):
                        last = dve.tensor_scalar(xn[:, b, 0:D], keep.x[:, b, :], aggr[:, b, 0:1], rstd[:, b:b + 1],
                                                 ALU.subtract, ALU.mult)
                    last.then_inc(normed, 1)
                dve.wait_ge(summed, 1)
                then(dve.tensor_copy(keep.node_sum[:, :], total[:, :]))

            @block.scalar
            def _(act):
                for i in range(NSB):
                    act.wait_ge(aggr_ready, i + 1)
                    here = slice(i * SB, (i + 1) * SB)
                    act.activation(std[:, here], aggr[:, here, 1], ACT.Sqrt, bias=eps[:, 0:1]).then_inc(std_ready, 1)

            @block.tensor
            def _(pe):
                for b in range(NB):
                    rows = P if b < NB - 1 else LAST
                    if b % SB == 0:
                        pe.wait_ge(normed, b // SB + 1)
                    last = pe.matmul(total[:, :], keep.ones[0:rows, :], xn[0:rows, b, 0:D], start=(b == 0), stop=(b == NB - 1))
                last.then_inc(summed, 1)


def route(nc, io, keep):
    with ExitStack() as ctx:
        s = Scope(nc, ctx, "route")
        wr = s.sb("wr", [P, KD, X1])
        br = s.sb("br", [P, X1])
        turned = s.sb("turned", [P, KD, P])
        p = s.sb("p", [P, X1])
        load = s.sb("load", [P, X1])
        scale = s.sb("scale", [P, X1])
        over = s.sb("over", [P, X1])
        left = s.sb("left", [P, X1])
        first = s.sb("first", [P, X1])
        peak = s.sb("peak", [P, TOP])
        low = s.sb("low", [P, 1])
        one = s.sb("one", [P, 1])
        gate = s.sb("gate", [P, TOP])
        chosen = s.sb("chosen", [P, TOP], I32)
        b2 = s.sb("b2", [P, TOP, D])
        turned_ps = s.ps("turned_ps", [P, KD, P])
        logits_ps = s.ps("logits_ps", [P, X1])

        params_in = s.sem("params_in")
        turned_over = s.sem("turned_over")
        turned_ready = s.sem("turned_ready")
        logits_ready = s.sem("logits_ready")
        exp_in = s.sem("exp_in")
        exp_out = s.sem("exp_out")
        chosen_ready = s.sem("chosen_ready")
        w1_in = s.sem("w1_in")
        w2_in = s.sem("w2_in")
        order = s.sem("order")

        with nc.Block() as block:

            @block.sync
            def _(sp):
                sp.dma_start(wr[:, :, :], io["L1_ffn_Wr"].rearrange("(k p) e -> p k e", p=P)).then_inc(params_in, 16)
                sp.dma_start(br[:, :], io["L1_ffn_br"].partition_broadcast(P)).then_inc(params_in, 16)
                sp.dma_start(keep.gamma[:, :], io["L1_ffn_gamma"].partition_broadcast(P)).then_inc(params_in, 16)
                sp.dma_start(keep.beta[:, :], io["L1_ffn_beta"].partition_broadcast(P)).then_inc(params_in, 16)
                sp.wait_ge(chosen_ready, TOP)
                regs = registers(sp, "route_expert", TOP)
                sp.load(regs, chosen[0:1, 0:TOP])
                for j, r in enumerate(regs):
                    expert = bass.ds(sp.snap(r, min_val=0, max_val=X1 - 1), 1)
                    sp.dma_start(keep.ew1[:, j, :, :], io["L1_ffn_W1"][expert, :, :].rearrange("e (k p) f -> p (e k) f", p=P)).then_inc(w1_in, 16)
                    with nc.allow_non_contiguous_dma(reason="512 words"):
                        sp.dma_start(keep.eb1[:, j, :], io["L1_ffn_b1"][expert, :].rearrange("e (c p) -> p (e c)", p=P)).then_inc(w1_in, 16)
                    sp.dma_start(keep.ew2[:, j, :, :], io["L1_ffn_W2"][expert, :, :].rearrange("e (c p) d -> p (e c) d", p=P)).then_inc(w2_in, 16)
                    sp.dma_start(b2[:, j, :], io["L1_ffn_b2"][expert, :].rearrange("e d -> (e d)").partition_broadcast(P)).then_inc(w2_in, 16)
                sp.wait_ge(w1_in, 32 * TOP)
                sp.wait_ge(params_in, 64)

            @block.tensor
            def _(pe):
                for k in range(KD):
                    last = pe.transpose(turned_ps[:, k, :], keep.node_sum[:, k * P:(k + 1) * P], keep.ident[:, :])
                last.then_inc(turned_over, 1)
                pe.wait_ge(turned_ready, 1)
                pe.wait_ge(params_in, 64)
                for k in range(KD):
                    last = pe.matmul(logits_ps[:, :], turned[:, k, :], wr[:, k, :], start=(k == 0), stop=(k == KD - 1))
                last.then_inc(logits_ready, 1)

            @block.scalar
            def _(act):
                act.wait_ge(exp_in, 1)
                act.activation(p[:, :], left[:, :], ACT.Exp).then_inc(exp_out, 1)
                act.wait_ge(exp_in, 2)
                act.activation(p[:, :], left[:, :], ACT.Exp).then_inc(exp_out, 1)
                act.wait_ge(exp_in, 3)
                act.activation(gate[:, :], peak[:, :], ACT.Exp).then_inc(exp_out, 1)

            @block.vector
            def _(dve):
                seq = Tally(order)

                def then(instruction):
                    seq.done(instruction)
                    dve.wait_ge(order, seq.now)

                def softmax(out, x, shifted, nth):
                    then(dve.tensor_reduce(low[:, :], x, AX.X, ALU.max))
                    dve.tensor_scalar(shifted, x, low[:, 0:1], None, ALU.subtract).then_inc(exp_in, 1)
                    dve.wait_ge(exp_out, nth)
                    then(dve.tensor_reduce(low[:, :], out, AX.X, ALU.add))
                    then(dve.reciprocal(low[:, :], low[:, :]))
                    then(dve.tensor_scalar(out, out, low[:, 0:1], None, ALU.mult))

                dve.wait_ge(turned_over, 1)
                dve.tensor_scalar(turned[:, :, :], turned_ps[:, :, :], 1.0 / N, None, ALU.mult).then_inc(turned_ready, 1)
                dve.wait_ge(logits_ready, 1)
                dve.wait_ge(params_in, 64)
                then(dve.tensor_tensor(left[:, :], logits_ps[:, :], br[:, :], ALU.add))
                softmax(p[:, :], left[:, :], left[:, :], 1)
                then(dve.tensor_scalar(load[:, :], p[:, :], float(N), None, ALU.mult))
                then(dve.reciprocal(scale[:, :], load[:, :]))
                then(dve.tensor_scalar(scale[:, :], scale[:, :], CAPACITY, 1.0, ALU.mult, ALU.subtract))
                then(dve.tensor_scalar(over[:, :], load[:, :], CAPACITY, None, ALU.is_gt))
                then(dve.tensor_tensor(scale[:, :], scale[:, :], over[:, :], ALU.mult))
                then(dve.scalar_tensor_tensor(left[:, :], scale[:, :], 1.0, p[:, :], ALU.add, ALU.mult))
                softmax(p[:, :], left[:, :], left[:, :], 2)
                lanes = keep.lane[:, 0:X1]
                for j in range(TOP):
                    then(dve.tensor_reduce(peak[:, j:j + 1], p[:, :], AX.X, ALU.max))
                    then(dve.tensor_scalar(over[:, :], p[:, :], peak[:, j:j + 1], None, ALU.is_ge))
                    then(dve.scalar_tensor_tensor(first[:, :], lanes, float(X1), over[:, :], ALU.subtract, ALU.mult))
                    then(dve.tensor_reduce(one[:, :], first[:, :], AX.X, ALU.min))
                    dve.tensor_scalar(chosen[:, j:j + 1], one[:, :], float(X1), None, ALU.add).then_inc(chosen_ready, 1)
                    if j + 1 < TOP:
                        then(dve.tensor_scalar(first[:, :], first[:, :], one[:, 0:1], None, ALU.is_equal))
                        then(dve.scalar_tensor_tensor(p[:, :], first[:, :], -2.0, p[:, :], ALU.mult, ALU.add))
                softmax(gate[:, :], peak[:, :], peak[:, :], 3)
                dve.wait_ge(w2_in, 32 * TOP)
                for j in range(TOP):
                    seq.done(dve.tensor_scalar(keep.ew2[:, j, :, :], keep.ew2[:, j, :, :], gate[:, j:j + 1], None, ALU.mult))
                    seq.done(dve.tensor_scalar(b2[:, j, :], b2[:, j, :], gate[:, j:j + 1], None, ALU.mult))
                dve.wait_ge(order, seq.now)
                then(dve.tensor_tensor(keep.eb2[:, :], b2[:, 0, :], b2[:, 1, :], ALU.add))


CH = F1 // P


def experts(nc, io, keep):
    with ExitStack() as ctx:
        s = Scope(nc, ctx, "ex")
        xt = s.sb("xt", [P, KD, TOK])
        h = s.sb("h", [P, TOP, CH, TOK])
        z = s.sb("z", [P, SB, D])
        stats = s.sb("stats", [P, SB, 6])
        aggr = s.sb("aggr", [P, SB, 2])
        std = s.sb("std", [P, SB])
        rstd = s.sb("rstd", [P, SB])
        eps = s.sb("eps", [P, 1])
        warmed = s.sb("warmed", [P, 1])
        turn = [s.ps(f"turn{n}", [P, KD, 2 * P]) for n in range(2)]
        wide = [s.ps(f"wide{n}", [P, 512]) for n in range(4)]
        sums = [s.ps(f"sums{n}", [P, 512]) for n in range(2)]
        xn = keep.xn

        turned = s.sem("turned")
        xt_ready = s.sem("xt_ready")
        wide_full = s.sem("wide_full")
        h_ready = s.sem("h_ready")
        sums_full = s.sem("sums_full")
        z_ready = s.sem("z_ready")
        biased = s.sem("biased")
        aggr_ready = s.sem("aggr_ready")
        std_ready = s.sem("std_ready")
        z_normed = s.sem("z_normed")
        scaled = s.sem("scaled")
        out_ready = s.sem("out_ready")
        stored = s.sem("stored")
        order = s.sem("order")
        pause = s.sem("pause")
        HW = TOP * CH * 2

        with nc.Block() as block:

            @block.sync
            def _(sp):
                for i in range(NSB):
                    sp.wait_ge(out_ready, i + 1)
                    if i < NSB - 1:
                        sp.dma_start(io["out"][i * TOK:(i + 1) * TOK, :].rearrange("(b p) d -> p b d", p=P),
                                     keep.x[:, i * SB:(i + 1) * SB, :]).then_inc(stored, 16)
                    else:
                        sp.dma_start(io["out"][i * TOK:(NB - 1) * P, :].rearrange("(b p) d -> p b d", p=P),
                                     keep.x[:, i * SB:NB - 1, :]).then_inc(stored, 16)
                        sp.dma_start(io["out"][(NB - 1) * P:N, :], keep.x[0:LAST, NB - 1, :]).then_inc(stored, 16)
                sp.wait_ge(stored, 16 * (NSB + 1))

            @block.tensor
            def _(pe):
                pe.sem_inc(wide_full, 1)
                for i in range(NSB):
                    for j in range(4):
                        t = i * 4 + j
                        if t >= 2:
                            pe.wait_ge(xt_ready, t - 1)
                        for b in turn_blocks(j):
                            for k in range(KD):
                                at0 = (b - 2 * j) * P
                                last = pe.transpose(turn[t % 2][:, k, at0:at0 + P], xn[:, i * SB + b, k * P:(k + 1) * P], keep.ident[:, :])
                        last.then_inc(turned, 1)
                    pe.wait_ge(xt_ready, 4 * i + 4)
                    for e in range(TOP):
                        for c in range(CH):
                            for half in range(2):
                                t = i * HW + (e * CH + c) * 2 + half
                                if t >= 4:
                                    pe.wait_ge(h_ready, t - 3)
                                for k in range(KD):
                                    last = pe.matmul(wide[t % 4][:, 0:HALF], keep.ew1[:, e, k, c * P:(c + 1) * P],
                                                     xt[:, k, half * HALF:(half + 1) * HALF], start=(k == 0), stop=(k == KD - 1))
                                last.then_inc(wide_full, 1)
                    pe.wait_ge(h_ready, (i + 1) * HW)
                    for b in range(SB):
                        t = i * SB + b
                        if t >= 2:
                            pe.wait_ge(z_ready, t - 1)
                        for e in range(TOP):
                            for c in range(CH):
                                last = pe.matmul(sums[t % 2][:, 0:D], h[:, e, c, b * P:(b + 1) * P], keep.ew2[:, e, c, :],
                                                 start=(e == 0 and c == 0), stop=(e == TOP - 1 and c == CH - 1))
                        last.then_inc(sums_full, 1)

            @block.scalar
            def _(act):
                for i in range(NSB):
                    for j in range(4):
                        t = i * 4 + j
                        width = len(turn_blocks(j)) * P
                        act.wait_ge(turned, t + 1)
                        if i >= 1:
                            act.wait_ge(wide_full, i * HW + 1)
                        act.copy(xt[:, :, 2 * j * P:2 * j * P + width], turn[t % 2][:, :, 0:width]).then_inc(xt_ready, 1)
                    for e in range(TOP):
                        for c in range(CH):
                            for half in range(2):
                                t = i * HW + (e * CH + c) * 2 + half
                                act.wait_ge(wide_full, t + 2)
                                if i >= 1:
                                    act.wait_ge(sums_full, i * SB)
                                act.activation(h[:, e, c, half * HALF:(half + 1) * HALF], wide[t % 4][:, 0:HALF], ACT.Gelu,
                                               bias=keep.eb1[:, e, c:c + 1]).then_inc(h_ready, 1)
                    act.wait_ge(aggr_ready, i + 1)
                    act.activation(std[:, :], aggr[:, :, 1], ACT.Sqrt, bias=eps[:, 0:1]).then_inc(std_ready, 1)

            @block.gpsimd
            def _(pool):
                for i in range(NSB):
                    here = slice(i * SB, (i + 1) * SB)
                    wide_row = lambda ap: spread(ap.rearrange("p (b d) -> p b d", b=1), [P, SB, D])
                    pool.wait_ge(turned, 4 * i + 4)
                    pool.tensor_tensor(xn[:, here, 0:D], xn[:, here, 0:D], wide_row(keep.eb2[:, :]), ALU.add).then_inc(biased, 1)
                    pool.tensor_tensor(keep.x[:, here, :], keep.x[:, here, :], wide_row(keep.beta[:, :]), ALU.add).then_inc(biased, 1)
                    pool.wait_ge(z_normed, i + 1)
                    pool.tensor_tensor(z[:, :, :], z[:, :, :], wide_row(keep.gamma[:, :]), ALU.mult).then_inc(scaled, 1)
                    pool.wait_ge(scaled, i + 1)
                    pool.wait_ge(biased, 2 * i + 2)
                    pool.tensor_tensor(keep.x[:, here, :], keep.x[:, here, :], z[:, :, :], ALU.add).then_inc(out_ready, 1)

            @block.vector
            def _(dve):
                seq = Tally(order)

                def then(instruction):
                    seq.done(instruction)
                    dve.wait_ge(order, seq.now)

                then(dve.memset(eps[:, :], 1e-5))
                for i in range(NSB):
                    dve.wait_ge(biased, 2 * i + 1)
                    if i >= 1:
                        dve.wait_ge(out_ready, i)
                    for b in range(SB):
                        t = i * SB + b
                        dve.wait_ge(sums_full, t + 1)
                        dve.tensor_tensor(z[:, b, :], sums[t % 2][:, 0:D], xn[:, t, 0:D], ALU.add).then_inc(z_ready, 1)
                        if b:
                            dve.wait_ge(z_ready, t)
                            last = dve.bn_stats(stats[:, b - 1, :], z[:, b - 1, :])
                    dve.wait_ge(z_ready, (i + 1) * SB)
                    then(dve.bn_stats(stats[:, SB - 1, :], z[:, SB - 1, :]))
                    for b in range(SB):
                        last = dve.bn_aggr(aggr[:, b, :], stats[:, b, :])
                    last.then_inc(aggr_ready, 1)
                    dve.wait_ge(std_ready, i + 1)
                    then(dve.reciprocal(rstd[:, :], std[:, :]))
                    for b in range(SB):
                        last = dve.tensor_scalar(z[:, b, :], z[:, b, :], aggr[:, b, 0:1], rstd[:, b:b + 1], ALU.subtract, ALU.mult)
                    last.then_inc(z_normed, 1)


def program(nc, io, upto=5):
    with ExitStack() as ctx:
        s = Scope(nc, ctx, "keep")
        keep = Kept()
        keep.x = s.sb("x", [P, NB, D])
        keep.xn = s.sb("xn", [P, NB, ROW])
        keep.step_edge = s.sb("step_edge", [1, TABLE * P], I32)
        keep.step_block = s.sb("step_block", [1, TABLE * P], I32)
        keep.ident = s.sb("ident", [P, P])
        keep.below = s.sb("below", [P, P], BF16)
        keep.ones = s.sb("ones", [P, P])
        keep.lane = s.sb("lane", [P, P])
        keep.node_id = s.sb("node_id", [P, NB])
        keep.block_base = s.sb("block_base", [P, NB])
        keep.spare_row = s.sb("spare_row", [P, 1])
        keep.node = s.sb("node", [P, NB, 2 * HEADS])
        keep.a2_bound = s.sb("a2_bound", [P, HEADS])
        keep.added = s.sems("added", LOTS)
        keep.rows_dram = nc.dram_tensor("rows_dram", [NP, GROW], F32, kind="Internal").ap()
        keep.residual_dram = nc.dram_tensor("residual_dram", [NP, D], F32, kind="Internal").ap()
        keep.src_list = nc.dram_tensor("src_list", [E + STEP], I32, kind="Internal").ap()
        keep.dst_list = nc.dram_tensor("dst_list", [E + STEP], I32, kind="Internal").ap()
        keep.pair_list = nc.dram_tensor("pair_list", [E + STEP, 2], I32, kind="Internal").ap()
        keep.table_dram = nc.dram_tensor("table_dram", [2, TABLE * P], I32, kind="Internal").ap()
        keep.partial = [nc.dram_tensor(f"partial{k}", [NP + P, D], F32, kind="Internal").ap() for k in range(SUMS)]
        load_and_index(nc, io, keep)
        if upto >= 1:
            scatter_sums(nc, io, keep)
        with ExitStack() as ctx2:
            w = Scope(nc, ctx2, "w")
            keep.w12 = w.sb("w12", [P, KD, D])
            keep.b12 = w.sb("b12", [P, D])
            keep.wr = w.sb("wr", [P, KD, X0])
            keep.br = w.sb("br", [P, X0])
            keep.bo = w.sb("bo", [X0, D])
            keep.bn = w.sb("bn", [P, 4, 2 * X0])
            keep.proj = w.sb("proj", [P, KD, PROJ])
            if upto >= 2:
                fold_weights(nc, io, keep)
                mixture(nc, io, keep)
        if upto >= 3:
            attend(nc, io, keep)
        with ExitStack() as ctx3:
            w = Scope(nc, ctx3, "last")
            keep.node_sum = w.sb("node_sum", [P, D])
            keep.ew1 = w.sb("ew1", [P, TOP, KD, F1])
            keep.eb1 = w.sb("eb1", [P, TOP, F1 // P])
            keep.ew2 = w.sb("ew2", [P, TOP, F1 // P, D])
            keep.eb2 = w.sb("eb2", [P, D])
            keep.gamma = w.sb("gamma", [P, D])
            keep.beta = w.sb("beta", [P, D])
            if upto >= 4:
                finish_attention(nc, io, keep)
            if upto >= 5:
                route(nc, io, keep)
                experts(nc, io, keep)
        return keep


def kernel(**inputs):
    import numpy as np
    import concourse.bacc as bacc
    from concourse.bass_utils import run_bass_kernel_spmd

    nc = bacc.Bacc("TRN2", target_bir_lowering=False, num_devices=1)
    io, arrays = {}, {}
    for name, value in inputs.items():
        arrays["in_" + name] = np.ascontiguousarray(value)
        io[name] = nc.dram_tensor("in_" + name, value.shape, mybir.dt.from_np(arrays["in_" + name].dtype),
                                           kind="ExternalInput").ap()
    io["out"] = nc.dram_tensor("out", [N, D], F32, kind="ExternalOutput").ap()
    program(nc, io)
    return run_bass_kernel_spmd(nc, [arrays], core_ids=[0]).results[0]["out"]
```

```python
from contextlib import ExitStack

import concourse.bass as bass
from concourse import mybir

F32 = mybir.dt.float32
BF16 = mybir.dt.bfloat16
I32 = mybir.dt.int32
U32 = mybir.dt.uint32
ALU = mybir.AluOpType
ACT = mybir.ActivationFunctionType
AX = mybir.AxisListType
F32R = mybir.dt.float32r

P = 128
N = 6250
E = 200000
D = 256
KD = D // P
NB = -(-N // P)
LAST = N - (NB - 1) * P
NP = NB * P
G = 2
STEP = G * P
STEPS = (E + NB * (STEP - 1)) // STEP
TABLE = -(-STEPS // P)
SLOTS = 8
ROUNDS = -(-STEPS // SLOTS)
LOTS = SLOTS * G
ASLOTS = 16
AROUNDS = -(-STEPS // ASLOTS)
MASKS = 8
TILES = 4
SUMS = 4
LAG = SUMS // G
NOWHERE = 1 << 14
ER = 125
EC = E // ER
H0 = 512
X0 = 8
HEADS, DO = 4, 64
SLOPE = 0.01
ROW = D + HEADS
GROW = D + 2 * HEADS
PROJ = GROW + ROW
TINY = 1e-30
SB = 7
NSB = NB // SB
TOK = SB * P
HALF = TOK // 2
X1, F1 = 8, 512
TOP = 2
CAPACITY = float(-(-N * 5 // (4 * X1)))
DVE_MIX = 21


class Tally:

    def __init__(self, sem):
        self.sem, self.base, self.n, self.outer = sem, 0, 0, []

    def done(self, instruction, by=1):
        instruction.then_inc(self.sem, by)
        self.n += by

    def enter(self, i, per_round):
        self.outer.append((self.base, self.n, per_round))
        self.base, self.n = self.base + self.n + i * per_round, 0

    def leave(self, rounds):
        base, n, per_round = self.outer.pop()
        assert self.n == per_round, (self.sem, self.n, per_round)
        self.base, self.n = base, n + rounds * per_round

    @property
    def now(self):
        return self.base + self.n


class Kept:
    pass


class Scope:

    def __init__(self, nc, ctx, stage):
        self.nc, self.ctx, self.stage, self.used = nc, ctx, stage, []
        ctx.callback(self.free_semaphores)

    def sb(self, name, shape, dtype=F32):
        return self.ctx.enter_context(self.nc.sbuf_tensor(f"{self.stage}_{name}", shape, dtype))

    def ps(self, name, shape, dtype=F32):
        return self.ctx.enter_context(self.nc.psum_tensor(f"{self.stage}_{name}", shape, dtype))

    def sem(self, name):
        self.used.append(self.nc.alloc_semaphore(name=f"{self.stage}_{name}"))
        return self.used[-1]

    def sems(self, name, n):
        return [self.sem(f"{name}{i}") for i in range(n)]

    def free_semaphores(self):
        if self.used:
            self.nc.clear_and_free_semaphores(self.used)
            self.nc.all_engine_barrier()


def spread(ap, shape):
    return ap.to_broadcast(shape)


def registers(eng, name, n):
    return [eng.alloc_register(f"{name}{u}") for u in range(n)]


def step_values(eng, regs, row, i, most):
    eng.load(regs, row[:, bass.ds(i * len(regs), len(regs))])
    return [eng.snap(r, min_val=0, max_val=most) for r in regs]


def load_and_index(nc, io, keep):
    with ExitStack() as ctx:
        s = Scope(nc, ctx, "prep")
        edges = s.sb("edges", [ER, 2, EC], I32)
        pairs = s.sb("pairs", [ER, EC, 2], I32)
        padding = s.sb("padding", [1, 4, STEP], I32)
        bounds = s.sb("bounds", [P, NB + 1])
        bounds_i = s.sb("bounds_i", [P, NB + 1], I32)
        last_dst = s.sb("last_dst", [ER, 1])
        ends_before = s.sb("ends_before", [ER, NB + 1])
        bound = s.sb("bound", [NB + 1, 1])
        row_of = s.sb("row_of", [NB + 1, 1])
        row_index = s.sb("row_index", [NB + 1, 1], I32)
        bound_row = s.sb("bound_row", [NB + 1, EC], I32)
        below_bound = s.sb("below_bound", [NB + 1, EC])
        start = s.sb("start", [NB + 1, 1])
        diagonal = s.sb("diagonal", [NB + 1, NB + 1])
        starts = s.sb("starts", [P, NB + 1])
        count = s.sb("count", [P, NB])
        nsteps_i = s.sb("nsteps_i", [P, NB], I32)
        nsteps = s.sb("nsteps", [P, NB])
        until = s.sb("until", [P, NB])
        zeros = s.sb("zeros", [P, 512])
        step_i = s.sb("step_i", [P, TABLE], I32)
        step_id = s.sb("step_id", [P, TABLE])
        past = s.sb("past", [P, TABLE, NB])
        part = s.sb("part", [P, TABLE, NB])
        block_of = s.sb("block_of", [P, TABLE])
        before = s.sb("before", [P, TABLE])
        edge0 = s.sb("edge0", [P, TABLE])
        inside = s.sb("inside", [P, TABLE])
        table = s.sb("table", [P, 2, TABLE], I32)
        ints = s.sb("ints", [P, P], I32)
        small_i = s.sb("small_i", [P, 2 * NB + 1], I32)
        stats = s.sb("stats", [P, NB, 6])
        aggr = s.sb("aggr", [P, NB, 2])
        std = s.sb("std", [P, NB])
        rstd = s.sb("rstd", [P, NB])
        eps = s.sb("eps", [P, 1])
        row_ps = s.ps("row_ps", [NB + 1, 1])
        total = s.ps("total", [P, NB + 1])

        x_in = s.sem("x_in")
        x_last = s.sem("x_last")
        edges_in = s.sem("edges_in")
        x_pad = s.sem("x_pad")
        made = s.sem("made")
        consts = s.sem("consts")
        ends_compared = s.sem("ends_compared")
        row_found = s.sem("row_found")
        row_ready = s.sem("row_ready")
        row_in = s.sem("row_in")
        start_ready = s.sem("start_ready")
        summed = s.sem("summed")
        stats_done = s.sem("stats_done")
        std_done = s.sem("std_done")
        edges_out = s.sem("edges_out")
        table_ready = s.sem("table_ready")
        table_io = s.sem("table_io")
        pairs_ready = s.sem("pairs_ready")
        pads_ready = s.sem("pads_ready")
        order = s.sem("order")
        xn_ready = s.sem("xn_ready")
        spare_out = s.sem("spare_out")

        with nc.Block() as block:

            @block.sync
            def _(sp):
                sp.dma_start(edges[:, 0, :], io["src"].rearrange("(p c) -> p c", p=ER)).then_inc(edges_in, 16)
                sp.dma_start(edges[:, 1, :], io["dst"].rearrange("(p c) -> p c", p=ER)).then_inc(edges_in, 16)
                blocks = io["x"][0:(NB - 1) * P, :].rearrange("(b p) d -> p b d", p=P)
                for b in range(0, NB - 1, 12):
                    sp.dma_start(keep.x[:, b:b + 12, :], blocks[:, b:b + 12, :]).then_inc(x_in, 16)
                sp.wait_ge(x_pad, 1)
                sp.dma_start(keep.x[0:LAST, NB - 1, :], io["x"][(NB - 1) * P:N, :]).then_inc(x_last, 16)
                sp.wait_ge(edges_in, 32)
                sp.dma_start(keep.src_list[0:E].rearrange("(p c) -> p c", p=ER), edges[:, 0, :]).then_inc(edges_out, 16)
                sp.dma_start(keep.dst_list[0:E].rearrange("(p c) -> p c", p=ER), edges[:, 1, :]).then_inc(edges_out, 16)
                sp.wait_ge(pads_ready, 3)
                one = lambda ap: ap.rearrange("(a c) -> a c", a=1)
                sp.dma_start(one(keep.src_list[E:E + STEP]), padding[:, 0, :]).then_inc(edges_out, 16)
                sp.dma_start(one(keep.dst_list[E:E + STEP]), padding[:, 1, :]).then_inc(edges_out, 16)
                sp.dma_start(keep.pair_list[E:E + STEP, :].rearrange("(a c) t -> a (c t)", a=1),
                             padding[:, 2:4, :].rearrange("p a b -> p (a b)")).then_inc(edges_out, 16)
                sp.wait_ge(pairs_ready, 2)
                sp.dma_start(keep.pair_list[0:E, :].rearrange("(p c) t -> p (c t)", p=ER),
                             pairs[:, :, :].rearrange("p c t -> p (c t)")).then_inc(edges_out, 16)
                sp.wait_ge(table_ready, 1)
                for t in range(2):
                    sp.dma_start(keep.table_dram[t:t + 1, :].rearrange("t (p j) -> p (t j)", p=P), table[:, t, :]).then_inc(table_io, 16)
                sp.wait_ge(table_io, 32)
                sp.dma_start(keep.step_edge[:, :], keep.table_dram[0:1, :]).then_inc(table_io, 16)
                sp.dma_start(keep.step_block[:, :], keep.table_dram[1:2, :]).then_inc(table_io, 16)
                sp.wait_ge(table_io, 64)
                sp.wait_ge(edges_out, 96)

            @block.gpsimd
            def _(pool):
                made_n = Tally(made)
                made_n.done(pool.memset(zeros[:, :], 0.0))
                made_n.done(pool.memset(keep.ident[:, :], 0.0))
                made_n.done(pool.memset(keep.below[:, :], 1.0))
                pool.memset(keep.ones[:, :], 1.0).then_inc(consts, 1)
                pool.wait_ge(made, 3)
                pool.affine_select(out=keep.ident[:, :], in_=keep.ident[:, :], compare_op=ALU.not_equal, fill=1.0,
                                   base=0, pattern=[[-1, P]], channel_multiplier=1).then_inc(consts, 1)
                pool.affine_select(out=keep.below[:, :], in_=keep.below[:, :], compare_op=ALU.is_gt, fill=0.0,
                                   base=0, pattern=[[-1, P]], channel_multiplier=1).then_inc(consts, 1)
                made_n.done(pool.iota(ints[:, :], pattern=[[1, P]], base=0, channel_multiplier=0))
                made_n.done(pool.iota(bounds_i[:, :], pattern=[[P, NB + 1]], base=0, channel_multiplier=0))
                made_n.done(pool.iota(small_i[:, 0:NB], pattern=[[P, NB]], base=0, channel_multiplier=1))
                made_n.done(pool.iota(small_i[:, NB:2 * NB], pattern=[[P, NB]], base=0, channel_multiplier=0))
                made_n.done(pool.iota(small_i[:, 2 * NB:2 * NB + 1], pattern=[[0, 1]], base=NP, channel_multiplier=1))
                made_n.done(pool.iota(step_i[:, :], pattern=[[1, TABLE]], base=0, channel_multiplier=TABLE))
                pool.wait_ge(row_ready, 1)
                pool.indirect_dma_start(out=bound_row[:, :], out_offset=None, in_=io["dst"].rearrange("(p c) -> p c", p=ER),
                                        in_offset=bass.IndirectOffsetOnAxis(ap=row_index[:, 0:1], axis=0)).then_inc(row_in, 16)
                part_rows = (NP + P) * SUMS // LOTS
                for k in range(LOTS):
                    if k % SUMS == 0:
                        continue
                    rows = keep.partial[k % SUMS][k // SUMS * part_rows:(k // SUMS + 1) * part_rows, :]
                    pool.dma_start(rows.rearrange("(p a) d -> p a d", p=64),
                                   spread(zeros[0:64, 0:D].rearrange("p (a d) -> p a d", a=1), [64, part_rows // 64, D]),
                                   ).then_inc(keep.added[k], 16)
                pool.wait_ge(xn_ready, NB)
                quarters = [NB * n // SUMS for n in range(SUMS + 1)]
                for n in range(SUMS):
                    b0, b1 = quarters[n], quarters[n + 1]
                    pool.dma_start(keep.partial[0][b0 * P:b1 * P, :].rearrange("(b p) d -> p b d", p=P),
                                   keep.xn[:, b0:b1, 0:D]).then_inc(keep.added[n * SUMS], 16)
                pool.dma_start(keep.partial[0][NP:NP + P, :], zeros[:, 0:D]).then_inc(spare_out, 16)
                pool.wait_ge(spare_out, 16)
                for k in range(LOTS):
                    pool.wait_ge(keep.added[k], 16)

            @block.scalar
            def _(act):
                act.wait_ge(stats_done, 1)
                act.activation(std[:, :], aggr[:, :, 1], ACT.Sqrt, bias=eps[:, 0:1]).then_inc(std_done, 1)

            @block.tensor
            def _(pe):
                pe.wait_ge(ends_compared, 1)
                pe.wait_ge(consts, 4)
                pe.matmul(row_ps[:, :], ends_before[:, :], keep.ones[0:ER, 0:1], start=True, stop=True).then_inc(row_found, 1)
                pe.wait_ge(start_ready, 1)
                pe.matmul(total[:, :], keep.ones[0:NB + 1, :], diagonal[:, :], start=True, stop=True).then_inc(summed, 1)

            @block.vector
            def _(dve):
                seq = Tally(order)

                def then(instruction):
                    seq.done(instruction)
                    dve.wait_ge(order, seq.now)

                dve.memset(keep.x[:, NB - 1, :], 0.0).then_inc(x_pad, 1)
                seq.done(dve.memset(eps[:, :], 1e-5))
                dve.memset(padding[:, 0, :], 0).then_inc(pads_ready, 1)
                dve.memset(padding[:, 1, :], NOWHERE).then_inc(pads_ready, 1)
                then(dve.memset(padding[:, 2:4, :], 0))
                dve.memset(padding[:, 2:4, :].rearrange("p a (b t) -> p (a b) t", t=2)[:, :, 1], NOWHERE).then_inc(pads_ready, 1)
                dve.wait_ge(made, 9)
                then(dve.tensor_copy(keep.lane[:, :], ints[:, :]))
                then(dve.tensor_scalar(bounds[:, :], bounds_i[:, :], 0.5, None, ALU.subtract))
                then(dve.tensor_copy(keep.node_id[:, :], small_i[:, 0:NB]))
                then(dve.tensor_copy(keep.block_base[:, :], small_i[:, NB:2 * NB]))
                then(dve.tensor_copy(keep.spare_row[:, :], small_i[:, 2 * NB:2 * NB + 1]))
                dve.tensor_copy(step_id[:, :], step_i[:, :]).then_inc(consts, 1)
                dve.wait_ge(edges_in, 32)
                then(dve.tensor_copy(last_dst[:, :], edges[:, 1, EC - 1:EC]))
                dve.tensor_scalar(ends_before[:, :], bounds[0:ER, :], last_dst[:, 0:1], None, ALU.is_gt).then_inc(ends_compared, 1)
                then(dve.tensor_scalar(bound[:, :], keep.node_id[0:NB + 1, 0:1], float(P), 0.5, ALU.mult, ALU.subtract))
                dve.wait_ge(row_found, 1)
                then(dve.tensor_scalar(row_of[:, :], row_ps[:, :], float(ER - 1), None, ALU.min))
                dve.tensor_copy(row_index[:, :], row_of[:, :]).then_inc(row_ready, 1)
                dve.tensor_copy(pairs[:, :, 0], edges[:, 0, :]).then_inc(pairs_ready, 1)
                dve.tensor_copy(pairs[:, :, 1], edges[:, 1, :]).then_inc(pairs_ready, 1)
                dve.wait_ge(x_in, 64)
                dve.wait_ge(x_last, 16)
                dve.wait_ge(x_pad, 1)
                dve.wait_ge(order, seq.now)
                with dve.Fori(0, NB) as b:
                    seq.enter(b, 1)
                    seq.done(dve.bn_stats(stats[:, bass.ds(b, 1), :], keep.x[:, bass.ds(b, 1), :]))
                    seq.leave(NB)
                dve.wait_ge(order, seq.now)
                for b in range(NB):
                    last = dve.bn_aggr(aggr[:, b, :], stats[:, b, :])
                last.then_inc(stats_done, 1)
                dve.wait_ge(std_done, 1)
                then(dve.reciprocal(rstd[:, :], std[:, :]))
                with dve.Fori(0, NB) as b:
                    dve.tensor_scalar(keep.xn[:, bass.ds(b, 1), 0:D], keep.x[:, bass.ds(b, 1), :],
                                      aggr[:, bass.ds(b, 1), 0], rstd[:, bass.ds(b, 1)],
                                      ALU.subtract, ALU.mult).then_inc(xn_ready, 1)
                dve.wait_ge(row_in, 16)
                then(dve.tensor_scalar(below_bound[:, :], bound_row[:, :], bound[:, 0:1], None, ALU.is_lt))
                then(dve.tensor_reduce(start[:, :], below_bound[:, :], AX.X, ALU.add))
                then(dve.scalar_tensor_tensor(start[:, :], row_of[:, :], float(EC), start[:, :], ALU.mult, ALU.add))
                dve.wait_ge(consts, 4)
                dve.tensor_scalar(diagonal[:, :], keep.ident[0:NB + 1, 0:NB + 1], start[:, 0:1], None, ALU.mult).then_inc(start_ready, 1)
                dve.wait_ge(summed, 1)
                then(dve.tensor_copy(starts[:, :], total[:, :]))
                then(dve.tensor_tensor(count[:, :], starts[:, 1:NB + 1], starts[:, 0:NB], ALU.subtract))
                then(dve.tensor_scalar(nsteps_i[:, :], count[:, :], float(STEP - 1), None, ALU.add))
                then(dve.tensor_scalar(nsteps_i[:, :], nsteps_i[:, :], STEP.bit_length() - 1, None, ALU.logical_shift_right))
                then(dve.tensor_copy(nsteps[:, :], nsteps_i[:, :]))
                dve.wait_ge(made, 1)
                then(dve.tensor_tensor_scan(until[:, :], nsteps[:, :], zeros[:, 0:NB], 0.0, ALU.add, ALU.add))
                every = [P, TABLE, NB]
                row = lambda ap: spread(ap.rearrange("p (j b) -> p j b", j=1), every)
                dve.wait_ge(consts, 4)
                then(dve.tensor_tensor(past[:, :, :], row(until[:, :]),
                                       spread(step_id[:, :].rearrange("p (j b) -> p j b", b=1), every), ALU.is_le))
                then(dve.tensor_reduce(block_of[:, :], past[:, :, :], AX.X, ALU.add))
                then(dve.tensor_tensor(part[:, :, :], past[:, :, :], row(count[:, :]), ALU.mult))
                then(dve.tensor_reduce(edge0[:, :], part[:, :, :], AX.X, ALU.add))
                then(dve.tensor_tensor(part[:, :, :], past[:, :, :], row(until[:, :]), ALU.mult))
                then(dve.tensor_reduce(before[:, :], part[:, :, :], AX.X, ALU.max))
                then(dve.tensor_tensor(inside[:, :], step_id[:, :], before[:, :], ALU.subtract))
                then(dve.scalar_tensor_tensor(edge0[:, :], inside[:, :], float(STEP), edge0[:, :], ALU.mult, ALU.add))
                then(dve.tensor_scalar(table[:, 0, :], edge0[:, :], float(E), None, ALU.min))
                dve.tensor_scalar(table[:, 1, :], block_of[:, :], float(NB - 1), None, ALU.min).then_inc(table_ready, 1)
                dve.wait_ge(order, seq.now)


def scatter_sums(nc, io, keep):
    with ExitStack() as ctx:
        s = Scope(nc, ctx, "scat")
        cols = s.sb("cols", [P, SLOTS, G, 2], I32)
        rows = s.sb("rows", [P, SLOTS, STEP], I32)
        dst_in = s.sb("dst_in", [P, SLOTS, G])
        is_dst = s.sb("is_dst", [P, SLOTS, G, P], BF16)
        same = s.sb("same", [P, SLOTS, G, P], BF16)
        junk = s.sb("junk", [P, 2, G, P], BF16)
        repeated = s.sb("repeated", [P, SLOTS, G])
        to_spare = s.sb("to_spare", [P, SLOTS, G])
        index = s.sb("index", [P, SLOTS, G], I32)
        merge = s.sb("merge", [P, SLOTS, G, P])
        values = s.sb("values", [P, SLOTS, G, D])
        merge_ps = [s.ps(f"merge_ps{u}", [P, G, P]) for u in range(2)]
        values_ps = [s.ps(f"values_ps{u}", [P, G, D]) for u in range(2)]

        cols_in = s.sems("cols_in", SLOTS)
        rows_in = s.sems("rows_in", SLOTS)
        masks_ready = s.sem("masks_ready")
        index_ready = s.sem("index_ready")
        merged = s.sem("merged")
        merge_ready = s.sem("merge_ready")
        summed = s.sem("summed")
        values_ready = s.sem("values_ready")
        lists_free = s.sem("lists_free")
        order = s.sem("order")
        turn = s.sem("turn")

        with nc.Block() as block:

            @block.sync
            def _(sp):
                regs = registers(sp, "scat_first", SLOTS)
                with sp.Fori(0, ROUNDS) as i:
                    firsts = step_values(sp, regs, keep.step_edge, i, E)
                    for u, first in enumerate(firsts):
                        sp.wait_ge(lists_free, i * SLOTS + u + 1)
                        sp.sem_inc(turn, 1)
                        sp.dma_start(cols[:, u, :, :].rearrange("p g t -> p (g t)"),
                                     keep.pair_list[bass.ds(first, STEP), :].rearrange("(p g) t -> p (g t)", g=G)
                                     ).then_inc(cols_in[u], 16)
                        sp.dma_start(rows[:, u, :], keep.src_list[bass.ds(first, STEP)].partition_broadcast(P)
                                     ).then_inc(rows_in[u], 16)

            @block.vector
            def _(dve):
                seq = Tally(order)

                def then(instruction):
                    seq.done(instruction)
                    dve.wait_ge(order, seq.now)

                every = [P, G, P]
                dve.sem_inc(lists_free, SLOTS)
                regs = registers(dve, "scat_dve", SLOTS)
                with dve.Fori(0, ROUNDS) as i:
                    in_block = step_values(dve, regs, keep.step_block, i, NB - 1)
                    seq.enter(i, SLOTS * (2 + G))

                    def write_index(u):
                        for g in range(G):
                            dve.wait_ge(keep.added[u * G + g], i * 16 + 16)
                        dve.wait_ge(order, ready[u])
                        for g in range(G):
                            last = dve.scalar_tensor_tensor(index[:, u, g:g + 1], to_spare[:, u, g:g + 1],
                                                            repeated[:, u, g:g + 1], cols[:, u, g:g + 1, 0],
                                                            ALU.mult, ALU.add)
                        last.then_inc(index_ready, 1)

                    ready = {}
                    for u in range(SLOTS):
                        src = cols[:, u, :, 0]
                        dve.wait_ge(cols_in[u], i * 16 + 16)
                        seq.done(dve.tensor_scalar(dst_in[:, u, :], cols[:, u, :, 1], keep.block_base[:, bass.ds(in_block[u], 1)],
                                                   None, ALU.subtract))
                        dst_done = seq.now
                        dve.wait_ge(merged, i * SLOTS + u + 1)
                        dve.wait_ge(rows_in[u], i * 16 + 16)
                        dve.tensor_tensor(same[:, u, :, :], rows[:, u, :].rearrange("p (q g) -> p g q", g=G),
                                          spread(src.rearrange("p (g n) -> p g n", n=1), every),
                                          ALU.is_equal).then_inc(masks_ready, 1)
                        seq.done(dve.tensor_scalar(to_spare[:, u, :], src, -1.0, keep.spare_row[:, 0:1], ALU.mult, ALU.add))
                        if u:
                            write_index(u - 1)
                        dve.wait_ge(order, dst_done)
                        dve.tensor_tensor(is_dst[:, u, :, :], spread(keep.lane[:, :].rearrange("p (g n) -> p g n", g=1), every),
                                          spread(dst_in[:, u, :].rearrange("p (g n) -> p g n", n=1), every),
                                          ALU.is_equal).then_inc(masks_ready, 1)
                        dve.wait_ge(masks_ready, (i * SLOTS + u) * 2 + 1)
                        dve.sem_inc(turn, 1)
                        for g in range(G):
                            seq.done(dve.tensor_tensor_reduce(out=junk[:, u % 2, g, :], in0=same[:, u, g, :], in1=keep.below[:, :],
                                                              scale=1.0, scalar=0.0, op0=ALU.mult, op1=ALU.max,
                                                              accum_out=repeated[:, u, g:g + 1]))
                        ready[u] = seq.now
                        if u:
                            dve.wait_ge(index_ready, i * SLOTS + u)
                            dve.sem_inc(lists_free, 1)
                    write_index(SLOTS - 1)
                    dve.wait_ge(index_ready, i * SLOTS + SLOTS)
                    dve.sem_inc(lists_free, 1)
                    seq.leave(ROUNDS)

            @block.tensor
            def _(pe):
                pe.sem_inc(merged, SLOTS)
                regs = registers(pe, "scat_pe", SLOTS)
                with pe.Fori(0, ROUNDS) as i:
                    in_block = step_values(pe, regs, keep.step_block, i, NB - 1)

                    def merge_edges(u):
                        pe.wait_ge(masks_ready, (i * SLOTS + u) * 2 + 2)
                        for g in range(G):
                            last = pe.matmul(merge_ps[u % 2][:, g, :], is_dst[:, u, g, :], same[:, u, g, :], start=True, stop=True)
                        last.then_inc(merged, 1)

                    def sum_values(u):
                        pe.wait_ge(merge_ready, i * SLOTS + u + 1)
                        for g in range(G):
                            last = pe.matmul(values_ps[u % 2][:, g, :], merge[:, u, g, :], keep.xn[:, bass.ds(in_block[u], 1), 0:D],
                                             start=True, stop=True)
                        last.then_inc(summed, 1)

                    merge_edges(0)
                    for u in range(1, SLOTS):
                        merge_edges(u)
                        sum_values(u - 1)
                    sum_values(SLOTS - 1)

            @block.scalar
            def _(act):
                with act.Fori(0, ROUNDS) as i:

                    def copy_merge(u):
                        act.wait_ge(merged, i * SLOTS + u + 1 + SLOTS)
                        act.copy(merge[:, u, :, :], merge_ps[u % 2][:, :, :]).then_inc(merge_ready, 1)

                    def copy_values(u):
                        act.wait_ge(summed, i * SLOTS + u + 1)
                        for g in range(G):
                            act.wait_ge(keep.added[u * G + g], i * 16 + 16)
                        act.copy(values[:, u, :, :], values_ps[u % 2][:, :, :]).then_inc(values_ready, 1)

                    copy_merge(0)
                    for u in range(1, SLOTS):
                        copy_merge(u)
                        copy_values(u - 1)
                    copy_values(SLOTS - 1)

            @block.gpsimd
            def _(pool):
                with pool.Fori(0, ROUNDS) as i:
                    for u in range(SLOTS):
                        pool.wait_ge(index_ready, i * SLOTS + u + 1)
                        pool.wait_ge(values_ready, i * SLOTS + u + 1)
                        pool.sem_inc(turn, 1)
                        for g in range(G):
                            k = u * G + g
                            pool.wait_ge(keep.added[(k - SUMS) % LOTS], i * 16 + (16 if u < LAG else 32))
                            pool.sem_inc(turn, 1)
                            pool.indirect_dma_start(
                                out=keep.partial[k % SUMS], out_offset=bass.IndirectOffsetOnAxis(ap=index[:, u, g:g + 1], axis=0),
                                in_=values[:, u, g, :], in_offset=None, compute_op=ALU.add).then_inc(keep.added[k], 16)
                for k in range(LOTS):
                    pool.wait_ge(keep.added[k], 16 * (ROUNDS + 1))


def fold_weights(nc, io, keep):
    with ExitStack() as ctx:
        s = Scope(nc, ctx, "fold")
        w1 = s.sb("w1", [P, KD, H0])
        w2 = s.sb("w2", [P, H0 // P, D])
        w1t = s.sb("w1t", [P, H0 // P, D])
        b1 = s.sb("b1", [P, H0 // P])
        b1_wide = s.sb("b1_wide", [P, H0 // P, P])
        b2 = s.sb("b2", [P, D])
        norms = s.sb("norms", [2 * X0, 2, 5, P])
        root = s.sb("root", [2 * X0, 2, P])
        eps = s.sb("eps", [P, 1])
        lines = s.sb("lines", [2 * X0, 4, P])
        al = s.sb("al", [P, 2, D])
        prod = s.sb("prod", [P, KD, 2, HEADS, DO])
        w1t_ps = [s.ps(f"w1t_ps{k}", [P, H0 // P, P]) for k in range(KD)]
        w12_ps = s.ps("w12_ps", [P, KD, D])
        b12_ps = s.ps("b12_ps", [P, D])
        norm_ps = s.ps("norm_ps", [P, 4, 2 * X0])

        w_in = s.sem("w_in")
        b_in = s.sem("b_in")
        norms_in = s.sem("norms_in")
        heads_in = s.sem("heads_in")
        others_in = s.sem("others_in")
        w1_turned = s.sem("w1_turned")
        w1t_ready = s.sem("w1t_ready")
        wide_ready = s.sem("wide_ready")
        w12_done = s.sem("w12_done")
        b12_done = s.sem("b12_done")
        var_ready = s.sem("var_ready")
        root_ready = s.sem("root_ready")
        lines_ready = s.sem("lines_ready")
        norm_done = s.sem("norm_done")
        order = s.sem("order")

        with nc.Block() as block:

            @block.sync
            def _(sp):
                sp.dma_start(w1[:, :, :], io["L0_gnn_W1"].rearrange("(k p) h -> p k h", p=P)).then_inc(w_in, 16)
                sp.dma_start(w2[:, :, :], io["L0_gnn_W2"].rearrange("(c p) d -> p c d", p=P)).then_inc(w_in, 16)
                with nc.allow_non_contiguous_dma(reason="512 words"):
                    sp.dma_start(b1[:, :], io["L0_gnn_b1"].rearrange("(c p) -> p c", p=P)).then_inc(b_in, 16)
                sp.dma_start(b2[:, :], io["L0_gnn_b2"].partition_broadcast(P)).then_inc(b_in, 16)
                for layer, names in enumerate((("g1", "be1", "m1", "v1", "b1"), ("g2", "be2", "m2", "v2", "b2"))):
                    vectors = (io["L0_ffn_g1"], io["L0_ffn_be1"], io["L0_ffn_m1"], io["L0_ffn_v1"], io["L0_ffn_b1"]) if layer == 0 else \
                              (io["L0_ffn_g2"], io["L0_ffn_be2"], io["L0_ffn_m2"], io["L0_ffn_v2"], io["L0_ffn_b2"])
                    for n, v in enumerate(vectors):
                        sp.dma_start(norms[:, layer, n, :], v.rearrange("e (c p) -> (e c) p", p=P)).then_inc(norms_in, 16)
                for k in range(KD):
                    rows = slice(k * P, (k + 1) * P)
                    sp.dma_start(keep.proj[:, k, 0:D].rearrange("p (h o) -> p h o", h=HEADS),
                                 io["L1_gnn_W_fc"][:, rows, :].rearrange("h p o -> p h o")).then_inc(heads_in, 16)
                    sp.dma_start(keep.proj[:, k, GROW + HEADS:PROJ].rearrange("p (h o) -> p h o", h=HEADS),
                                 io["L1_gnn_W_res"][:, rows, :].rearrange("h p o -> p h o")).then_inc(others_in, 16)
                sp.dma_start(al[:, 0, :], io["L1_gnn_W_ar"].rearrange("h o a -> (h o a)").partition_broadcast(P)).then_inc(heads_in, 16)
                sp.dma_start(al[:, 1, :], io["L1_gnn_W_al"].rearrange("h o a -> (h o a)").partition_broadcast(P)).then_inc(heads_in, 16)
                sp.dma_start(keep.wr[:, :, :], io["L0_ffn_Wr"].rearrange("(k p) e -> p k e", p=P)).then_inc(others_in, 16)
                sp.dma_start(keep.br[:, :], io["L0_ffn_br"].partition_broadcast(P)).then_inc(others_in, 16)
                sp.dma_start(keep.bo[:, :], io["L0_ffn_bo"]).then_inc(others_in, 16)
                sp.wait_ge(others_in, 16 * (KD + 3))

            @block.tensor
            def _(pe):
                pe.wait_ge(w_in, 32)
                for k in range(KD):
                    for c in range(H0 // P):
                        last = pe.transpose(w1t_ps[k][:, c, :], w1[:, k, c * P:(c + 1) * P], keep.ident[:, :])
                last.then_inc(w1_turned, 1)
                pe.wait_ge(b_in, 32)
                pe.wait_ge(wide_ready, 1)
                for c in range(H0 // P):
                    last = pe.matmul(b12_ps[:, :], b1_wide[:, c, :], w2[:, c, :], start=(c == 0), stop=(c == H0 // P - 1))
                last.then_inc(b12_done, 1)
                pe.wait_ge(w1t_ready, KD)
                for k in range(KD):
                    for c in range(H0 // P):
                        last = pe.matmul(w12_ps[:, k, :], w1t[:, c, k * P:(k + 1) * P], w2[:, c, :],
                                         start=(c == 0), stop=(c == H0 // P - 1))
                last.then_inc(w12_done, 1)
                pe.wait_ge(lines_ready, 4)
                for n in range(4):
                    last = pe.transpose(norm_ps[:, n, :], lines[:, n, :], keep.ident[0:2 * X0, 0:2 * X0])
                last.then_inc(norm_done, 1)

            @block.scalar
            def _(act):
                act.wait_ge(w1_turned, 1)
                for k in range(KD):
                    act.copy(w1t[:, :, k * P:(k + 1) * P], w1t_ps[k][:, :, :]).then_inc(w1t_ready, 1)
                act.wait_ge(var_ready, 1)
                act.wait_ge(norms_in, 160)
                act.activation(root[:, :, :], norms[:, :, 3, :], ACT.Sqrt, bias=eps[0:2 * X0, 0:1]).then_inc(root_ready, 1)

            @block.vector
            def _(dve):
                seq = Tally(order)

                def then(instruction):
                    seq.done(instruction)
                    dve.wait_ge(order, seq.now)

                dve.memset(eps[:, :], 1e-3).then_inc(var_ready, 1)
                dve.wait_ge(b_in, 32)
                dve.tensor_copy(b1_wide[:, :, :], spread(b1[:, :].rearrange("p (c n) -> p c n", n=1), [P, H0 // P, P]))\
                   .then_inc(wide_ready, 1)
                dve.wait_ge(root_ready, 1)
                then(dve.reciprocal(root[:, :, :], root[:, :, :]))
                for layer in range(2):
                    g, be, m, v, b = (norms[:, layer, n, :] for n in range(5))
                    scale, shift = lines[:, 2 * layer, :], lines[:, 2 * layer + 1, :]
                    dve.tensor_tensor(scale, g, root[:, layer, :], ALU.mult).then_inc(lines_ready, 1)
                    then(dve.tensor_tensor(b, b, m, ALU.subtract))
                    dve.wait_ge(lines_ready, 2 * layer + 1)
                    then(dve.tensor_tensor(b, b, scale, ALU.mult))
                    dve.tensor_tensor(shift, b, be, ALU.add).then_inc(lines_ready, 1)
                dve.wait_ge(heads_in, 16 * (KD + 2))
                for k in range(KD):
                    for n in range(2):
                        then(dve.tensor_tensor(prod[:, k, n, :, :], keep.proj[:, k, 0:D].rearrange("p (h o) -> p h o", h=HEADS),
                                               al[:, n, :].rearrange("p (h o) -> p h o", h=HEADS), ALU.mult))
                        at = D + 2 * n * HEADS
                        seq.done(dve.tensor_reduce(keep.proj[:, k, at:at + HEADS], prod[:, k, n, :, :], AX.X, ALU.add))
                dve.wait_ge(order, seq.now)
                seq.done(dve.tensor_scalar(keep.proj[:, :, D + HEADS:GROW], keep.proj[:, :, D:ROW], SLOPE, None, ALU.mult))
                dve.wait_ge(b12_done, 1)
                seq.done(dve.tensor_tensor(keep.b12[:, :], b12_ps[:, :], b2[:, :], ALU.add))
                dve.wait_ge(order, seq.now)
                bias = lambda n: spread(keep.b12[:, :].rearrange("p (b d) -> p b d", b=1), [P, n, D])
                seq.done(dve.tensor_tensor(keep.x[:, 0:NB // 2, :], keep.x[:, 0:NB // 2, :], bias(NB // 2), ALU.add))
                seq.done(dve.tensor_tensor(keep.x[:, NB // 2:NB, :], keep.x[:, NB // 2:NB, :], bias(NB - NB // 2), ALU.add))
                dve.wait_ge(w12_done, 1)
                seq.done(dve.tensor_copy(keep.w12[:, :, :], w12_ps[:, :, :]))
                dve.wait_ge(norm_done, 1)
                seq.done(dve.tensor_copy(keep.bn[:, :, :], norm_ps[:, :, :]))
                dve.wait_ge(order, seq.now)


T_H, T_X, T_R = 0, 4, 8
T_H1, T_W, T_X1, T_R1, T_Z = 10, 14, 16, 20, 22
T_W_LAST, T_Z_LAST = 10, 12
TURNS = 16
C_G, C_E = 0, SB
C_G1, C_E6, C_BO, C_E7, C_P = (n * SB for n in (7, 8, 9, 10, 11))
C_E6_LAST, C_BO_LAST, C_E7_LAST, C_P_LAST = (n * SB for n in (7, 8, 9, 10))
SUMS_C = 12 * SB
WIDES = X0 * 8


def turn_blocks(j):
    return range(2 * j, min(2 * j + 2, SB))


def mixture(nc, io, keep):
    with ExitStack() as ctx:
        s = Scope(nc, ctx, "mix")
        parts = s.sb("parts", [P, SUMS - 1, 3, D])
        h = s.sb("h", [P, SB, D])
        normed = [h, s.sb("normed1", [P, SB, D])]
        at = s.sb("at", [P, KD, TOK])
        xt = s.sb("xt", [P, KD, TOK])
        xt_parts = [s.sb(f"xt_{n}", [P, KD, TOK]) for n in ("high", "low")]
        hidden = s.sb("hidden", [P, KD, TOK])
        h1_parts = [s.sb(f"h1_{n}", [P, KD, TOK]) for n in ("high", "low")]
        h2_parts = [s.sb(f"h2_{n}", [P, KD, TOK]) for n in ("high", "low")]
        weights = s.sb("weights", [P, 3, KD, D])
        weights_parts = [s.sb(f"weights_{n}", [P, 2, 3, KD, D]) for n in ("high", "low")]
        rows = s.sb("rows", [P, SB, GROW])
        residual = s.sb("residual", [P, SB, ROW])
        stats = [s.sb(f"stats{n}", [P, SB, 6]) for n in range(2)]
        aggr = [s.sb(f"aggr{n}", [P, SB, 2]) for n in range(2)]
        std = [s.sb(f"std{n}", [P, SB]) for n in range(2)]
        rstd = [s.sb(f"rstd{n}", [P, SB]) for n in range(2)]
        eps = s.sb("eps", [P, 1])
        logits = s.sb("logits", [P, SB, X0])
        gate = s.sb("gate", [P, SB, X0])
        top = s.sb("top", [P, SB])
        gate_t = s.sb("gate_t", [X0, SB, P])
        a2_top = s.sb("a2_top", [P, HEADS])
        a2_new = s.sb("a2_new", [P, HEADS])
        shift = s.sb("shift", [P, NB, HEADS])
        turn = [s.ps(f"turn{n}", [P, 512]) for n in range(2)]
        wide = [s.ps(f"wide{n}", [P, 512]) for n in range(4)]
        sums = [s.ps(f"sums{n}", [P, 512]) for n in range(2)]

        h_in = s.sem("h_in")
        parts_in = s.sem("parts_in")
        h_ready = s.sem("h_ready")
        weights_in = s.sems("weights_in", 3)
        weights_high = s.sem("weights_high")
        weights_low = s.sem("weights_low")
        turn_full = s.sem("turn_full")
        turn_free = s.sems("turn_free", 2)
        wide_full = s.sem("wide_full")
        sums_full = s.sem("sums_full")
        sums_free = s.sems("sums_free", 2)
        aggr_ready = s.sems("aggr_ready", 2)
        std_ready = s.sems("std_ready", 2)
        normed_ready = s.sems("normed_ready", 2)
        exp_in = s.sem("exp_in")
        exp_out = s.sem("exp_out")
        gate_ready = s.sem("gate_ready")
        rows_ready = s.sem("rows_ready")
        rows_out = s.sem("rows_out")
        node_ready = s.sem("node_ready")
        at_ready = s.sem("at_ready")
        xt_ready = s.sem("xt_ready")
        xt_high = s.sem("xt_high")
        xt_low = s.sem("xt_low")
        h1_ready = s.sem("h1_ready")
        h1_high = s.sem("h1_high")
        h1_low = s.sem("h1_low")
        h2_ready = s.sem("h2_ready")
        h2_high = s.sem("h2_high")
        h2_low = s.sem("h2_low")
        gate_t_ready = s.sem("gate_t_ready")
        a1_taken = s.sem("a1_taken")
        order = s.sem("order")
        pause = s.sem("pause")

        def unused(half, c):
            return half + c // 2 + 1

        def used(half, c):
            return half + c // 2 + 2

        def full(half, c):
            return 2 * half + c + 2

        T, S = TURNS // 2, SUMS_C // 2

        with nc.Block() as block:

            @block.sync
            def _(sp):
                sp.sem_inc(rows_out, 32)

                rows_of = lambda k, i, b, n: keep.partial[k][bass.ds(i * TOK + b * P, n * P), :].rearrange("(b p) d -> p b d", p=P)

                def load_h(i):
                    sp.dma_start(h[:, :, :], rows_of(0, i, 0, SB)).then_inc(h_in, 16)

                def load_parts(i, j, n, loads):
                    if loads is not None:
                        sp.wait_ge(parts_in, loads * 16 * (SUMS - 1))
                        sp.sem_inc(pause, 1)
                    for k in range(1, SUMS):
                        sp.dma_start(parts[:, k - 1, 0:2, :] if n == 2 else parts[:, k - 1, 2:3, :],
                                     rows_of(k, i, j * 2, n)).then_inc(parts_in, 16)

                def load_weights(expert, splits):
                    for n, w in enumerate((io["L0_ffn_W1"], io["L0_ffn_W2"], io["L0_ffn_Wo"])):
                        if splits is not None:
                            sp.wait_ge(weights_low, splits + n)
                            sp.sem_inc(pause, 1)
                        sp.dma_start(weights[:, n, :, :], w[bass.ds(expert, 1), :, :].rearrange("e (k p) h -> p (e k) h", p=P)
                                     ).then_inc(weights_in[n], 16)

                def store_rows(i):
                    sp.wait_ge(rows_ready, (i + 1) * 2 * SB)
                    sp.sem_inc(pause, 1)
                    sp.dma_start(keep.rows_dram[bass.ds(i * TOK, TOK), :].rearrange("(b p) d -> p b d", p=P),
                                 rows[:, :, :]).then_inc(rows_out, 16)
                    sp.dma_start(keep.residual_dram[bass.ds(i * TOK, TOK), :].rearrange("(b p) d -> p b d", p=P),
                                 residual[:, :, HEADS:ROW]).then_inc(rows_out, 16)

                def super_block(i, first=False, last=False):
                    if not last:
                        sp.wait_ge(turn_full, full(i * T, T_X + 3))
                        sp.wait_ge(h_ready, (i + 1) * (SUMS - 1) * SB)
                        sp.sem_inc(pause, 1)
                        load_h(i + 1)
                        load_parts(i + 1, X0 // 2 - 1, 1, (i + 1) * 4)
                    with sp.Fori(0, X0 // 2 - 1) as j:
                        if not last:
                            sp.wait_ge(h_ready, ((i + 1) * SB + j * 2) * (SUMS - 1))
                            load_parts(i + 1, j, 2, (i + 1) * 4 + j + 1)
                        for e in range(2):
                            load_weights(j * 2 + 2 + e, (i * X0 + j * 2 + e) * 3 + 4)
                    if not last:
                        load_weights(0, (i * X0 + X0 - 2) * 3 + 4)
                    if not first:
                        store_rows(i - 1)
                    if not last:
                        load_weights(1, (i * X0 + X0 - 1) * 3 + 4)

                load_h(0)
                load_parts(0, X0 // 2 - 1, 1, None)
                load_parts(0, 0, 2, 1)
                load_weights(0, None)
                for j in range(1, X0 // 2 - 1):
                    sp.wait_ge(h_ready, j * 2 * (SUMS - 1))
                    load_parts(0, j, 2, j + 1)
                load_weights(1, 1)
                super_block(0, first=True)
                with sp.Fori(1, NSB - 1) as i:
                    super_block(i)
                super_block(NSB - 1, last=True)
                store_rows(NSB - 1)
                sp.wait_ge(rows_out, 32 * (NSB + 1))

            @block.gpsimd
            def _(pool):
                low = lambda part, whole, high: pool.tensor_tensor(part.bitcast(F32R), whole, high, ALU.subtract)

                def split_weights(q, n, slot, nth):
                    pool.wait_ge(weights_high, nth + 1)
                    high, part = (weights_parts[m][:, slot, n, :, :] for m in range(2))
                    low(part, weights[:, n, :, :], high).then_inc(weights_low, 1)

                def split_h1(q):
                    for part in range(2):
                        for k in range(KD):
                            cols = slice(part * HALF, (part + 1) * HALF)
                            pool.wait_ge(h1_high, q * 4 + part * 2 + k + 1)
                            low(h1_parts[1][:, k, cols], hidden[:, k, cols], h1_parts[0][:, k, cols]).then_inc(h1_low, 1)

                def split_input(n):
                    for j in range(4):
                        cols = slice(2 * j * P, 2 * j * P + len(turn_blocks(j)) * P)
                        pool.wait_ge(xt_high, n * 4 + j + 1)
                        low(xt_parts[1][:, :, cols], xt[:, :, cols], xt_parts[0][:, :, cols]).then_inc(xt_low, 1)

                def add_parts(n, j, blocks, loads, done):
                    pool.wait_ge(h_in, (n + 1) * 16)
                    pool.wait_ge(parts_in, (n * 4 + loads) * 16 * (SUMS - 1))
                    pool.sem_inc(pause, 1)
                    for k in range(SUMS - 1):
                        here = bass.ds(j * 2, blocks)
                        if k:
                            pool.wait_ge(h_ready, (n * SB + done) * (SUMS - 1) + k * blocks)
                            pool.sem_inc(pause, 1)
                        part = parts[:, k, 0:2, :] if blocks == 2 else parts[:, k, 2:3, :]
                        pool.tensor_tensor(h[:, here, :], h[:, here, :], part, ALU.add).then_inc(h_ready, blocks)

                def split_next_weights(q, e):
                    for m, (n, slot) in enumerate(((1, 1 - e), (2, 1 - e), (0, e))):
                        split_weights(q, n, slot, q * 3 + 4 + m)

                def super_block(i, last=False):
                    pool.sem_inc(pause, 1)
                    with pool.Fori(0, X0 // 2 - 1) as j:
                        for e in range(2):
                            q = i * X0 + j * 2 + e
                            split_next_weights(q, e)
                            split_h1(q + 1)
                            if e == 0 and not last:
                                add_parts(i + 1, j, 2, j + 2, j * 2)
                    if not last:
                        add_parts(i + 1, X0 // 2 - 1, 1, 1, SB - 1)
                    for e in range(2):
                        q = i * X0 + X0 - 2 + e
                        if last and e:
                            continue
                        if last:
                            for m, n in enumerate((1, 2)):
                                split_weights(q, n, 1, q * 3 + 4 + m)
                        else:
                            split_next_weights(q, e)
                        if e == 0:
                            split_h1(q + 1)
                    if not last:
                        split_input(i + 1)
                        split_h1((i + 1) * X0)

                for j in range(X0 // 2 - 1):
                    add_parts(0, j, 2, j + 2, j * 2)
                add_parts(0, X0 // 2 - 1, 1, 1, SB - 1)
                for m, (n, slot) in enumerate(((0, 0), (1, 0), (2, 0), (0, 1))):
                    split_weights(0, n, slot, m)
                split_input(0)
                split_h1(0)
                with pool.Fori(0, NSB - 1) as i:
                    super_block(i)
                super_block(NSB - 1, last=True)
                pool.wait_ge(a1_taken, NSB + 1)
                pool.partition_all_reduce(keep.a2_bound[:, :], a2_top[:, :], P, bass.bass_isa.ReduceOp.max).then_inc(node_ready, 1)
                pool.wait_ge(node_ready, 1)

            @block.tensor
            def _(pe):
                pe.sem_inc(turn_full, 1)
                pe.sem_inc(sums_full, 1)

                def turn_over(half, c, tile, ready=None, first=0):
                    for j in range(4):
                        for b in turn_blocks(j):
                            if ready is not None:
                                pe.wait_ge(ready, first + b + 1)
                            if b == 2 * j:
                                pe.wait_ge(turn_free[(c + j) % 2], unused(half, c + j))
                            for k in range(KD):
                                at0 = (k * 2 + b - 2 * j) * P
                                last = pe.transpose(turn[(c + j) % 2][:, at0:at0 + P], tile[:, b, k * P:(k + 1) * P], keep.ident[:, :])
                        last.then_inc(turn_full, 1)

                def sum_tile(half, c, left, right, width=D):
                    pe.wait_ge(sums_free[c % 2], unused(half, c))
                    for k in range(KD):
                        last = pe.matmul(sums[c % 2][:, 0:width], left(k), right(k), start=(k == 0), stop=(k == KD - 1))
                    last.then_inc(sums_full, 1)

                def gin(n, t, half_t, c, half_c, turned):
                    pe.wait_ge(h_ready, (n + 1) * (SUMS - 1) * SB)
                    turn_over(half_t, t, h)
                    for b in range(SB):
                        pe.wait_ge(at_ready, turned + b // 2 + 1)
                        sum_tile(half_c, c + b, lambda k: at[:, k, b * P:(b + 1) * P], lambda k: keep.w12[:, k, :])

                def gate_logits(n, half, tx, tr):
                    turn_over(half, tx, normed[0], normed_ready[0], n * SB)
                    for part, blocks in enumerate((range(0, 4), range(4, SB))):
                        t = tr + part
                        pe.wait_ge(turn_free[t % 2], unused(half, t))
                        for b in blocks:
                            pe.wait_ge(xt_ready, n * 4 + b // 2 + 1)
                            for k in range(KD):
                                last = pe.matmul(turn[t % 2][:, b * X0:(b + 1) * X0], xt[:, k, b * P:(b + 1) * P], keep.wr[:, k, :],
                                                 start=(k == 0), stop=(k == KD - 1))
                        last.then_inc(turn_full, 1)

                def product(out, left, right):
                    terms = [(l, r, k) for k in range(KD) for l, r in ((0, 0), (0, 1), (1, 0))]
                    for n, (l, r, k) in enumerate(terms):
                        last = pe.matmul(out, left(l, k).bitcast(F32R), right(r, k).bitcast(F32R),
                                         start=(n == 0), stop=(n == len(terms) - 1))
                    return last

                def layer(q, n, slot):
                    source = (xt_parts, h1_parts)[n]
                    pe.wait_ge(weights_low, q * 3 + (1 if n == 0 else 2))
                    for part in range(2):
                        if n == 1:
                            pe.wait_ge(h1_low, q * 4 + 2 * part + 2)
                        for m in range(KD):
                            t = part * 2 + m
                            if n == 1:
                                pe.wait_ge(h1_ready, q * 4 + t + 1)
                            else:
                                pe.wait_ge(h2_ready, q * 4 + t + 1)
                            product(wide[t][:, 0:HALF], lambda l, k: weights_parts[l][:, slot, n, k, m * P:(m + 1) * P],
                                    lambda r, k: source[r][:, k, part * HALF:(part + 1) * HALF]).then_inc(wide_full, 1)

                def sums_of_expert(q, slot, half, c):
                    pe.wait_ge(weights_low, q * 3 + 3)
                    for b in range(SB):
                        pe.wait_ge(h2_low, q * 4 + (2 if (b + 1) * P <= HALF else 4) + 4)
                        pe.wait_ge(sums_free[(c + b) % 2], unused(half, c + b))
                        product(sums[(c + b) % 2][:, 0:D], lambda l, k: h2_parts[l][:, k, b * P:(b + 1) * P],
                                lambda r, k: weights_parts[r][:, slot, 2, k, :]).then_inc(sums_full, 1)

                def last_biases(i, half_t, t0, half_c, c):
                    for part, blocks in enumerate((range(0, 4), range(4, SB))):
                        t = t0 + part
                        pe.wait_ge(gate_ready, i + 1)
                        pe.wait_ge(turn_free[t % 2], unused(half_t, t))
                        for n, b in enumerate(blocks):
                            last = pe.transpose(turn[t % 2][0:X0, n * P:(n + 1) * P], gate[:, b, :], keep.ident[:, :])
                        last.then_inc(turn_full, 1)
                    for b in range(SB):
                        pe.wait_ge(gate_t_ready, i * 2 + b // 4 + 1)
                        pe.wait_ge(sums_free[(c + b) % 2], unused(half_c, c + b))
                        pe.matmul(sums[(c + b) % 2][:, 0:D], gate_t[:, b, :], keep.bo[:, :], start=True, stop=True).then_inc(sums_full, 1)

                def projections(i, half_t, t, half_c, c, turned):
                    turn_over(half_t, t, normed[1], normed_ready[1], i * SB)
                    for b in range(SB):
                        pe.wait_ge(at_ready, turned + b // 2 + 1)
                        for n, (c0, c1) in enumerate(((0, GROW), (GROW, PROJ))):
                            sum_tile(half_c, c + 2 * b + n, lambda k: at[:, k, b * P:(b + 1) * P],
                                     lambda k: keep.proj[:, k, c0:c1], width=c1 - c0)

                def super_block(i, last=False):
                    with pe.Fori(0, X0 // 2 - 1) as j:
                        for e in range(2):
                            q = i * X0 + j * 2 + e
                            layer(q, 1, e)
                            layer(q + 1, 0, 1 - e)
                            sums_of_expert(q, e, i * S + j * SB, C_E + e * SB)
                    if not last:
                        gin(i + 1, T_H1, i * T, C_G1, i * S, i * 8 + 4)
                    q = i * X0 + X0 - 2
                    layer(q, 1, 0)
                    layer(q + 1, 0, 1)
                    sums_of_expert(q, 0, i * S, C_E6_LAST if last else C_E6)
                    layer(q + 1, 1, 1)
                    last_biases(i, i * T, T_W_LAST if last else T_W, i * S, C_BO_LAST if last else C_BO)
                    sums_of_expert(q + 1, 1, i * S, C_E7_LAST if last else C_E7)
                    if not last:
                        gate_logits(i + 1, i * T, T_X1, T_R1)
                        first_layer(i + 1)
                    projections(i, i * T, T_Z_LAST if last else T_Z, i * S, C_P_LAST if last else C_P, i * 8 + (4 if last else 8))

                def first_layer(i):
                    pe.wait_ge(xt_low, i * 4 + 4)
                    layer(i * X0, 0, 0)

                gin(0, T_H, 0, C_G, 0, 0)
                gate_logits(0, 0, T_X, T_R)
                first_layer(0)
                with pe.Fori(0, NSB - 1) as i:
                    super_block(i)
                super_block(NSB - 1, last=True)

            @block.scalar
            def _(act):
                act.sem_inc(a1_taken, 1)
                act.sem_inc(h2_ready, 4)

                def copy_turns(half, c, tile, ready, before):
                    for j in range(4):
                        t = c + j
                        width = len(turn_blocks(j)) * P
                        act.wait_ge(turn_full, full(half, t))
                        act.copy(tile[:, :, 2 * j * P:2 * j * P + width],
                                 turn[t % 2][:, :].rearrange("p (k n) -> p k n", k=KD)[:, :, 0:width]).then_inc(ready, 1)
                        act.wait_ge(ready, before + j + 1)
                        act.sem_inc(turn_free[t % 2], 1)

                def roots(nth, n):
                    act.wait_ge(aggr_ready[nth], n + 1)
                    act.activation(std[nth][:, :], aggr[nth][:, :, 1], ACT.Sqrt, bias=eps[:, 0:1]).then_inc(std_ready[nth], 1)

                def exponentials(n):
                    act.wait_ge(exp_in, n + 1)
                    act.activation(gate[:, :, :], logits[:, :, :], ACT.Exp).then_inc(exp_out, 1)

                def relu(i, q, n, cols):
                    ready = (h1_ready, h2_ready)[n]
                    for part in range(2):
                        for m in range(KD):
                            t = part * 2 + m
                            act.wait_ge(wide_full, q * 8 + n * 4 + t + 1)
                            if n == 0:
                                act.wait_ge(h2_low, q * 4 + t + 1)
                            act.sem_inc(pause, 1)
                            act.activation(hidden[:, m, part * HALF:(part + 1) * HALF], wide[t][:, 0:HALF], ACT.Relu,
                                           bias=keep.bn[:, 2 * n + 1, bass.ds(cols + m, 1)],
                                           scale=keep.bn[:, 2 * n, bass.ds(cols + m, 1)]).then_inc(ready, 1)

                def copy_gate(i, half, c):
                    for part, n in enumerate((4, SB - 4)):
                        t = c + part
                        act.wait_ge(turn_full, full(half, t))
                        act.copy(gate_t[:, 4 * part:4 * part + n, :], turn[t % 2][0:X0, 0:n * P].rearrange("p (b n) -> p b n", n=P))\
                           .then_inc(gate_t_ready, 1)
                        act.wait_ge(gate_t_ready, i * 2 + part + 1)
                        act.sem_inc(turn_free[t % 2], 1)

                def copy_rows(i, half, c0):
                    act.wait_ge(rows_out, (i + 1) * 32)
                    act.wait_ge(a1_taken, i + 1)
                    for b in range(SB):
                        for n in range(2):
                            c = c0 + 2 * b + n
                            act.wait_ge(sums_full, full(half, c))
                            if n == 0:
                                act.copy(rows[:, b, :], sums[c % 2][:, 0:GROW]).then_inc(rows_ready, 1)
                            else:
                                act.copy(residual[:, b, :], sums[c % 2][:, 0:ROW]).then_inc(rows_ready, 1)
                            act.wait_ge(rows_ready, i * 2 * SB + 2 * b + n + 1)
                            act.sem_inc(sums_free[c % 2], 1)

                def super_block(i, last=False):
                    with act.Fori(0, X0 // 2 - 1) as j:
                        for e in range(2):
                            q = i * X0 + j * 2 + e
                            relu(i, q, 1, j * 4 + e * 2)
                            relu(i, q + 1, 0, j * 4 + e * 2 + 2)
                    if not last:
                        copy_turns(i * T, T_H1, at, at_ready, i * 8 + 4)
                    q = i * X0 + X0 - 2
                    relu(i, q, 1, 2 * X0 - 4)
                    if not last:
                        roots(0, i + 1)
                    relu(i, q + 1, 0, 2 * X0 - 2)
                    relu(i, q + 1, 1, 2 * X0 - 2)
                    copy_gate(i, i * T, T_W_LAST if last else T_W)
                    if not last:
                        copy_turns(i * T, T_X1, xt, xt_ready, (i + 1) * 4)
                    roots(1, i)
                    if not last:
                        relu(i + 1, q + 2, 0, 0)
                    copy_turns(i * T, T_Z_LAST if last else T_Z, at, at_ready, i * 8 + (4 if last else 8))
                    if not last:
                        exponentials(i + 1)
                    copy_rows(i, i * S, C_P_LAST if last else C_P)

                copy_turns(0, T_H, at, at_ready, 0)
                roots(0, 0)
                copy_turns(0, T_X, xt, xt_ready, 0)
                relu(0, 0, 0, 0)
                exponentials(0)
                with act.Fori(0, NSB - 1) as i:
                    super_block(i)
                super_block(NSB - 1, last=True)

            @block.vector
            def _(dve):
                seq = Tally(order)

                def then(instruction):
                    seq.done(instruction)
                    dve.wait_ge(order, seq.now)

                dve.sem_inc(h2_low, 4)
                for n in range(2):
                    dve.sem_inc(turn_free[n], 1)
                    dve.sem_inc(sums_free[n], 1)
                then(dve.memset(eps[:, :], 1e-5))
                then(dve.memset(a2_top[:, :], -3e38))

                def node(i, b):
                    return bass.ds(i * SB + b, 1)

                def add_sum(i, b, half, c):
                    x = keep.x[:, node(i, b), :]
                    dve.wait_ge(sums_full, full(half, c))
                    dve.tensor_tensor(x, sums[c % 2][:, 0:D].rearrange("p (b d) -> p b d", b=1), x, ALU.add)\
                       .then_inc(sums_free[c % 2], 1)

                def norm_stats(nth, i, half, c):
                    for b in range(SB):
                        dve.wait_ge(sums_free[(c + b) % 2], used(half, c + b))
                        dve.sem_inc(pause, 1)
                        seq.done(dve.bn_stats(stats[nth][:, b, :], keep.x[:, node(i, b), :]))
                    dve.wait_ge(order, seq.now)
                    dve.sem_inc(pause, 1)
                    for b in range(SB):
                        last = dve.bn_aggr(aggr[nth][:, b, :], stats[nth][:, b, :])
                    last.then_inc(aggr_ready[nth], 1)

                def normalize(nth, i):
                    dve.wait_ge(std_ready[nth], i + 1)
                    then(dve.reciprocal(rstd[nth][:, :], std[nth][:, :]))
                    for b in range(SB):
                        dve.tensor_scalar(normed[nth][:, b, :], keep.x[:, node(i, b), :], aggr[nth][:, b, 0:1], rstd[nth][:, b:b + 1],
                                          ALU.subtract, ALU.mult).then_inc(normed_ready[nth], 1)

                def high(part, whole):
                    return dve.tensor_copy(part.bitcast(F32R), whole)

                def split_weights(q, n, slot):
                    dve.wait_ge(weights_in[n], q * 16 + 16)
                    dve.sem_inc(pause, 1)
                    high(weights_parts[0][:, slot, n, :, :], weights[:, n, :, :]).then_inc(weights_high, 1)

                def split_next_weights(q, e):
                    split_weights(q + 1, 1, 1 - e)
                    split_weights(q + 1, 2, 1 - e)
                    split_weights(q + 2, 0, e)

                def split_h1(q, tiles=range(4)):
                    for part in range(2):
                        for k in range(KD):
                            if part * 2 + k not in tiles:
                                continue
                            cols = slice(part * HALF, (part + 1) * HALF)
                            dve.wait_ge(h1_ready, q * 4 + part * 2 + k + 1)
                            dve.sem_inc(pause, 1)
                            high(h1_parts[0][:, k, cols], hidden[:, k, cols]).then_inc(h1_high, 1)

                def split_h2(q):
                    for part in range(2):
                        cols = slice(part * HALF, (part + 1) * HALF)
                        for k in range(KD):
                            dve.wait_ge(h2_ready, q * 4 + part * 2 + k + 1 + 4)
                            dve.sem_inc(pause, 1)
                            high(h2_parts[0][:, k, cols], hidden[:, k, cols]).then_inc(h2_high, 1)
                        for k in range(KD):
                            dve.wait_ge(h2_high, q * 4 + part * 2 + k + 1)
                            dve.tensor_tensor(h2_parts[1][:, k, cols].bitcast(F32R), hidden[:, k, cols], h2_parts[0][:, k, cols], ALU.subtract).then_inc(h2_low, 1)

                def split_input(n):
                    for j in range(4):
                        cols = slice(2 * j * P, 2 * j * P + len(turn_blocks(j)) * P)
                        dve.wait_ge(xt_ready, n * 4 + j + 1)
                        dve.sem_inc(pause, 1)
                        high(xt_parts[0][:, :, cols], xt[:, :, cols]).then_inc(xt_high, 1)

                def gin(i, half, c):
                    for b in range(SB):
                        add_sum(i, b, half, c + b)
                    norm_stats(0, i, half, c)

                every = [P, SB, X0]
                wide_col = lambda ap: spread(ap.rearrange("p (b e) -> p b e", e=1), every)

                def gate_shifted(i, half, t0):
                    for part, (b0, b1) in enumerate(((0, 4), (4, SB))):
                        t = t0 + part
                        dve.wait_ge(turn_full, full(half, t))
                        dve.tensor_tensor(logits[:, b0:b1, :], turn[t % 2][:, b0 * X0:b1 * X0].rearrange("p (b e) -> p b e", e=X0),
                                          spread(keep.br[:, :].rearrange("p (b e) -> p b e", b=1), [P, b1 - b0, X0]),
                                          ALU.add).then_inc(turn_free[t % 2], 1)
                    for part in range(2):
                        dve.wait_ge(turn_free[(t0 + part) % 2], used(half, t0 + part))
                    then(dve.tensor_reduce(top[:, :], logits[:, :, :], AX.X, ALU.max))
                    dve.tensor_tensor(logits[:, :, :], logits[:, :, :], wide_col(top[:, :]), ALU.subtract).then_inc(exp_in, 1)

                def gate_softmax(i):
                    dve.wait_ge(exp_out, i + 1)
                    then(dve.tensor_reduce(top[:, :], gate[:, :, :], AX.X, ALU.add))
                    then(dve.reciprocal(top[:, :], top[:, :]))
                    dve.tensor_tensor(gate[:, :, :], gate[:, :, :], wide_col(top[:, :]), ALU.mult).then_inc(gate_ready, 1)
                    dve.wait_ge(gate_ready, i + 1)
                    dve.sem_inc(pause, 1)

                def add_expert(i, j, e, half, c0, blocks=range(SB)):
                    for b in blocks:
                        c = c0 + b
                        x = keep.x[:, node(i, b), :]
                        dve.wait_ge(sums_full, full(half, c))
                        dve.scalar_tensor_tensor(x, sums[c % 2][:, 0:D].rearrange("p (b d) -> p b d", b=1),
                                                 gate[:, b, bass.ds(j * 2 + e, 1)], x, ALU.mult, ALU.add).then_inc(sums_free[c % 2], 1)

                def take_a(i):
                    dve.wait_ge(rows_ready, (i + 1) * 2 * SB)
                    then(dve.tensor_reduce(a2_new[:, :], rows[:, :, D:ROW].rearrange("p b h -> p h b"), AX.X, ALU.max))
                    then(dve.tensor_tensor(a2_top[:, :], a2_top[:, :], a2_new[:, :], ALU.max))
                    dve.sem_inc(pause, 1)
                    dve.tensor_copy(keep.node[:, bass.ds(i * SB, SB), 0:HEADS], residual[:, :, 0:HEADS]).then_inc(a1_taken, 1)

                def super_block(i, last=False):
                    dve.sem_inc(pause, 1)
                    with dve.Fori(0, X0 // 2 - 1) as j:
                        for e in range(2):
                            q = i * X0 + j * 2 + e
                            split_h2(q)
                            split_next_weights(q, e)
                            split_h1(q + 1, range(3))
                            add_expert(i, j, e, i * S + j * SB, C_E + e * SB, range(1))
                            split_h1(q + 1, range(3, 4))
                            add_expert(i, j, e, i * S + j * SB, C_E + e * SB, range(1, SB))
                    if not last:
                        gin(i + 1, i * S, C_G1)
                    j, q = X0 // 2 - 1, i * X0 + X0 - 2
                    split_h2(q)
                    if last:
                        for n in (1, 2):
                            split_weights(q + 1, n, 1)
                    else:
                        split_next_weights(q, 0)
                    split_h1(q + 1)
                    if not last:
                        normalize(0, i + 1)
                    add_expert(i, j, 0, i * S, C_E6_LAST if last else C_E6)
                    split_h2(q + 1)
                    if not last:
                        split_next_weights(q + 1, 1)
                    c = C_BO_LAST if last else C_BO
                    for b in range(SB):
                        add_sum(i, b, i * S, c + b)
                    c = C_E7_LAST if last else C_E7
                    add_expert(i, j, 1, i * S, c)
                    norm_stats(1, i, i * S, c)
                    if not last:
                        split_input(i + 1)
                    normalize(1, i)
                    if not last:
                        gate_shifted(i + 1, i * T, T_R1)
                        split_h1((i + 1) * X0)
                        gate_softmax(i + 1)
                    take_a(i)

                gin(0, 0, C_G)
                for n in range(3):
                    split_weights(0, n, 0)
                split_weights(1, 0, 1)
                normalize(0, 0)
                split_input(0)
                gate_shifted(0, 0, T_R)
                split_h1(0)
                gate_softmax(0)
                with dve.Fori(0, NSB - 1) as i:
                    seq.enter(i, DVE_MIX)
                    super_block(i)
                    seq.leave(NSB - 1)
                super_block(NSB - 1, last=True)
                dve.wait_ge(a1_taken, NSB + 1)
                dve.wait_ge(node_ready, 1)
                a1, low = keep.node[:, :, 0:HEADS], keep.node[:, :, HEADS:2 * HEADS]
                then(dve.tensor_tensor(shift[:, :, :], a1, spread(keep.a2_bound[:, :].rearrange("p (b h) -> p b h", b=1), [P, NB, HEADS]), ALU.add))
                then(dve.scalar_tensor_tensor(shift[:, :, :], shift[:, :, :], SLOPE, shift[:, :, :], ALU.mult, ALU.max))
                then(dve.scalar_tensor_tensor(low, a1, SLOPE, shift[:, :, :], ALU.mult, ALU.subtract))
                then(dve.tensor_tensor(a1, a1, shift[:, :, :], ALU.subtract))


def pipeline(eng, stages, registers_of=None):
    def run(i, us, first=False, last=False):
        for u in us:
            for stage, lag in stages:
                if (u - lag >= 0 or not first) and (u - lag < 0 or not last):
                    stage(i, u - lag)

    if registers_of:
        registers_of(0)
    run(0, range(ASLOTS), first=True)
    with eng.Fori(1, AROUNDS) as i:
        if registers_of:
            registers_of(i)
        run(i, range(ASLOTS))
    if registers_of:
        registers_of(AROUNDS)
    run(AROUNDS, range(max(lag for _, lag in stages)), last=True)


def attend(nc, io, keep):
    with ExitStack() as ctx:
        s = Scope(nc, ctx, "att")
        cols = s.sb("cols", [P, ASLOTS, G, 2], I32)
        rows = s.sb("rows", [P, MASKS, STEP], I32)
        dst_in = s.sb("dst_in", [P, ASLOTS, G])
        is_dst = s.sb("is_dst", [P, MASKS, G, P])
        to_edge = s.sb("to_edge", [P, MASKS, G, P])
        gathered = s.sb("gathered", [P, ASLOTS, G, GROW])
        terms = s.sb("terms", [P, ASLOTS, G, 2, HEADS])
        scores = s.sb("scores", [P, ASLOTS, G, HEADS])
        warmed = s.sb("warmed", [P, 1])
        node_ps = [s.ps(f"node_ps{u}", [P, 512]) for u in range(TILES)]
        sums_ps = [s.ps(f"sums_ps{u}", [P, 512]) for u in range(TILES)]
        acc = keep.xn

        cols_in = s.sems("cols_in", ASLOTS)
        rows_in = s.sems("rows_in", MASKS)
        row_in = s.sems("row_in", ASLOTS)
        masks_ready = s.sem("masks_ready")
        node_ready = s.sem("node_ready")
        terms_ready = s.sem("terms_ready")
        scores_ready = s.sem("scores_ready")
        p_ready = s.sem("p_ready")
        lot0_ready = s.sem("lot0_ready")
        lot1_ready = s.sem("lot1_ready")
        summed = s.sem("summed")
        added = s.sem("added")
        zeroed = s.sem("zeroed")
        order = s.sem("order")
        turn = s.sem("turn")

        def upto(i, u):
            return i * ASLOTS + u + 1

        def slot_use(i, u, slots=ASLOTS):
            return i * (ASLOTS // slots) + u // slots + 1

        class Blocks:

            def __init__(self, eng, name, back):
                self.eng, self.back = eng, back
                self.regs = registers(eng, name, ASLOTS + back)

            def load(self, i):
                back, n = self.back, len(self.regs)
                if isinstance(i, int):
                    first, n = (0, ASLOTS) if i == 0 else (i * ASLOTS - back, back)
                    entries, regs = keep.step_block[:, first:first + n], self.regs[back:] if i == 0 else self.regs[:back]
                else:
                    entries, regs = keep.step_block[:, bass.ds(i * ASLOTS - back, n)], self.regs
                if not regs:
                    return
                self.eng.load(regs, entries)
                values = [self.eng.snap(r, min_val=0, max_val=NB - 1) for r in regs]
                self.of = {u: v for u, v in zip(range(0 if isinstance(i, int) and i == 0 else -back, ASLOTS), values)}

            def __getitem__(self, u):
                return bass.ds(self.of[u], 1)

        with nc.Block() as block:

            @block.sync
            def _(sp):
                regs = registers(sp, "att_first", ASLOTS)
                with sp.Fori(0, AROUNDS) as i:
                    firsts = step_values(sp, regs, keep.step_edge, i, E)
                    for u, first in enumerate(firsts):
                        sp.wait_ge(terms_ready, upto(i, u + ASLOTS - MASKS))
                        sp.sem_inc(turn, 1)
                        sp.dma_start(cols[:, u, :, :].rearrange("p g t -> p (g t)"),
                                     keep.pair_list[bass.ds(first, STEP), :].rearrange("(p g) t -> p (g t)", g=G)
                                     ).then_inc(cols_in[u], 16)
                        sp.dma_start(rows[:, u % MASKS, :], keep.dst_list[bass.ds(first, STEP)].partition_broadcast(P)
                                     ).then_inc(rows_in[u % MASKS], 16)

            @block.gpsimd
            def _(pool):
                with pool.Fori(0, AROUNDS) as i:
                    for u in range(ASLOTS):
                        pool.wait_ge(cols_in[u], i * 16 + 16)
                        pool.wait_ge(summed, upto(i, u))
                        pool.sem_inc(turn, 1)
                        for g in range(G):
                            pool.indirect_dma_start(
                                out=gathered[:, u, g, :], out_offset=None, in_=keep.rows_dram[:, :],
                                in_offset=bass.IndirectOffsetOnAxis(ap=cols[:, u, g, 0:1], axis=0)).then_inc(row_in[u], 16)
                for u in range(ASLOTS):
                    pool.wait_ge(row_in[u], 32 * AROUNDS)

            @block.vector
            def _(dve):
                every = [P, G, P]
                dve.sem_inc(added, TILES)
                dve.memset(acc[:, :, :], 0.0).then_inc(zeroed, 1)
                dve.wait_ge(zeroed, 1)
                blocks = Blocks(dve, "att_dve", 5)

                def make_masks(i, u):
                    m = u % MASKS
                    dve.wait_ge(cols_in[u], slot_use(i, u) * 16)
                    dve.tensor_scalar(dst_in[:, u, :], cols[:, u, :, 1], keep.block_base[:, blocks[u]],
                                      None, ALU.subtract).then_inc(order, 1)
                    dve.wait_ge(rows_in[m], slot_use(i, u, MASKS) * 16)
                    dve.wait_ge(summed, upto(i, u + ASLOTS - MASKS))
                    dve.tensor_scalar(to_edge[:, m, :, :], rows[:, m, :].rearrange("p (q g) -> p g q", g=G),
                                      keep.node_id[:, blocks[u]], None, ALU.is_equal).then_inc(masks_ready, 1)
                    dve.wait_ge(order, upto(i, u))
                    dve.tensor_tensor(is_dst[:, m, :, :], spread(keep.lane[:, :].rearrange("p (g n) -> p g n", g=1), every),
                                      spread(dst_in[:, u, :].rearrange("p (g n) -> p g n", n=1), every),
                                      ALU.is_equal).then_inc(masks_ready, 1)

                def make_terms(i, u):
                    at = u % ASLOTS
                    dve.wait_ge(node_ready, upto(i, u))
                    dve.wait_ge(row_in[at], slot_use(i, u) * 32)
                    dve.tensor_tensor(terms[:, at, :, :, :].rearrange("p g t h -> p g (t h)"),
                                      node_ps[u % TILES][:, 0:G * 2 * HEADS].rearrange("p (g c) -> p g c", g=G),
                                      gathered[:, at, :, D:GROW], ALU.add).then_inc(terms_ready, 1)

                def make_scores(i, u):
                    at = u % ASLOTS
                    dve.wait_ge(terms_ready, upto(i, u) + ASLOTS)
                    dve.scalar_tensor_tensor(scores[:, at, :, :], terms[:, at, :, 0, :], 0.0, terms[:, at, :, 1, :],
                                             ALU.min, ALU.max).then_inc(scores_ready, 1)

                def weigh(i, u):
                    at = u % ASLOTS
                    dve.wait_ge(p_ready, upto(i, u))
                    row = gathered[:, at, 0, 0:D].rearrange("p (h o) -> p h o", h=HEADS)
                    dve.tensor_tensor(row, row, spread(gathered[:, at, 0, D:ROW].rearrange("p (h o) -> p h o", o=1), [P, HEADS, DO]),
                                      ALU.mult).then_inc(lot0_ready, 1)

                def add(i, u):
                    dve.wait_ge(summed, upto(i, u) + ASLOTS)
                    dve.wait_ge(added, upto(i, u) - 1 + TILES)
                    here = acc[:, blocks[u], :]
                    dve.tensor_tensor(here, sums_ps[u % TILES][:, 0:ROW].rearrange("p (b d) -> p b d", b=1), here,
                                      ALU.add).then_inc(added, 1)

                pipeline(dve, ((make_masks, 0), (make_terms, 2), (weigh, 3), (make_scores, 2), (add, 5)), blocks.load)
                dve.wait_ge(added, AROUNDS * ASLOTS + TILES)

            @block.scalar
            def _(act):
                act.activation(warmed[:, :], keep.ones[:, 0:1], ACT.Exp).then_inc(turn, 1)

                def exponentials(i, u):
                    at = u % ASLOTS
                    act.wait_ge(scores_ready, upto(i, u))
                    act.activation(gathered[:, at, :, D:ROW], scores[:, at, :, :], ACT.Exp).then_inc(p_ready, 1)

                def weigh(i, u):
                    at = u % ASLOTS
                    act.wait_ge(p_ready, upto(i, u))
                    for h in range(HEADS):
                        row = gathered[:, at, 1, h * DO:(h + 1) * DO]
                        last = act.activation(row, row, ACT.Copy, scale=gathered[:, at, 1, D + h:D + h + 1])
                    last.then_inc(lot1_ready, 1)

                pipeline(act, ((exponentials, 0), (weigh, 1)))

            @block.tensor
            def _(pe):
                pe.sem_inc(summed, ASLOTS)
                pe.sem_inc(terms_ready, ASLOTS)
                blocks = Blocks(pe, "att_pe", 0)

                def expand(i, u):
                    pe.wait_ge(masks_ready, 2 * upto(i, u) - 1)
                    pe.wait_ge(terms_ready, upto(i, u) - TILES + ASLOTS)
                    for g in range(G):
                        last = pe.matmul(node_ps[u % TILES][:, g * 2 * HEADS:(g + 1) * 2 * HEADS], to_edge[:, u % MASKS, g, :],
                                         keep.node[:, blocks[u], :].rearrange("p b c -> p (b c)"), start=True, stop=True)
                    last.then_inc(node_ready, 1)

                def total(i, u):
                    pe.wait_ge(masks_ready, 2 * upto(i, u))
                    pe.wait_ge(lot0_ready, upto(i, u))
                    pe.wait_ge(lot1_ready, upto(i, u))
                    pe.wait_ge(added, upto(i, u))
                    for g in range(G):
                        last = pe.matmul(sums_ps[u % TILES][:, 0:ROW], is_dst[:, u % MASKS, g, :], gathered[:, u % ASLOTS, g, 0:ROW],
                                         start=(g == 0), stop=(g == G - 1))
                    last.then_inc(summed, 1)

                pipeline(pe, ((expand, 0), (total, 3)), blocks.load)


def finish_attention(nc, io, keep):
    with ExitStack() as ctx:
        s = Scope(nc, ctx, "fin")
        residual = s.sb("residual", [P, 2, SB, D])
        den = s.sb("den", [P, NB, HEADS])
        stats = s.sb("stats", [P, NB, 6])
        aggr = s.sb("aggr", [P, NB, 2])
        std = s.sb("std", [P, NB])
        rstd = s.sb("rstd", [P, NB])
        eps = s.sb("eps", [P, 1])
        acc, xn = keep.xn, keep.xn
        total = s.ps("total", [P, D])

        residual_in = s.sems("residual_in", 2)
        divided = s.sem("divided")
        outs_ready = s.sem("outs_ready")
        aggr_ready = s.sem("aggr_ready")
        std_ready = s.sem("std_ready")
        normed = s.sem("normed")
        summed = s.sem("summed")
        order = s.sem("order")
        pause = s.sem("pause")

        with nc.Block() as block:

            @block.sync
            def _(sp):
                for i in range(NSB):
                    if i >= 2:
                        sp.wait_ge(outs_ready, i - 1)
                    sp.dma_start(residual[:, i % 2, :, :], keep.residual_dram[i * TOK:(i + 1) * TOK, :].rearrange("(b p) d -> p b d", p=P)
                                 ).then_inc(residual_in[i % 2], 16)

            @block.gpsimd
            def _(pool):
                for i in range(NSB):
                    pool.wait_ge(divided, i + 1)
                    pool.wait_ge(residual_in[i % 2], i // 2 * 16 + 16)
                    here = slice(i * SB, (i + 1) * SB)
                    pool.tensor_tensor(acc[:, here, 0:D], acc[:, here, 0:D], residual[:, i % 2, :, :], ALU.add).then_inc(outs_ready, 1)

            @block.vector
            def _(dve):
                seq = Tally(order)

                def then(instruction):
                    seq.done(instruction)
                    dve.wait_ge(order, seq.now)

                seq.done(dve.memset(eps[:, :], 1e-5))
                then(dve.tensor_scalar(den[:, :, :], acc[:, :, D:ROW], TINY, None, ALU.max))
                then(dve.reciprocal(den[:, :, :], den[:, :, :]))
                heads = lambda ap: ap.rearrange("p b (h o) -> p (b h) o", h=HEADS)

                def divide(i):
                    here = slice(i * SB, (i + 1) * SB)
                    for b in range(i * SB, (i + 1) * SB):
                        row = acc[:, b, 0:D].rearrange("p (h o) -> p h o", h=HEADS)
                        last = dve.tensor_tensor(row, row, spread(den[:, b, :].rearrange("p (h o) -> p h o", o=1), [P, HEADS, DO]), ALU.mult)
                    last.then_inc(divided, 1)

                divide(0)
                for i in range(NSB):
                    if i + 1 < NSB:
                        divide(i + 1)
                    dve.wait_ge(outs_ready, i + 1)
                    here = slice(i * SB, (i + 1) * SB)
                    then(dve.scalar_tensor_tensor(keep.x[:, here, :], acc[:, here, 0:D], 0.0, keep.x[:, here, :], ALU.max, ALU.add))
                    for b in range(i * SB, (i + 1) * SB):
                        last = dve.bn_stats(stats[:, b, :], keep.x[:, b, :])
                    then(last)
                    for b in range(i * SB, (i + 1) * SB):
                        last = dve.bn_aggr(aggr[:, b, :], stats[:, b, :])
                    last.then_inc(aggr_ready, 1)
                    dve.wait_ge(std_ready, i + 1)
                    then(dve.reciprocal(rstd[:, here], std[:, here]))
                    for b in range(i * SB, (i + 1) * SB):
                        last = dve.tensor_scalar(xn[:, b, 0:D], keep.x[:, b, :], aggr[:, b, 0:1], rstd[:, b:b + 1],
                                                 ALU.subtract, ALU.mult)
                    last.then_inc(normed, 1)
                dve.wait_ge(summed, 1)
                then(dve.tensor_copy(keep.node_sum[:, :], total[:, :]))

            @block.scalar
            def _(act):
                for i in range(NSB):
                    act.wait_ge(aggr_ready, i + 1)
                    here = slice(i * SB, (i + 1) * SB)
                    act.activation(std[:, here], aggr[:, here, 1], ACT.Sqrt, bias=eps[:, 0:1]).then_inc(std_ready, 1)

            @block.tensor
            def _(pe):
                for b in range(NB):
                    rows = P if b < NB - 1 else LAST
                    if b % SB == 0:
                        pe.wait_ge(normed, b // SB + 1)
                    last = pe.matmul(total[:, :], keep.ones[0:rows, :], xn[0:rows, b, 0:D], start=(b == 0), stop=(b == NB - 1))
                last.then_inc(summed, 1)


def route(nc, io, keep):
    with ExitStack() as ctx:
        s = Scope(nc, ctx, "route")
        wr = s.sb("wr", [P, KD, X1])
        br = s.sb("br", [P, X1])
        turned = s.sb("turned", [P, KD, P])
        p = s.sb("p", [P, X1])
        load = s.sb("load", [P, X1])
        scale = s.sb("scale", [P, X1])
        over = s.sb("over", [P, X1])
        left = s.sb("left", [P, X1])
        first = s.sb("first", [P, X1])
        peak = s.sb("peak", [P, TOP])
        low = s.sb("low", [P, 1])
        one = s.sb("one", [P, 1])
        gate = s.sb("gate", [P, TOP])
        chosen = s.sb("chosen", [P, TOP], I32)
        b2 = s.sb("b2", [P, TOP, D])
        turned_ps = s.ps("turned_ps", [P, KD, P])
        logits_ps = s.ps("logits_ps", [P, X1])

        params_in = s.sem("params_in")
        turned_over = s.sem("turned_over")
        turned_ready = s.sem("turned_ready")
        logits_ready = s.sem("logits_ready")
        exp_in = s.sem("exp_in")
        exp_out = s.sem("exp_out")
        chosen_ready = s.sem("chosen_ready")
        w1_in = s.sem("w1_in")
        w2_in = s.sem("w2_in")
        order = s.sem("order")

        with nc.Block() as block:

            @block.sync
            def _(sp):
                sp.dma_start(wr[:, :, :], io["L1_ffn_Wr"].rearrange("(k p) e -> p k e", p=P)).then_inc(params_in, 16)
                sp.dma_start(br[:, :], io["L1_ffn_br"].partition_broadcast(P)).then_inc(params_in, 16)
                sp.dma_start(keep.gamma[:, :], io["L1_ffn_gamma"].partition_broadcast(P)).then_inc(params_in, 16)
                sp.dma_start(keep.beta[:, :], io["L1_ffn_beta"].partition_broadcast(P)).then_inc(params_in, 16)
                sp.wait_ge(chosen_ready, TOP)
                regs = registers(sp, "route_expert", TOP)
                sp.load(regs, chosen[0:1, 0:TOP])
                for j, r in enumerate(regs):
                    expert = bass.ds(sp.snap(r, min_val=0, max_val=X1 - 1), 1)
                    sp.dma_start(keep.ew1[:, j, :, :], io["L1_ffn_W1"][expert, :, :].rearrange("e (k p) f -> p (e k) f", p=P)).then_inc(w1_in, 16)
                    with nc.allow_non_contiguous_dma(reason="512 words"):
                        sp.dma_start(keep.eb1[:, j, :], io["L1_ffn_b1"][expert, :].rearrange("e (c p) -> p (e c)", p=P)).then_inc(w1_in, 16)
                    sp.dma_start(keep.ew2[:, j, :, :], io["L1_ffn_W2"][expert, :, :].rearrange("e (c p) d -> p (e c) d", p=P)).then_inc(w2_in, 16)
                    sp.dma_start(b2[:, j, :], io["L1_ffn_b2"][expert, :].rearrange("e d -> (e d)").partition_broadcast(P)).then_inc(w2_in, 16)
                sp.wait_ge(w1_in, 32 * TOP)
                sp.wait_ge(params_in, 64)

            @block.tensor
            def _(pe):
                for k in range(KD):
                    last = pe.transpose(turned_ps[:, k, :], keep.node_sum[:, k * P:(k + 1) * P], keep.ident[:, :])
                last.then_inc(turned_over, 1)
                pe.wait_ge(turned_ready, 1)
                pe.wait_ge(params_in, 64)
                for k in range(KD):
                    last = pe.matmul(logits_ps[:, :], turned[:, k, :], wr[:, k, :], start=(k == 0), stop=(k == KD - 1))
                last.then_inc(logits_ready, 1)

            @block.scalar
            def _(act):
                act.wait_ge(exp_in, 1)
                act.activation(p[:, :], left[:, :], ACT.Exp).then_inc(exp_out, 1)
                act.wait_ge(exp_in, 2)
                act.activation(p[:, :], left[:, :], ACT.Exp).then_inc(exp_out, 1)
                act.wait_ge(exp_in, 3)
                act.activation(gate[:, :], peak[:, :], ACT.Exp).then_inc(exp_out, 1)

            @block.vector
            def _(dve):
                seq = Tally(order)

                def then(instruction):
                    seq.done(instruction)
                    dve.wait_ge(order, seq.now)

                def softmax(out, x, shifted, nth):
                    then(dve.tensor_reduce(low[:, :], x, AX.X, ALU.max))
                    dve.tensor_scalar(shifted, x, low[:, 0:1], None, ALU.subtract).then_inc(exp_in, 1)
                    dve.wait_ge(exp_out, nth)
                    then(dve.tensor_reduce(low[:, :], out, AX.X, ALU.add))
                    then(dve.reciprocal(low[:, :], low[:, :]))
                    then(dve.tensor_scalar(out, out, low[:, 0:1], None, ALU.mult))

                dve.wait_ge(turned_over, 1)
                dve.tensor_scalar(turned[:, :, :], turned_ps[:, :, :], 1.0 / N, None, ALU.mult).then_inc(turned_ready, 1)
                dve.wait_ge(logits_ready, 1)
                dve.wait_ge(params_in, 64)
                then(dve.tensor_tensor(left[:, :], logits_ps[:, :], br[:, :], ALU.add))
                softmax(p[:, :], left[:, :], left[:, :], 1)
                then(dve.tensor_scalar(load[:, :], p[:, :], float(N), None, ALU.mult))
                then(dve.reciprocal(scale[:, :], load[:, :]))
                then(dve.tensor_scalar(scale[:, :], scale[:, :], CAPACITY, 1.0, ALU.mult, ALU.subtract))
                then(dve.tensor_scalar(over[:, :], load[:, :], CAPACITY, None, ALU.is_gt))
                then(dve.tensor_tensor(scale[:, :], scale[:, :], over[:, :], ALU.mult))
                then(dve.scalar_tensor_tensor(left[:, :], scale[:, :], 1.0, p[:, :], ALU.add, ALU.mult))
                softmax(p[:, :], left[:, :], left[:, :], 2)
                lanes = keep.lane[:, 0:X1]
                for j in range(TOP):
                    then(dve.tensor_reduce(peak[:, j:j + 1], p[:, :], AX.X, ALU.max))
                    then(dve.tensor_scalar(over[:, :], p[:, :], peak[:, j:j + 1], None, ALU.is_ge))
                    then(dve.scalar_tensor_tensor(first[:, :], lanes, float(X1), over[:, :], ALU.subtract, ALU.mult))
                    then(dve.tensor_reduce(one[:, :], first[:, :], AX.X, ALU.min))
                    dve.tensor_scalar(chosen[:, j:j + 1], one[:, :], float(X1), None, ALU.add).then_inc(chosen_ready, 1)
                    if j + 1 < TOP:
                        then(dve.tensor_scalar(first[:, :], first[:, :], one[:, 0:1], None, ALU.is_equal))
                        then(dve.scalar_tensor_tensor(p[:, :], first[:, :], -2.0, p[:, :], ALU.mult, ALU.add))
                softmax(gate[:, :], peak[:, :], peak[:, :], 3)
                dve.wait_ge(w2_in, 32 * TOP)
                for j in range(TOP):
                    seq.done(dve.tensor_scalar(keep.ew2[:, j, :, :], keep.ew2[:, j, :, :], gate[:, j:j + 1], None, ALU.mult))
                    seq.done(dve.tensor_scalar(b2[:, j, :], b2[:, j, :], gate[:, j:j + 1], None, ALU.mult))
                dve.wait_ge(order, seq.now)
                then(dve.tensor_tensor(keep.eb2[:, :], b2[:, 0, :], b2[:, 1, :], ALU.add))


CH = F1 // P


def experts(nc, io, keep):
    with ExitStack() as ctx:
        s = Scope(nc, ctx, "ex")
        xt = s.sb("xt", [P, KD, TOK])
        h = s.sb("h", [P, TOP, CH, TOK])
        z = s.sb("z", [P, SB, D])
        stats = s.sb("stats", [P, SB, 6])
        aggr = s.sb("aggr", [P, SB, 2])
        std = s.sb("std", [P, SB])
        rstd = s.sb("rstd", [P, SB])
        eps = s.sb("eps", [P, 1])
        warmed = s.sb("warmed", [P, 1])
        turn = [s.ps(f"turn{n}", [P, KD, 2 * P]) for n in range(2)]
        wide = [s.ps(f"wide{n}", [P, 512]) for n in range(4)]
        sums = [s.ps(f"sums{n}", [P, 512]) for n in range(2)]
        xn = keep.xn

        turned = s.sem("turned")
        xt_ready = s.sem("xt_ready")
        wide_full = s.sem("wide_full")
        h_ready = s.sem("h_ready")
        sums_full = s.sem("sums_full")
        z_ready = s.sem("z_ready")
        biased = s.sem("biased")
        aggr_ready = s.sem("aggr_ready")
        std_ready = s.sem("std_ready")
        z_normed = s.sem("z_normed")
        scaled = s.sem("scaled")
        out_ready = s.sem("out_ready")
        stored = s.sem("stored")
        order = s.sem("order")
        pause = s.sem("pause")
        HW = TOP * CH * 2

        with nc.Block() as block:

            @block.sync
            def _(sp):
                for i in range(NSB):
                    sp.wait_ge(out_ready, i + 1)
                    if i < NSB - 1:
                        sp.dma_start(io["out"][i * TOK:(i + 1) * TOK, :].rearrange("(b p) d -> p b d", p=P),
                                     keep.x[:, i * SB:(i + 1) * SB, :]).then_inc(stored, 16)
                    else:
                        sp.dma_start(io["out"][i * TOK:(NB - 1) * P, :].rearrange("(b p) d -> p b d", p=P),
                                     keep.x[:, i * SB:NB - 1, :]).then_inc(stored, 16)
                        sp.dma_start(io["out"][(NB - 1) * P:N, :], keep.x[0:LAST, NB - 1, :]).then_inc(stored, 16)
                sp.wait_ge(stored, 16 * (NSB + 1))

            @block.tensor
            def _(pe):
                pe.sem_inc(wide_full, 1)
                for i in range(NSB):
                    for j in range(4):
                        t = i * 4 + j
                        if t >= 2:
                            pe.wait_ge(xt_ready, t - 1)
                        for b in turn_blocks(j):
                            for k in range(KD):
                                at0 = (b - 2 * j) * P
                                last = pe.transpose(turn[t % 2][:, k, at0:at0 + P], xn[:, i * SB + b, k * P:(k + 1) * P], keep.ident[:, :])
                        last.then_inc(turned, 1)
                    pe.wait_ge(xt_ready, 4 * i + 4)
                    for e in range(TOP):
                        for c in range(CH):
                            for half in range(2):
                                t = i * HW + (e * CH + c) * 2 + half
                                if t >= 4:
                                    pe.wait_ge(h_ready, t - 3)
                                for k in range(KD):
                                    last = pe.matmul(wide[t % 4][:, 0:HALF], keep.ew1[:, e, k, c * P:(c + 1) * P],
                                                     xt[:, k, half * HALF:(half + 1) * HALF], start=(k == 0), stop=(k == KD - 1))
                                last.then_inc(wide_full, 1)
                    pe.wait_ge(h_ready, (i + 1) * HW)
                    for b in range(SB):
                        t = i * SB + b
                        if t >= 2:
                            pe.wait_ge(z_ready, t - 1)
                        for e in range(TOP):
                            for c in range(CH):
                                last = pe.matmul(sums[t % 2][:, 0:D], h[:, e, c, b * P:(b + 1) * P], keep.ew2[:, e, c, :],
                                                 start=(e == 0 and c == 0), stop=(e == TOP - 1 and c == CH - 1))
                        last.then_inc(sums_full, 1)

            @block.scalar
            def _(act):
                for i in range(NSB):
                    for j in range(4):
                        t = i * 4 + j
                        width = len(turn_blocks(j)) * P
                        act.wait_ge(turned, t + 1)
                        if i >= 1:
                            act.wait_ge(wide_full, i * HW + 1)
                        act.copy(xt[:, :, 2 * j * P:2 * j * P + width], turn[t % 2][:, :, 0:width]).then_inc(xt_ready, 1)
                    for e in range(TOP):
                        for c in range(CH):
                            for half in range(2):
                                t = i * HW + (e * CH + c) * 2 + half
                                act.wait_ge(wide_full, t + 2)
                                if i >= 1:
                                    act.wait_ge(sums_full, i * SB)
                                act.activation(h[:, e, c, half * HALF:(half + 1) * HALF], wide[t % 4][:, 0:HALF], ACT.Gelu,
                                               bias=keep.eb1[:, e, c:c + 1]).then_inc(h_ready, 1)
                    act.wait_ge(aggr_ready, i + 1)
                    act.activation(std[:, :], aggr[:, :, 1], ACT.Sqrt, bias=eps[:, 0:1]).then_inc(std_ready, 1)

            @block.gpsimd
            def _(pool):
                for i in range(NSB):
                    here = slice(i * SB, (i + 1) * SB)
                    wide_row = lambda ap: spread(ap.rearrange("p (b d) -> p b d", b=1), [P, SB, D])
                    pool.wait_ge(turned, 4 * i + 4)
                    pool.tensor_tensor(xn[:, here, 0:D], xn[:, here, 0:D], wide_row(keep.eb2[:, :]), ALU.add).then_inc(biased, 1)
                    pool.tensor_tensor(keep.x[:, here, :], keep.x[:, here, :], wide_row(keep.beta[:, :]), ALU.add).then_inc(biased, 1)
                    pool.wait_ge(z_normed, i + 1)
                    pool.tensor_tensor(z[:, :, :], z[:, :, :], wide_row(keep.gamma[:, :]), ALU.mult).then_inc(scaled, 1)
                    pool.wait_ge(scaled, i + 1)
                    pool.wait_ge(biased, 2 * i + 2)
                    pool.tensor_tensor(keep.x[:, here, :], keep.x[:, here, :], z[:, :, :], ALU.add).then_inc(out_ready, 1)

            @block.vector
            def _(dve):
                seq = Tally(order)

                def then(instruction):
                    seq.done(instruction)
                    dve.wait_ge(order, seq.now)

                then(dve.memset(eps[:, :], 1e-5))
                for i in range(NSB):
                    dve.wait_ge(biased, 2 * i + 1)
                    if i >= 1:
                        dve.wait_ge(out_ready, i)
                    for b in range(SB):
                        t = i * SB + b
                        dve.wait_ge(sums_full, t + 1)
                        dve.tensor_tensor(z[:, b, :], sums[t % 2][:, 0:D], xn[:, t, 0:D], ALU.add).then_inc(z_ready, 1)
                        if b:
                            dve.wait_ge(z_ready, t)
                            last = dve.bn_stats(stats[:, b - 1, :], z[:, b - 1, :])
                    dve.wait_ge(z_ready, (i + 1) * SB)
                    then(dve.bn_stats(stats[:, SB - 1, :], z[:, SB - 1, :]))
                    for b in range(SB):
                        last = dve.bn_aggr(aggr[:, b, :], stats[:, b, :])
                    last.then_inc(aggr_ready, 1)
                    dve.wait_ge(std_ready, i + 1)
                    then(dve.reciprocal(rstd[:, :], std[:, :]))
                    for b in range(SB):
                        last = dve.tensor_scalar(z[:, b, :], z[:, b, :], aggr[:, b, 0:1], rstd[:, b:b + 1], ALU.subtract, ALU.mult)
                    last.then_inc(z_normed, 1)


def program(nc, io, upto=5):
    with ExitStack() as ctx:
        s = Scope(nc, ctx, "keep")
        keep = Kept()
        keep.x = s.sb("x", [P, NB, D])
        keep.step_edge = s.sb("step_edge", [1, TABLE * P], I32)
        keep.step_block = s.sb("step_block", [1, TABLE * P], I32)
        keep.lane = s.sb("lane", [P, P])
        keep.ident = s.sb("ident", [P, P])
        keep.below = s.sb("below", [P, P], BF16)
        keep.ones = s.sb("ones", [P, P])
        keep.node_id = s.sb("node_id", [P, NB])
        keep.block_base = s.sb("block_base", [P, NB])
        keep.spare_row = s.sb("spare_row", [P, 1])
        keep.node = s.sb("node", [P, NB, 2 * HEADS])
        keep.a2_bound = s.sb("a2_bound", [P, HEADS])
        keep.added = s.sems("added", LOTS)
        keep.rows_dram = nc.dram_tensor("rows_dram", [NP, GROW], F32, kind="Internal").ap()
        keep.residual_dram = nc.dram_tensor("residual_dram", [NP, D], F32, kind="Internal").ap()
        keep.src_list = nc.dram_tensor("src_list", [E + STEP], I32, kind="Internal").ap()
        keep.dst_list = nc.dram_tensor("dst_list", [E + STEP], I32, kind="Internal").ap()
        keep.pair_list = nc.dram_tensor("pair_list", [E + STEP, 2], I32, kind="Internal").ap()
        keep.table_dram = nc.dram_tensor("table_dram", [2, TABLE * P], I32, kind="Internal").ap()
        keep.partial = [nc.dram_tensor(f"partial{k}", [NP + P, D], F32, kind="Internal").ap() for k in range(SUMS)]
        with ExitStack() as ctx1:
            keep.xn = Scope(nc, ctx1, "first").sb("xn", [P, NB, ROW])
            load_and_index(nc, io, keep)
            scatter_sums(nc, io, keep)
        with ExitStack() as ctx2:
            w = Scope(nc, ctx2, "w")
            keep.w12 = w.sb("w12", [P, KD, D])
            keep.b12 = w.sb("b12", [P, D])
            keep.wr = w.sb("wr", [P, KD, X0])
            keep.br = w.sb("br", [P, X0])
            keep.bo = w.sb("bo", [X0, D])
            keep.bn = w.sb("bn", [P, 4, 2 * X0])
            keep.proj = w.sb("proj", [P, KD, PROJ])
            if upto >= 2:
                fold_weights(nc, io, keep)
                mixture(nc, io, keep)
        keep.xn = s.sb("acc", [P, NB, ROW])
        if upto >= 3:
            attend(nc, io, keep)
        with ExitStack() as ctx3:
            w = Scope(nc, ctx3, "last")
            keep.ew1 = w.sb("ew1", [P, TOP, KD, F1])
            keep.eb1 = w.sb("eb1", [P, TOP, F1 // P])
            keep.ew2 = w.sb("ew2", [P, TOP, F1 // P, D])
            keep.eb2 = w.sb("eb2", [P, D])
            keep.gamma = w.sb("gamma", [P, D])
            keep.beta = w.sb("beta", [P, D])
            with ExitStack() as ctx4:
                keep.node_sum = Scope(nc, ctx4, "mean").sb("node_sum", [P, D])
                if upto >= 4:
                    finish_attention(nc, io, keep)
                if upto >= 5:
                    route(nc, io, keep)
            if upto >= 5:
                experts(nc, io, keep)
        return keep


def kernel(**inputs):
    import numpy as np
    import concourse.bacc as bacc
    from concourse.bass_utils import run_bass_kernel_spmd

    nc = bacc.Bacc("TRN2", target_bir_lowering=False, num_devices=1)
    io, arrays = {}, {}
    for name, value in inputs.items():
        arrays["in_" + name] = np.ascontiguousarray(value)
        io[name] = nc.dram_tensor("in_" + name, value.shape, mybir.dt.from_np(arrays["in_" + name].dtype),
                                           kind="ExternalInput").ap()
    io["out"] = nc.dram_tensor("out", [N, D], F32, kind="ExternalOutput").ap()
    program(nc, io)
    return run_bass_kernel_spmd(nc, [arrays], core_ids=[0]).results[0]["out"]
```

```python
from contextlib import ExitStack

import concourse.bass as bass
from concourse import mybir

F32 = mybir.dt.float32
BF16 = mybir.dt.bfloat16
I32 = mybir.dt.int32
ALU = mybir.AluOpType
ACT = mybir.ActivationFunctionType
AX = mybir.AxisListType
F32R = mybir.dt.float32r

P = 128
N = 6250
E = 200000
D = 256
KD = D // P
NB = -(-N // P)
LAST = N - (NB - 1) * P
NP = NB * P
G = 2
STEP = G * P
STEPS = (E + NB * (STEP - 1)) // STEP
TABLE = -(-STEPS // P)
SLOTS = 8
ROUNDS = -(-STEPS // SLOTS)
LOTS = SLOTS * G
ASLOTS = 16
AROUNDS = -(-STEPS // ASLOTS)
MASKS = 8
TILES = 4
SUMS = 4
LAG = SUMS // G
NOWHERE = 1 << 14
ER = 125
EC = E // ER
H0 = 512
X0 = 8
HEADS, DO = 4, 64
SLOPE = 0.01
ROW = D + HEADS
GROW = D + 2 * HEADS
PROJ = GROW + ROW
TINY = 1e-30
SB = 7
NSB = NB // SB
TOK = SB * P
HALF = TOK // 2
X1, F1 = 8, 512
TOP = 2
CAPACITY = float(-(-N * 5 // (4 * X1)))
DVE_MIX = 21


class Tally:

    def __init__(self, sem):
        self.sem, self.base, self.n, self.outer = sem, 0, 0, []

    def done(self, instruction, by=1):
        instruction.then_inc(self.sem, by)
        self.n += by

    def enter(self, i, per_round):
        self.outer.append((self.base, self.n, per_round))
        self.base, self.n = self.base + self.n + i * per_round, 0

    def leave(self, rounds):
        base, n, per_round = self.outer.pop()
        assert self.n == per_round, (self.sem, self.n, per_round)
        self.base, self.n = base, n + rounds * per_round

    @property
    def now(self):
        return self.base + self.n


class Kept:
    pass


class Scope:

    def __init__(self, nc, ctx, stage):
        self.nc, self.ctx, self.stage, self.used = nc, ctx, stage, []
        ctx.callback(self.free_semaphores)

    def sb(self, name, shape, dtype=F32):
        return self.ctx.enter_context(self.nc.sbuf_tensor(f"{self.stage}_{name}", shape, dtype))

    def ps(self, name, shape, dtype=F32):
        return self.ctx.enter_context(self.nc.psum_tensor(f"{self.stage}_{name}", shape, dtype))

    def sem(self, name):
        self.used.append(self.nc.alloc_semaphore(name=f"{self.stage}_{name}"))
        return self.used[-1]

    def sems(self, name, n):
        return [self.sem(f"{name}{i}") for i in range(n)]

    def free_semaphores(self):
        if self.used:
            self.nc.clear_and_free_semaphores(self.used)
            self.nc.all_engine_barrier()


def spread(ap, shape):
    return ap.to_broadcast(shape)


def registers(eng, name, n):
    return [eng.alloc_register(f"{name}{u}") for u in range(n)]


def step_values(eng, regs, row, i, most):
    eng.load(regs, row[:, bass.ds(i * len(regs), len(regs))])
    return [eng.snap(r, min_val=0, max_val=most) for r in regs]


def load_and_index(nc, io, keep):
    with ExitStack() as ctx:
        s = Scope(nc, ctx, "prep")
        edges = s.sb("edges", [ER, 2, EC], I32)
        pairs = s.sb("pairs", [ER, EC, 2], I32)
        padding = s.sb("padding", [1, 4, STEP], I32)
        bounds = s.sb("bounds", [P, NB + 1])
        bounds_i = s.sb("bounds_i", [P, NB + 1], I32)
        last_dst = s.sb("last_dst", [ER, 1])
        ends_before = s.sb("ends_before", [ER, NB + 1])
        bound = s.sb("bound", [NB + 1, 1])
        row_of = s.sb("row_of", [NB + 1, 1])
        row_index = s.sb("row_index", [NB + 1, 1], I32)
        bound_row = s.sb("bound_row", [NB + 1, EC], I32)
        below_bound = s.sb("below_bound", [NB + 1, EC])
        start = s.sb("start", [NB + 1, 1])
        diagonal = s.sb("diagonal", [NB + 1, NB + 1])
        starts = s.sb("starts", [P, NB + 1])
        count = s.sb("count", [P, NB])
        nsteps_i = s.sb("nsteps_i", [P, NB], I32)
        nsteps = s.sb("nsteps", [P, NB])
        until = s.sb("until", [P, NB])
        zeros = s.sb("zeros", [P, 512])
        step_i = s.sb("step_i", [P, TABLE], I32)
        step_id = s.sb("step_id", [P, TABLE])
        past = s.sb("past", [P, TABLE, NB])
        part = s.sb("part", [P, TABLE, NB])
        block_of = s.sb("block_of", [P, TABLE])
        before = s.sb("before", [P, TABLE])
        edge0 = s.sb("edge0", [P, TABLE])
        inside = s.sb("inside", [P, TABLE])
        table = s.sb("table", [P, 2, TABLE], I32)
        ints = s.sb("ints", [P, P], I32)
        small_i = s.sb("small_i", [P, 2 * NB + 1], I32)
        stats = s.sb("stats", [P, NB, 6])
        aggr = s.sb("aggr", [P, NB, 2])
        std = s.sb("std", [P, NB])
        rstd = s.sb("rstd", [P, NB])
        eps = s.sb("eps", [P, 1])
        row_ps = s.ps("row_ps", [NB + 1, 1])
        total = s.ps("total", [P, NB + 1])

        x_in = s.sem("x_in")
        x_last = s.sem("x_last")
        edges_in = s.sem("edges_in")
        x_pad = s.sem("x_pad")
        made = s.sem("made")
        consts = s.sem("consts")
        ends_compared = s.sem("ends_compared")
        row_found = s.sem("row_found")
        row_ready = s.sem("row_ready")
        row_in = s.sem("row_in")
        start_ready = s.sem("start_ready")
        summed = s.sem("summed")
        stats_done = s.sem("stats_done")
        std_done = s.sem("std_done")
        edges_out = s.sem("edges_out")
        table_ready = s.sem("table_ready")
        table_io = s.sem("table_io")
        pairs_ready = s.sem("pairs_ready")
        pads_ready = s.sem("pads_ready")
        order = s.sem("order")
        xn_ready = s.sem("xn_ready")
        spare_out = s.sem("spare_out")

        with nc.Block() as block:

            @block.sync
            def _(sp):
                sp.dma_start(edges[:, 0, :], io["src"].rearrange("(p c) -> p c", p=ER)).then_inc(edges_in, 16)
                sp.dma_start(edges[:, 1, :], io["dst"].rearrange("(p c) -> p c", p=ER)).then_inc(edges_in, 16)
                blocks = io["x"][0:(NB - 1) * P, :].rearrange("(b p) d -> p b d", p=P)
                for b in range(0, NB - 1, 12):
                    sp.dma_start(keep.x[:, b:b + 12, :], blocks[:, b:b + 12, :]).then_inc(x_in, 16)
                sp.wait_ge(x_pad, 1)
                sp.dma_start(keep.x[0:LAST, NB - 1, :], io["x"][(NB - 1) * P:N, :]).then_inc(x_last, 16)
                sp.wait_ge(edges_in, 32)
                sp.dma_start(keep.src_list[0:E].rearrange("(p c) -> p c", p=ER), edges[:, 0, :]).then_inc(edges_out, 16)
                sp.dma_start(keep.dst_list[0:E].rearrange("(p c) -> p c", p=ER), edges[:, 1, :]).then_inc(edges_out, 16)
                sp.wait_ge(pads_ready, 3)
                one = lambda ap: ap.rearrange("(a c) -> a c", a=1)
                sp.dma_start(one(keep.src_list[E:E + STEP]), padding[:, 0, :]).then_inc(edges_out, 16)
                sp.dma_start(one(keep.dst_list[E:E + STEP]), padding[:, 1, :]).then_inc(edges_out, 16)
                sp.dma_start(keep.pair_list[E:E + STEP, :].rearrange("(a c) t -> a (c t)", a=1),
                             padding[:, 2:4, :].rearrange("p a b -> p (a b)")).then_inc(edges_out, 16)
                sp.wait_ge(pairs_ready, 2)
                sp.dma_start(keep.pair_list[0:E, :].rearrange("(p c) t -> p (c t)", p=ER),
                             pairs[:, :, :].rearrange("p c t -> p (c t)")).then_inc(edges_out, 16)
                sp.wait_ge(table_ready, 1)
                for t in range(2):
                    sp.dma_start(keep.table_dram[t:t + 1, :].rearrange("t (p j) -> p (t j)", p=P), table[:, t, :]).then_inc(table_io, 16)
                sp.wait_ge(table_io, 32)
                sp.dma_start(keep.step_edge[:, :], keep.table_dram[0:1, :]).then_inc(table_io, 16)
                sp.dma_start(keep.step_block[:, :], keep.table_dram[1:2, :]).then_inc(table_io, 16)
                sp.wait_ge(table_io, 64)
                sp.wait_ge(edges_out, 96)

            @block.gpsimd
            def _(pool):
                made_n = Tally(made)
                made_n.done(pool.memset(zeros[:, :], 0.0))
                made_n.done(pool.memset(keep.ident[:, :], 0.0))
                made_n.done(pool.memset(keep.below[:, :], 1.0))
                pool.memset(keep.ones[:, :], 1.0).then_inc(consts, 1)
                pool.wait_ge(made, 3)
                pool.affine_select(out=keep.ident[:, :], in_=keep.ident[:, :], compare_op=ALU.not_equal, fill=1.0,
                                   base=0, pattern=[[-1, P]], channel_multiplier=1).then_inc(consts, 1)
                pool.affine_select(out=keep.below[:, :], in_=keep.below[:, :], compare_op=ALU.is_gt, fill=0.0,
                                   base=0, pattern=[[-1, P]], channel_multiplier=1).then_inc(consts, 1)
                made_n.done(pool.iota(ints[:, :], pattern=[[1, P]], base=0, channel_multiplier=0))
                made_n.done(pool.iota(bounds_i[:, :], pattern=[[P, NB + 1]], base=0, channel_multiplier=0))
                made_n.done(pool.iota(small_i[:, 0:NB], pattern=[[P, NB]], base=0, channel_multiplier=1))
                made_n.done(pool.iota(small_i[:, NB:2 * NB], pattern=[[P, NB]], base=0, channel_multiplier=0))
                made_n.done(pool.iota(small_i[:, 2 * NB:2 * NB + 1], pattern=[[0, 1]], base=NP, channel_multiplier=1))
                made_n.done(pool.iota(step_i[:, :], pattern=[[1, TABLE]], base=0, channel_multiplier=TABLE))
                pool.wait_ge(row_ready, 1)
                pool.indirect_dma_start(out=bound_row[:, :], out_offset=None, in_=io["dst"].rearrange("(p c) -> p c", p=ER),
                                        in_offset=bass.IndirectOffsetOnAxis(ap=row_index[:, 0:1], axis=0)).then_inc(row_in, 16)
                part_rows = (NP + P) * SUMS // LOTS
                for k in range(LOTS):
                    if k % SUMS == 0:
                        continue
                    rows = keep.partial[k % SUMS][k // SUMS * part_rows:(k // SUMS + 1) * part_rows, :]
                    pool.dma_start(rows.rearrange("(p a) d -> p a d", p=64),
                                   spread(zeros[0:64, 0:D].rearrange("p (a d) -> p a d", a=1), [64, part_rows // 64, D]),
                                   ).then_inc(keep.added[k], 16)
                quarters = [NB * n // SUMS for n in range(SUMS + 1)]
                for n in range(SUMS):
                    b0, b1 = quarters[n], quarters[n + 1]
                    pool.wait_ge(xn_ready, b1)
                    pool.dma_start(keep.partial[0][b0 * P:b1 * P, :].rearrange("(b p) d -> p b d", p=P),
                                   keep.xn[:, b0:b1, 0:D]).then_inc(keep.added[n * SUMS], 16)
                pool.dma_start(keep.partial[0][NP:NP + P, :], zeros[:, 0:D]).then_inc(spare_out, 16)
                pool.wait_ge(spare_out, 16)
                for k in range(LOTS):
                    pool.wait_ge(keep.added[k], 16)

            @block.scalar
            def _(act):
                act.wait_ge(stats_done, 1)
                act.activation(std[:, :], aggr[:, :, 1], ACT.Sqrt, bias=eps[:, 0:1]).then_inc(std_done, 1)

            @block.tensor
            def _(pe):
                pe.wait_ge(ends_compared, 1)
                pe.wait_ge(consts, 4)
                pe.matmul(row_ps[:, :], ends_before[:, :], keep.ones[0:ER, 0:1], start=True, stop=True).then_inc(row_found, 1)
                pe.wait_ge(start_ready, 1)
                pe.matmul(total[:, :], keep.ones[0:NB + 1, :], diagonal[:, :], start=True, stop=True).then_inc(summed, 1)

            @block.vector
            def _(dve):
                seq = Tally(order)

                def then(instruction):
                    seq.done(instruction)
                    dve.wait_ge(order, seq.now)

                dve.memset(keep.x[:, NB - 1, :], 0.0).then_inc(x_pad, 1)
                seq.done(dve.memset(eps[:, :], 1e-5))
                dve.memset(padding[:, 0, :], 0).then_inc(pads_ready, 1)
                dve.memset(padding[:, 1, :], NOWHERE).then_inc(pads_ready, 1)
                then(dve.memset(padding[:, 2:4, :], 0))
                dve.memset(padding[:, 2:4, :].rearrange("p a (b t) -> p (a b) t", t=2)[:, :, 1], NOWHERE).then_inc(pads_ready, 1)
                dve.wait_ge(made, 9)
                then(dve.tensor_copy(keep.lane[:, :], ints[:, :]))
                then(dve.tensor_scalar(bounds[:, :], bounds_i[:, :], 0.5, None, ALU.subtract))
                then(dve.tensor_copy(keep.node_id[:, :], small_i[:, 0:NB]))
                then(dve.tensor_copy(keep.block_base[:, :], small_i[:, NB:2 * NB]))
                then(dve.tensor_copy(keep.spare_row[:, :], small_i[:, 2 * NB:2 * NB + 1]))
                dve.tensor_copy(step_id[:, :], step_i[:, :]).then_inc(consts, 1)
                dve.wait_ge(edges_in, 32)
                then(dve.tensor_copy(last_dst[:, :], edges[:, 1, EC - 1:EC]))
                dve.tensor_scalar(ends_before[:, :], bounds[0:ER, :], last_dst[:, 0:1], None, ALU.is_gt).then_inc(ends_compared, 1)
                then(dve.tensor_scalar(bound[:, :], keep.node_id[0:NB + 1, 0:1], float(P), 0.5, ALU.mult, ALU.subtract))
                dve.wait_ge(row_found, 1)
                then(dve.tensor_scalar(row_of[:, :], row_ps[:, :], float(ER - 1), None, ALU.min))
                dve.tensor_copy(row_index[:, :], row_of[:, :]).then_inc(row_ready, 1)
                dve.tensor_copy(pairs[:, :, 0], edges[:, 0, :]).then_inc(pairs_ready, 1)
                dve.tensor_copy(pairs[:, :, 1], edges[:, 1, :]).then_inc(pairs_ready, 1)
                dve.wait_ge(x_in, 64)
                dve.wait_ge(x_last, 16)
                dve.wait_ge(x_pad, 1)
                dve.wait_ge(order, seq.now)
                with dve.Fori(0, NB) as b:
                    seq.enter(b, 1)
                    seq.done(dve.bn_stats(stats[:, bass.ds(b, 1), :], keep.x[:, bass.ds(b, 1), :]))
                    seq.leave(NB)
                dve.wait_ge(order, seq.now)
                for b in range(NB):
                    last = dve.bn_aggr(aggr[:, b, :], stats[:, b, :])
                last.then_inc(stats_done, 1)
                dve.wait_ge(std_done, 1)
                then(dve.reciprocal(rstd[:, :], std[:, :]))
                with dve.Fori(0, NB) as b:
                    dve.tensor_scalar(keep.xn[:, bass.ds(b, 1), 0:D], keep.x[:, bass.ds(b, 1), :],
                                      aggr[:, bass.ds(b, 1), 0], rstd[:, bass.ds(b, 1)],
                                      ALU.subtract, ALU.mult).then_inc(xn_ready, 1)
                dve.wait_ge(row_in, 16)
                then(dve.tensor_scalar(below_bound[:, :], bound_row[:, :], bound[:, 0:1], None, ALU.is_lt))
                then(dve.tensor_reduce(start[:, :], below_bound[:, :], AX.X, ALU.add))
                then(dve.scalar_tensor_tensor(start[:, :], row_of[:, :], float(EC), start[:, :], ALU.mult, ALU.add))
                dve.wait_ge(consts, 4)
                dve.tensor_scalar(diagonal[:, :], keep.ident[0:NB + 1, 0:NB + 1], start[:, 0:1], None, ALU.mult).then_inc(start_ready, 1)
                dve.wait_ge(summed, 1)
                then(dve.tensor_copy(starts[:, :], total[:, :]))
                then(dve.tensor_tensor(count[:, :], starts[:, 1:NB + 1], starts[:, 0:NB], ALU.subtract))
                then(dve.tensor_scalar(nsteps_i[:, :], count[:, :], float(STEP - 1), None, ALU.add))
                then(dve.tensor_scalar(nsteps_i[:, :], nsteps_i[:, :], STEP.bit_length() - 1, None, ALU.logical_shift_right))
                then(dve.tensor_copy(nsteps[:, :], nsteps_i[:, :]))
                dve.wait_ge(made, 1)
                then(dve.tensor_tensor_scan(until[:, :], nsteps[:, :], zeros[:, 0:NB], 0.0, ALU.add, ALU.add))
                every = [P, TABLE, NB]
                row = lambda ap: spread(ap.rearrange("p (j b) -> p j b", j=1), every)
                dve.wait_ge(consts, 4)
                then(dve.tensor_tensor(past[:, :, :], row(until[:, :]),
                                       spread(step_id[:, :].rearrange("p (j b) -> p j b", b=1), every), ALU.is_le))
                then(dve.tensor_reduce(block_of[:, :], past[:, :, :], AX.X, ALU.add))
                then(dve.tensor_tensor(part[:, :, :], past[:, :, :], row(count[:, :]), ALU.mult))
                then(dve.tensor_reduce(edge0[:, :], part[:, :, :], AX.X, ALU.add))
                then(dve.tensor_tensor(part[:, :, :], past[:, :, :], row(until[:, :]), ALU.mult))
                then(dve.tensor_reduce(before[:, :], part[:, :, :], AX.X, ALU.max))
                then(dve.tensor_tensor(inside[:, :], step_id[:, :], before[:, :], ALU.subtract))
                then(dve.scalar_tensor_tensor(edge0[:, :], inside[:, :], float(STEP), edge0[:, :], ALU.mult, ALU.add))
                then(dve.tensor_scalar(table[:, 0, :], edge0[:, :], float(E), None, ALU.min))
                dve.tensor_scalar(table[:, 1, :], block_of[:, :], float(NB - 1), None, ALU.min).then_inc(table_ready, 1)
                dve.wait_ge(order, seq.now)


def fold_weights(nc, io, keep, ctx):
    s = Scope(nc, ctx, "fold")
    w1 = s.sb("w1", [P, KD, H0])
    w2 = s.sb("w2", [P, H0 // P, D])
    w1t = s.sb("w1t", [P, H0 // P, D])
    b1 = s.sb("b1", [P, H0 // P])
    b1_wide = s.sb("b1_wide", [P, H0 // P, P])
    b2 = s.sb("b2", [P, D])
    norms = s.sb("norms", [2 * X0, 2, 5, P])
    root = s.sb("root", [2 * X0, 2, P])
    eps = s.sb("eps", [P, 1])
    lines = s.sb("lines", [2 * X0, 4, P])
    al = s.sb("al", [P, 2, D])
    prod = s.sb("prod", [P, KD, 2, HEADS, DO])
    w1t_ps = [s.ps(f"w1t_ps{k}", [P, H0 // P, P]) for k in range(KD)]
    w12_ps = s.ps("w12_ps", [P, KD, D])
    b12_ps = s.ps("b12_ps", [P, D])
    norm_ps = w1t_ps[0][:, 0, 0:8 * X0].rearrange("p (n c) -> p n c", n=4)

    w_in = s.sem("w_in")
    b_in = s.sem("b_in")
    norms_in = s.sem("norms_in")
    heads_in = s.sem("heads_in")
    others_in = s.sem("others_in")
    w1_turned = s.sem("w1_turned")
    w1t_ready = s.sem("w1t_ready")
    wide_ready = s.sem("wide_ready")
    w12_done = s.sem("w12_done")
    b12_done = s.sem("b12_done")
    var_ready = s.sem("var_ready")
    root_ready = s.sem("root_ready")
    lines_ready = s.sem("lines_ready")
    norm_done = s.sem("norm_done")
    order = s.sem("order")


    def load(sp):
        sp.dma_start(w1[:, :, :], io["L0_gnn_W1"].rearrange("(k p) h -> p k h", p=P)).then_inc(w_in, 16)
        sp.dma_start(w2[:, :, :], io["L0_gnn_W2"].rearrange("(c p) d -> p c d", p=P)).then_inc(w_in, 16)
        with nc.allow_non_contiguous_dma(reason="512 words"):
            sp.dma_start(b1[:, :], io["L0_gnn_b1"].rearrange("(c p) -> p c", p=P)).then_inc(b_in, 16)
        sp.dma_start(b2[:, :], io["L0_gnn_b2"].partition_broadcast(P)).then_inc(b_in, 16)
        for layer, names in enumerate((("g1", "be1", "m1", "v1", "b1"), ("g2", "be2", "m2", "v2", "b2"))):
            vectors = (io["L0_ffn_g1"], io["L0_ffn_be1"], io["L0_ffn_m1"], io["L0_ffn_v1"], io["L0_ffn_b1"]) if layer == 0 else \
                      (io["L0_ffn_g2"], io["L0_ffn_be2"], io["L0_ffn_m2"], io["L0_ffn_v2"], io["L0_ffn_b2"])
            for n, v in enumerate(vectors):
                sp.dma_start(norms[:, layer, n, :], v.rearrange("e (c p) -> (e c) p", p=P)).then_inc(norms_in, 16)
        for k in range(KD):
            rows = slice(k * P, (k + 1) * P)
            sp.dma_start(keep.proj[:, k, 0:D].rearrange("p (h o) -> p h o", h=HEADS),
                         io["L1_gnn_W_fc"][:, rows, :].rearrange("h p o -> p h o")).then_inc(heads_in, 16)
            sp.dma_start(keep.proj[:, k, GROW + HEADS:PROJ].rearrange("p (h o) -> p h o", h=HEADS),
                         io["L1_gnn_W_res"][:, rows, :].rearrange("h p o -> p h o")).then_inc(others_in, 16)
        sp.dma_start(al[:, 0, :], io["L1_gnn_W_ar"].rearrange("h o a -> (h o a)").partition_broadcast(P)).then_inc(heads_in, 16)
        sp.dma_start(al[:, 1, :], io["L1_gnn_W_al"].rearrange("h o a -> (h o a)").partition_broadcast(P)).then_inc(heads_in, 16)
        sp.dma_start(keep.wr[:, :, :], io["L0_ffn_Wr"].rearrange("(k p) e -> p k e", p=P)).then_inc(others_in, 16)
        sp.dma_start(keep.br[:, :], io["L0_ffn_br"].partition_broadcast(P)).then_inc(others_in, 16)
        sp.dma_start(keep.bo[:, :], io["L0_ffn_bo"]).then_inc(others_in, 16)

    def tensor(pe):
        pe.wait_ge(w_in, 32)
        for k in range(KD):
            for c in range(H0 // P):
                last = pe.transpose(w1t_ps[k][:, c, :], w1[:, k, c * P:(c + 1) * P], keep.ident[:, :])
        last.then_inc(w1_turned, 1)
        pe.wait_ge(b_in, 32)
        pe.wait_ge(wide_ready, 1)
        for c in range(H0 // P):
            last = pe.matmul(b12_ps[:, :], b1_wide[:, c, :], w2[:, c, :], start=(c == 0), stop=(c == H0 // P - 1))
        last.then_inc(b12_done, 1)
        pe.wait_ge(w1t_ready, KD)
        for k in range(KD):
            for c in range(H0 // P):
                last = pe.matmul(w12_ps[:, k, :], w1t[:, c, k * P:(k + 1) * P], w2[:, c, :],
                                 start=(c == 0), stop=(c == H0 // P - 1))
        last.then_inc(w12_done, 1)
        pe.wait_ge(lines_ready, 4)
        for n in range(4):
            last = pe.transpose(norm_ps[:, n, :], lines[:, n, :], keep.ident[0:2 * X0, 0:2 * X0])
        last.then_inc(norm_done, 1)

    def scalar(act):
        act.wait_ge(w1_turned, 1)
        for k in range(KD):
            act.copy(w1t[:, :, k * P:(k + 1) * P], w1t_ps[k][:, :, :]).then_inc(w1t_ready, 1)
        act.wait_ge(var_ready, 1)
        act.wait_ge(norms_in, 160)
        act.activation(root[:, :, :], norms[:, :, 3, :], ACT.Sqrt, bias=eps[0:2 * X0, 0:1]).then_inc(root_ready, 1)

    def vector(dve):
        seq = Tally(order)

        def then(instruction):
            seq.done(instruction)
            dve.wait_ge(order, seq.now)

        dve.memset(eps[:, :], 1e-3).then_inc(var_ready, 1)
        dve.wait_ge(b_in, 32)
        dve.tensor_copy(b1_wide[:, :, :], spread(b1[:, :].rearrange("p (c n) -> p c n", n=1), [P, H0 // P, P]))\
           .then_inc(wide_ready, 1)
        dve.wait_ge(root_ready, 1)
        then(dve.reciprocal(root[:, :, :], root[:, :, :]))
        for layer in range(2):
            g, be, m, v, b = (norms[:, layer, n, :] for n in range(5))
            scale, shift = lines[:, 2 * layer, :], lines[:, 2 * layer + 1, :]
            dve.tensor_tensor(scale, g, root[:, layer, :], ALU.mult).then_inc(lines_ready, 1)
            then(dve.tensor_tensor(b, b, m, ALU.subtract))
            dve.wait_ge(lines_ready, 2 * layer + 1)
            then(dve.tensor_tensor(b, b, scale, ALU.mult))
            dve.tensor_tensor(shift, b, be, ALU.add).then_inc(lines_ready, 1)
        dve.wait_ge(heads_in, 16 * (KD + 2))
        for k in range(KD):
            for n in range(2):
                then(dve.tensor_tensor(prod[:, k, n, :, :], keep.proj[:, k, 0:D].rearrange("p (h o) -> p h o", h=HEADS),
                                       al[:, n, :].rearrange("p (h o) -> p h o", h=HEADS), ALU.mult))
                at = D + 2 * n * HEADS
                seq.done(dve.tensor_reduce(keep.proj[:, k, at:at + HEADS], prod[:, k, n, :, :], AX.X, ALU.add))
        dve.wait_ge(order, seq.now)
        seq.done(dve.tensor_scalar(keep.proj[:, :, D + HEADS:GROW], keep.proj[:, :, D:ROW], SLOPE, None, ALU.mult))
        dve.wait_ge(b12_done, 1)
        seq.done(dve.tensor_tensor(keep.b12[:, :], b12_ps[:, :], b2[:, :], ALU.add))
        dve.wait_ge(order, seq.now)
        bias = lambda n: spread(keep.b12[:, :].rearrange("p (b d) -> p b d", b=1), [P, n, D])
        seq.done(dve.tensor_tensor(keep.x[:, 0:NB // 2, :], keep.x[:, 0:NB // 2, :], bias(NB // 2), ALU.add))
        seq.done(dve.tensor_tensor(keep.x[:, NB // 2:NB, :], keep.x[:, NB // 2:NB, :], bias(NB - NB // 2), ALU.add))
        dve.wait_ge(w12_done, 1)
        seq.done(dve.tensor_copy(keep.w12[:, :, :], w12_ps[:, :, :]))
        dve.wait_ge(norm_done, 1)
        seq.done(dve.tensor_copy(keep.bn[:, :, :], norm_ps[:, :, :]))
        dve.wait_ge(order, seq.now)

    def loaded(sp):
        sp.wait_ge(others_in, 16 * (KD + 3))

    return load, loaded, tensor, scalar, vector


def scatter_sums(nc, io, keep):
    with ExitStack() as ctx:
        s = Scope(nc, ctx, "scat")
        cols = s.sb("cols", [P, SLOTS, G, 2], I32)
        rows = s.sb("rows", [P, SLOTS, STEP], I32)
        dst_in = s.sb("dst_in", [P, SLOTS, G])
        is_dst = s.sb("is_dst", [P, SLOTS, G, P], BF16)
        same = s.sb("same", [P, SLOTS, G, P], BF16)
        junk = s.sb("junk", [P, 2, G, P], BF16)
        repeated = s.sb("repeated", [P, SLOTS, G])
        to_spare = s.sb("to_spare", [P, SLOTS, G])
        index = s.sb("index", [P, SLOTS, G], I32)
        merge = s.sb("merge", [P, SLOTS, G, P])
        values = s.sb("values", [P, SLOTS, G, D])
        merge_ps = [s.ps(f"merge_ps{u}", [P, G, P]) for u in range(2)]
        values_ps = [s.ps(f"values_ps{u}", [P, G, D]) for u in range(2)]

        cols_in = s.sems("cols_in", SLOTS)
        rows_in = s.sems("rows_in", SLOTS)
        masks_ready = s.sem("masks_ready")
        index_ready = s.sem("index_ready")
        merged = s.sem("merged")
        merge_ready = s.sem("merge_ready")
        summed = s.sem("summed")
        values_ready = s.sem("values_ready")
        lists_free = s.sem("lists_free")
        order = s.sem("order")
        turn = s.sem("turn")

        fold_load, fold_loaded, fold_tensor, fold_scalar, fold_vector = fold_weights(nc, io, keep, ctx)

        with nc.Block() as block:

            @block.sync
            def _(sp):
                regs = registers(sp, "scat_first", SLOTS)
                with sp.Fori(0, ROUNDS) as i:
                    firsts = step_values(sp, regs, keep.step_edge, i, E)
                    for u, first in enumerate(firsts):
                        sp.wait_ge(lists_free, i * SLOTS + u + 1)
                        sp.sem_inc(turn, 1)
                        sp.dma_start(cols[:, u, :, :].rearrange("p g t -> p (g t)"),
                                     keep.pair_list[bass.ds(first, STEP), :].rearrange("(p g) t -> p (g t)", g=G)
                                     ).then_inc(cols_in[u], 16)
                        sp.dma_start(rows[:, u, :], keep.src_list[bass.ds(first, STEP)].partition_broadcast(P)
                                     ).then_inc(rows_in[u], 16)
                fold_load(sp)
                fold_loaded(sp)

            @block.vector
            def _(dve):
                seq = Tally(order)

                every = [P, G, P]
                dve.sem_inc(lists_free, SLOTS)
                regs = registers(dve, "scat_dve", SLOTS)
                with dve.Fori(0, ROUNDS) as i:
                    in_block = step_values(dve, regs, keep.step_block, i, NB - 1)
                    seq.enter(i, SLOTS * (2 + G))

                    def write_index(u):
                        for g in range(G):
                            dve.wait_ge(keep.added[u * G + g], i * 16 + 16)
                        dve.wait_ge(order, ready[u])
                        for g in range(G):
                            last = dve.scalar_tensor_tensor(index[:, u, g:g + 1], to_spare[:, u, g:g + 1],
                                                            repeated[:, u, g:g + 1], cols[:, u, g:g + 1, 0],
                                                            ALU.mult, ALU.add)
                        last.then_inc(index_ready, 1)

                    ready = {}
                    for u in range(SLOTS):
                        src = cols[:, u, :, 0]
                        dve.wait_ge(cols_in[u], i * 16 + 16)
                        seq.done(dve.tensor_scalar(dst_in[:, u, :], cols[:, u, :, 1], keep.block_base[:, bass.ds(in_block[u], 1)],
                                                   None, ALU.subtract))
                        dst_done = seq.now
                        dve.wait_ge(merged, i * SLOTS + u + 1)
                        dve.wait_ge(rows_in[u], i * 16 + 16)
                        dve.tensor_tensor(same[:, u, :, :], rows[:, u, :].rearrange("p (q g) -> p g q", g=G),
                                          spread(src.rearrange("p (g n) -> p g n", n=1), every),
                                          ALU.is_equal).then_inc(masks_ready, 1)
                        seq.done(dve.tensor_scalar(to_spare[:, u, :], src, -1.0, keep.spare_row[:, 0:1], ALU.mult, ALU.add))
                        if u:
                            write_index(u - 1)
                        dve.wait_ge(order, dst_done)
                        dve.tensor_tensor(is_dst[:, u, :, :], spread(keep.lane[:, :].rearrange("p (g n) -> p g n", g=1), every),
                                          spread(dst_in[:, u, :].rearrange("p (g n) -> p g n", n=1), every),
                                          ALU.is_equal).then_inc(masks_ready, 1)
                        dve.wait_ge(masks_ready, (i * SLOTS + u) * 2 + 1)
                        dve.sem_inc(turn, 1)
                        for g in range(G):
                            seq.done(dve.tensor_tensor_reduce(out=junk[:, u % 2, g, :], in0=same[:, u, g, :], in1=keep.below[:, :],
                                                              scale=1.0, scalar=0.0, op0=ALU.mult, op1=ALU.max,
                                                              accum_out=repeated[:, u, g:g + 1]))
                        ready[u] = seq.now
                        if u:
                            dve.wait_ge(index_ready, i * SLOTS + u)
                            dve.sem_inc(lists_free, 1)
                    write_index(SLOTS - 1)
                    dve.wait_ge(index_ready, i * SLOTS + SLOTS)
                    dve.sem_inc(lists_free, 1)
                    seq.leave(ROUNDS)
                fold_vector(dve)

            @block.tensor
            def _(pe):
                pe.sem_inc(merged, SLOTS)
                regs = registers(pe, "scat_pe", SLOTS)
                with pe.Fori(0, ROUNDS) as i:
                    in_block = step_values(pe, regs, keep.step_block, i, NB - 1)

                    def merge_edges(u):
                        pe.wait_ge(masks_ready, (i * SLOTS + u) * 2 + 2)
                        for g in range(G):
                            last = pe.matmul(merge_ps[u % 2][:, g, :], is_dst[:, u, g, :], same[:, u, g, :], start=True, stop=True)
                        last.then_inc(merged, 1)

                    def sum_values(u):
                        pe.wait_ge(merge_ready, i * SLOTS + u + 1)
                        for g in range(G):
                            last = pe.matmul(values_ps[u % 2][:, g, :], merge[:, u, g, :], keep.xn[:, bass.ds(in_block[u], 1), 0:D],
                                             start=True, stop=True)
                        last.then_inc(summed, 1)

                    merge_edges(0)
                    for u in range(1, SLOTS):
                        merge_edges(u)
                        sum_values(u - 1)
                    sum_values(SLOTS - 1)
                fold_tensor(pe)

            @block.scalar
            def _(act):
                with act.Fori(0, ROUNDS) as i:

                    def copy_merge(u):
                        act.wait_ge(merged, i * SLOTS + u + 1 + SLOTS)
                        act.copy(merge[:, u, :, :], merge_ps[u % 2][:, :, :]).then_inc(merge_ready, 1)

                    def copy_values(u):
                        act.wait_ge(summed, i * SLOTS + u + 1)
                        for g in range(G):
                            act.wait_ge(keep.added[u * G + g], i * 16 + 16)
                        act.copy(values[:, u, :, :], values_ps[u % 2][:, :, :]).then_inc(values_ready, 1)

                    copy_merge(0)
                    for u in range(1, SLOTS):
                        copy_merge(u)
                        copy_values(u - 1)
                    copy_values(SLOTS - 1)
                fold_scalar(act)

            @block.gpsimd
            def _(pool):
                with pool.Fori(0, ROUNDS) as i:
                    for u in range(SLOTS):
                        pool.wait_ge(index_ready, i * SLOTS + u + 1)
                        pool.wait_ge(values_ready, i * SLOTS + u + 1)
                        pool.sem_inc(turn, 1)
                        for g in range(G):
                            k = u * G + g
                            pool.wait_ge(keep.added[(k - SUMS) % LOTS], i * 16 + (16 if u < LAG else 32))
                            pool.sem_inc(turn, 1)
                            pool.indirect_dma_start(
                                out=keep.partial[k % SUMS], out_offset=bass.IndirectOffsetOnAxis(ap=index[:, u, g:g + 1], axis=0),
                                in_=values[:, u, g, :], in_offset=None, compute_op=ALU.add).then_inc(keep.added[k], 16)
                for k in range(LOTS):
                    pool.wait_ge(keep.added[k], 16 * (ROUNDS + 1))


T_H, T_X, T_R = 0, 4, 8
T_H1, T_W, T_X1, T_R1, T_Z = 10, 14, 16, 20, 22
T_W_LAST, T_Z_LAST = 10, 12
TURNS = 16
C_G, C_E = 0, SB
C_G1, C_E6, C_BO, C_E7, C_P = (n * SB for n in (7, 8, 9, 10, 11))
C_E6_LAST, C_BO_LAST, C_E7_LAST, C_P_LAST = (n * SB for n in (7, 8, 9, 10))
SUMS_C = 12 * SB


def turn_blocks(j):
    return range(2 * j, min(2 * j + 2, SB))


def mixture(nc, io, keep):
    with ExitStack() as ctx:
        s = Scope(nc, ctx, "mix")
        parts = s.sb("parts", [P, SUMS - 1, 3, D])
        h = s.sb("h", [P, SB, D])
        normed = [h, s.sb("normed1", [P, SB, D])]
        at = s.sb("at", [P, KD, TOK])
        xt = s.sb("xt", [P, KD, TOK])
        xt_parts = [s.sb(f"xt_{n}", [P, KD, TOK]) for n in ("high", "low")]
        hidden = s.sb("hidden", [P, KD, TOK])
        h1_parts = [s.sb(f"h1_{n}", [P, KD, TOK]) for n in ("high", "low")]
        h2_parts = [s.sb(f"h2_{n}", [P, KD, TOK]) for n in ("high", "low")]
        weights = s.sb("weights", [P, 3, KD, D])
        weights_parts = [s.sb(f"weights_{n}", [P, 2, 3, KD, D]) for n in ("high", "low")]
        rows = s.sb("rows", [P, SB, GROW])
        residual = s.sb("residual", [P, SB, ROW])
        stats = [s.sb(f"stats{n}", [P, SB, 6]) for n in range(2)]
        aggr = [s.sb(f"aggr{n}", [P, SB, 2]) for n in range(2)]
        std = [s.sb(f"std{n}", [P, SB]) for n in range(2)]
        rstd = [s.sb(f"rstd{n}", [P, SB]) for n in range(2)]
        eps = s.sb("eps", [P, 1])
        logits = s.sb("logits", [P, SB, X0])
        gate = s.sb("gate", [P, SB, X0])
        top = s.sb("top", [P, SB])
        gate_t = s.sb("gate_t", [X0, SB, P])
        a2_top = s.sb("a2_top", [P, HEADS])
        a2_new = s.sb("a2_new", [P, HEADS])
        shift = s.sb("shift", [P, NB, HEADS])
        turn = [s.ps(f"turn{n}", [P, 512]) for n in range(2)]
        wide = [s.ps(f"wide{n}", [P, 512]) for n in range(3)]
        sums = [s.ps(f"sums{n}", [P, 512]) for n in range(3)]
        wide_of = ((1, 2, 0, 1), (0, 1, 2, 0))

        h_in = s.sem("h_in")
        parts_in = s.sem("parts_in")
        h_ready = s.sem("h_ready")
        weights_in = s.sems("weights_in", 3)
        weights_high = s.sem("weights_high")
        weights_low = s.sem("weights_low")
        turn_full = s.sem("turn_full")
        turn_free = s.sems("turn_free", 2)
        wide_full = s.sem("wide_full")
        sums_full = s.sem("sums_full")
        sums_read = s.sem("sums_read")
        aggr_ready = s.sems("aggr_ready", 2)
        std_ready = s.sems("std_ready", 2)
        normed_ready = s.sems("normed_ready", 2)
        exp_in = s.sem("exp_in")
        exp_out = s.sem("exp_out")
        gate_ready = s.sem("gate_ready")
        rows_ready = s.sem("rows_ready")
        rows_out = s.sem("rows_out")
        node_ready = s.sem("node_ready")
        at_ready = s.sem("at_ready")
        xt_ready = s.sem("xt_ready")
        xt_high = s.sem("xt_high")
        xt_low = s.sem("xt_low")
        h1_ready = s.sem("h1_ready")
        h1_high = s.sem("h1_high")
        h1_low = s.sem("h1_low")
        h2_ready = s.sem("h2_ready")
        h2_high = s.sem("h2_high")
        h2_low = s.sem("h2_low")
        gate_t_ready = s.sem("gate_t_ready")
        a1_taken = s.sem("a1_taken")
        order = s.sem("order")
        pause = s.sem("pause")

        def unused(half, c):
            return half + c // 2 + 1

        def used(half, c):
            return half + c // 2 + 2

        def full(half, c):
            return 2 * half + c + 2

        def sums_unused(half, c0, n):
            return 2 * half + c0 + max(n - 3 + 1, 0) + 1

        T, S = TURNS // 2, SUMS_C // 2

        with nc.Block() as block:

            @block.sync
            def _(sp):
                sp.sem_inc(rows_out, 32)

                rows_of = lambda k, i, b, n: keep.partial[k][bass.ds(i * TOK + b * P, n * P), :].rearrange("(b p) d -> p b d", p=P)

                def load_h(i):
                    sp.dma_start(h[:, :, :], rows_of(0, i, 0, SB)).then_inc(h_in, 16)

                def load_parts(i, j, n, loads):
                    if loads is not None:
                        sp.wait_ge(parts_in, loads * 16 * (SUMS - 1))
                        sp.sem_inc(pause, 1)
                    for k in range(1, SUMS):
                        sp.dma_start(parts[:, k - 1, 0:2, :] if n == 2 else parts[:, k - 1, 2:3, :],
                                     rows_of(k, i, j * 2, n)).then_inc(parts_in, 16)

                def load_weights(expert, splits):
                    for n, w in enumerate((io["L0_ffn_W1"], io["L0_ffn_W2"], io["L0_ffn_Wo"])):
                        if splits is not None:
                            sp.wait_ge(weights_low, splits + n)
                            sp.sem_inc(pause, 1)
                        sp.dma_start(weights[:, n, :, :], w[bass.ds(expert, 1), :, :].rearrange("e (k p) h -> p (e k) h", p=P)
                                     ).then_inc(weights_in[n], 16)

                def store_rows(i):
                    sp.wait_ge(rows_ready, (i + 1) * 2 * SB)
                    sp.sem_inc(pause, 1)
                    sp.dma_start(keep.rows_dram[bass.ds(i * TOK, TOK), :].rearrange("(b p) d -> p b d", p=P),
                                 rows[:, :, :]).then_inc(rows_out, 16)
                    sp.dma_start(keep.residual_dram[bass.ds(i * TOK, TOK), :].rearrange("(b p) d -> p b d", p=P),
                                 residual[:, :, HEADS:ROW]).then_inc(rows_out, 16)

                def super_block(i, first=False, last=False):
                    if not last:
                        sp.wait_ge(turn_full, full(i * T, T_X + 3))
                        sp.wait_ge(h_ready, (i + 1) * (SUMS - 1) * SB)
                        sp.sem_inc(pause, 1)
                        load_h(i + 1)
                        load_parts(i + 1, X0 // 2 - 1, 1, (i + 1) * 4)
                    with sp.Fori(0, X0 // 2 - 1) as j:
                        if not last:
                            sp.wait_ge(h_ready, ((i + 1) * SB + 1 + j * 2) * (SUMS - 1))
                            load_parts(i + 1, j, 2, (i + 1) * 4 + j + 1)
                        for e in range(2):
                            load_weights(j * 2 + 2 + e, (i * X0 + j * 2 + e) * 3 + 4)
                    if not last:
                        load_weights(0, (i * X0 + X0 - 2) * 3 + 4)
                    if not first:
                        store_rows(i - 1)
                    if not last:
                        load_weights(1, (i * X0 + X0 - 1) * 3 + 4)

                load_h(0)
                load_parts(0, X0 // 2 - 1, 1, None)
                load_parts(0, 0, 2, 1)
                load_weights(0, None)
                for j in range(1, X0 // 2 - 1):
                    sp.wait_ge(h_ready, (1 + j * 2) * (SUMS - 1))
                    load_parts(0, j, 2, j + 1)
                load_weights(1, 1)
                super_block(0, first=True)
                with sp.Fori(1, NSB - 1) as i:
                    super_block(i)
                super_block(NSB - 1, last=True)
                store_rows(NSB - 1)
                sp.wait_ge(rows_out, 32 * (NSB + 1))

            @block.gpsimd
            def _(pool):
                low = lambda part, whole, high: pool.tensor_tensor(part.bitcast(F32R), whole, high, ALU.subtract)

                def split_weights(q, n, slot, nth):
                    pool.wait_ge(weights_high, nth + 1)
                    high, part = (weights_parts[m][:, slot, n, :, :] for m in range(2))
                    low(part, weights[:, n, :, :], high).then_inc(weights_low, 1)

                def split_h1(q):
                    for part in range(2):
                        for k in range(KD):
                            cols = slice(part * HALF, (part + 1) * HALF)
                            pool.wait_ge(h1_high, q * 4 + part * 2 + k + 1)
                            low(h1_parts[1][:, k, cols], hidden[:, k, cols], h1_parts[0][:, k, cols]).then_inc(h1_low, 1)

                def split_input(n):
                    for j in range(4):
                        cols = slice(2 * j * P, 2 * j * P + len(turn_blocks(j)) * P)
                        pool.wait_ge(xt_high, n * 4 + j + 1)
                        low(xt_parts[1][:, :, cols], xt[:, :, cols], xt_parts[0][:, :, cols]).then_inc(xt_low, 1)

                def add_parts(n, j, blocks, loads, done):
                    pool.wait_ge(h_in, (n + 1) * 16)
                    pool.wait_ge(parts_in, (n * 4 + loads) * 16 * (SUMS - 1))
                    pool.sem_inc(pause, 1)
                    for k in range(SUMS - 1):
                        here = bass.ds(j * 2, blocks)
                        if k:
                            pool.wait_ge(h_ready, (n * SB + done) * (SUMS - 1) + k * blocks)
                            pool.sem_inc(pause, 1)
                        part = parts[:, k, 0:2, :] if blocks == 2 else parts[:, k, 2:3, :]
                        pool.tensor_tensor(h[:, here, :], h[:, here, :], part, ALU.add).then_inc(h_ready, blocks)

                def split_next_weights(q, e):
                    for m, (n, slot) in enumerate(((1, 1 - e), (2, 1 - e), (0, e))):
                        split_weights(q, n, slot, q * 3 + 4 + m)

                def super_block(i, last=False):
                    if not last:
                        add_parts(i + 1, X0 // 2 - 1, 1, 1, 0)
                    pool.sem_inc(pause, 1)
                    with pool.Fori(0, X0 // 2 - 1) as j:
                        for e in range(2):
                            q = i * X0 + j * 2 + e
                            split_next_weights(q, e)
                            split_h1(q + 1)
                            if e == 0 and not last:
                                add_parts(i + 1, j, 2, j + 2, 1 + j * 2)
                    for e in range(2):
                        q = i * X0 + X0 - 2 + e
                        if last and e:
                            continue
                        if e:
                            split_input(i + 1)
                        if last:
                            for m, n in enumerate((1, 2)):
                                split_weights(q, n, 1, q * 3 + 4 + m)
                        else:
                            split_next_weights(q, e)
                        split_h1(q + 1)

                add_parts(0, X0 // 2 - 1, 1, 1, 0)
                for j in range(X0 // 2 - 1):
                    add_parts(0, j, 2, j + 2, 1 + j * 2)
                for m, (n, slot) in enumerate(((0, 0), (1, 0), (2, 0), (0, 1))):
                    split_weights(0, n, slot, m)
                split_input(0)
                split_h1(0)
                with pool.Fori(0, NSB - 1) as i:
                    super_block(i)
                super_block(NSB - 1, last=True)
                pool.wait_ge(a1_taken, NSB + 1)
                pool.partition_all_reduce(keep.a2_bound[:, :], a2_top[:, :], P, bass.bass_isa.ReduceOp.max).then_inc(node_ready, 1)
                pool.wait_ge(node_ready, 1)

            @block.tensor
            def _(pe):
                pe.sem_inc(turn_full, 1)
                pe.sem_inc(sums_full, 1)

                def turn_over(half, c, tile, ready, count):
                    for j in range(4):
                        for b in turn_blocks(j):
                            pe.wait_ge(ready, count(b))
                            if b == 2 * j:
                                pe.wait_ge(turn_free[(c + j) % 2], unused(half, c + j))
                            for k in range(KD):
                                at0 = (k * 2 + b - 2 * j) * P
                                last = pe.transpose(turn[(c + j) % 2][:, at0:at0 + P], tile[:, b, k * P:(k + 1) * P], keep.ident[:, :])
                        last.then_inc(turn_full, 1)

                def sum_tile(half, c0, n, left, right, width=D):
                    pe.wait_ge(sums_read, sums_unused(half, c0, n))
                    for k in range(KD):
                        last = pe.matmul(sums[n % 3][:, 0:width], left(k), right(k), start=(k == 0), stop=(k == KD - 1))
                    last.then_inc(sums_full, 1)

                def gin(n, t, half_t, c, half_c, turned):
                    turn_over(half_t, t, h, h_ready, lambda b: (n * SB + (1 if b == SB - 1 else 3 + b // 2 * 2)) * (SUMS - 1))
                    for b in range(SB):
                        pe.wait_ge(at_ready, turned + b // 2 + 1)
                        sum_tile(half_c, c, b, lambda k: at[:, k, b * P:(b + 1) * P], lambda k: keep.w12[:, k, :])

                def gate_logits(n, half, tx, tr):
                    turn_over(half, tx, normed[0], normed_ready[0], lambda b: n * SB + b + 1)
                    for part, blocks in enumerate((range(0, 4), range(4, SB))):
                        t = tr + part
                        pe.wait_ge(turn_free[t % 2], unused(half, t))
                        for b in blocks:
                            pe.wait_ge(xt_ready, n * 4 + b // 2 + 1)
                            for k in range(KD):
                                last = pe.matmul(turn[t % 2][:, b * X0:(b + 1) * X0], xt[:, k, b * P:(b + 1) * P], keep.wr[:, k, :],
                                                 start=(k == 0), stop=(k == KD - 1))
                        last.then_inc(turn_full, 1)

                def product(out, left, right):
                    terms = [(l, r, k) for k in range(KD) for l, r in ((0, 0), (0, 1), (1, 0))]
                    for n, (l, r, k) in enumerate(terms):
                        last = pe.matmul(out, left(l, k).bitcast(F32R), right(r, k).bitcast(F32R),
                                         start=(n == 0), stop=(n == len(terms) - 1))
                    return last

                def layer(q, n, slot):
                    source = (xt_parts, h1_parts)[n]
                    pe.wait_ge(weights_low, q * 3 + (1 if n == 0 else 2))
                    for part in range(2):
                        if n == 1:
                            pe.wait_ge(h1_low, q * 4 + 2 * part + 2)
                        for m in range(KD):
                            t = part * 2 + m
                            if n == 0 and t < 3:
                                pe.wait_ge(h2_ready, q * 4 + t + 2)
                            elif n == 0:
                                pe.wait_ge(h1_ready, q * 4 + 1)
                            elif t < 3:
                                pe.wait_ge(h1_ready, q * 4 + 4)
                            else:
                                pe.wait_ge(h2_ready, q * 4 + 1 + 4)
                            product(wide[wide_of[n][t]][:, 0:HALF], lambda l, k: weights_parts[l][:, slot, n, k, m * P:(m + 1) * P],
                                    lambda r, k: source[r][:, k, part * HALF:(part + 1) * HALF]).then_inc(wide_full, 1)

                def sums_of_expert(q, slot, half, c):
                    pe.wait_ge(weights_low, q * 3 + 3)
                    for b in range(SB):
                        pe.wait_ge(h2_low, q * 4 + (2 if (b + 1) * P <= HALF else 4) + 4)
                        pe.wait_ge(sums_read, sums_unused(half, c, b))
                        product(sums[b % 3][:, 0:D], lambda l, k: h2_parts[l][:, k, b * P:(b + 1) * P],
                                lambda r, k: weights_parts[r][:, slot, 2, k, :]).then_inc(sums_full, 1)

                def last_biases(i, half_t, t0, half_c, c):
                    for part, blocks in enumerate((range(0, 4), range(4, SB))):
                        t = t0 + part
                        pe.wait_ge(gate_ready, i + 1)
                        pe.wait_ge(turn_free[t % 2], unused(half_t, t))
                        for n, b in enumerate(blocks):
                            last = pe.transpose(turn[t % 2][0:X0, n * P:(n + 1) * P], gate[:, b, :], keep.ident[:, :])
                        last.then_inc(turn_full, 1)
                    for b in range(SB):
                        pe.wait_ge(gate_t_ready, i * 2 + b // 4 + 1)
                        pe.wait_ge(sums_read, sums_unused(half_c, c - SB, b + SB))
                        pe.matmul(sums[(b + SB) % 3][:, 0:D], gate_t[:, b, :], keep.bo[:, :], start=True, stop=True).then_inc(sums_full, 1)

                def projections(i, half_t, t, half_c, c, turned):
                    turn_over(half_t, t, normed[1], normed_ready[1], lambda b: i * SB + b + 1)
                    for b in range(SB):
                        pe.wait_ge(at_ready, turned + b // 2 + 1)
                        for n, (c0, c1) in enumerate(((0, GROW), (GROW, PROJ))):
                            sum_tile(half_c, c, 2 * b + n, lambda k: at[:, k, b * P:(b + 1) * P],
                                     lambda k: keep.proj[:, k, c0:c1], width=c1 - c0)

                def super_block(i, last=False):
                    with pe.Fori(0, X0 // 2 - 1) as j:
                        for e in range(2):
                            q = i * X0 + j * 2 + e
                            layer(q, 1, e)
                            layer(q + 1, 0, 1 - e)
                            sums_of_expert(q, e, i * S + j * SB, C_E + e * SB)
                    if not last:
                        gin(i + 1, T_H1, i * T, C_G1, i * S, i * 8 + 4)
                    q = i * X0 + X0 - 2
                    layer(q, 1, 0)
                    layer(q + 1, 0, 1)
                    sums_of_expert(q, 0, i * S, C_E6_LAST if last else C_E6)
                    last_biases(i, i * T, T_W_LAST if last else T_W, i * S, C_BO_LAST if last else C_BO)
                    layer(q + 1, 1, 1)
                    if not last:
                        gate_logits(i + 1, i * T, T_X1, T_R1)
                    sums_of_expert(q + 1, 1, i * S, C_E7_LAST if last else C_E7)
                    if not last:
                        first_layer(i + 1)
                    projections(i, i * T, T_Z_LAST if last else T_Z, i * S, C_P_LAST if last else C_P, i * 8 + (4 if last else 8))

                def first_layer(i):
                    pe.wait_ge(xt_low, i * 4 + 4)
                    layer(i * X0, 0, 0)

                gin(0, T_H, 0, C_G, 0, 0)
                gate_logits(0, 0, T_X, T_R)
                first_layer(0)
                with pe.Fori(0, NSB - 1) as i:
                    super_block(i)
                super_block(NSB - 1, last=True)

            @block.scalar
            def _(act):
                act.sem_inc(a1_taken, 1)
                act.sem_inc(h2_ready, 4)

                def copy_turns(half, c, tile, ready, before):
                    for j in range(4):
                        t = c + j
                        width = len(turn_blocks(j)) * P
                        act.wait_ge(turn_full, full(half, t))
                        act.copy(tile[:, :, 2 * j * P:2 * j * P + width],
                                 turn[t % 2][:, :].rearrange("p (k n) -> p k n", k=KD)[:, :, 0:width]).then_inc(ready, 1)
                        act.wait_ge(ready, before + j + 1)
                        act.sem_inc(turn_free[t % 2], 1)

                def roots(nth, n):
                    act.wait_ge(aggr_ready[nth], n + 1)
                    act.activation(std[nth][:, :], aggr[nth][:, :, 1], ACT.Sqrt, bias=eps[:, 0:1]).then_inc(std_ready[nth], 1)

                def exponentials(n):
                    act.wait_ge(exp_in, n + 1)
                    act.activation(gate[:, :, :], logits[:, :, :], ACT.Exp).then_inc(exp_out, 1)

                def relu(q, n, cols, tiles=range(4)):
                    ready = (h1_ready, h2_ready)[n]
                    for part in range(2):
                        for m in range(KD):
                            t = part * 2 + m
                            if t not in tiles:
                                continue
                            act.wait_ge(wide_full, q * 8 + n * 4 + t + 1)
                            if n == 0:
                                act.wait_ge(h2_low, q * 4 + t + 1)
                            act.sem_inc(pause, 1)
                            act.activation(hidden[:, m, part * HALF:(part + 1) * HALF], wide[wide_of[n][t]][:, 0:HALF], ACT.Relu,
                                           bias=keep.bn[:, 2 * n + 1, bass.ds(cols + m, 1)],
                                           scale=keep.bn[:, 2 * n, bass.ds(cols + m, 1)]).then_inc(ready, 1)

                def copy_gate(i, half, c):
                    for part, n in enumerate((4, SB - 4)):
                        t = c + part
                        act.wait_ge(turn_full, full(half, t))
                        act.copy(gate_t[:, 4 * part:4 * part + n, :], turn[t % 2][0:X0, 0:n * P].rearrange("p (b n) -> p b n", n=P))\
                           .then_inc(gate_t_ready, 1)
                        act.wait_ge(gate_t_ready, i * 2 + part + 1)
                        act.sem_inc(turn_free[t % 2], 1)

                def copy_rows(i, half, c0):
                    act.wait_ge(rows_out, (i + 1) * 32)
                    act.wait_ge(a1_taken, i + 1)
                    for b in range(SB):
                        for n in range(2):
                            c = c0 + 2 * b + n
                            act.wait_ge(sums_full, full(half, c))
                            if n == 0:
                                act.copy(rows[:, b, :], sums[(2 * b + n) % 3][:, 0:GROW]).then_inc(rows_ready, 1)
                            else:
                                act.copy(residual[:, b, :], sums[(2 * b + n) % 3][:, 0:ROW]).then_inc(rows_ready, 1)
                            act.wait_ge(rows_ready, i * 2 * SB + 2 * b + n + 1)
                            act.sem_inc(sums_read, 1)

                def super_block(i, last=False):
                    with act.Fori(0, X0 // 2 - 1) as j:
                        for e in range(2):
                            q = i * X0 + j * 2 + e
                            relu(q, 1, j * 4 + e * 2)
                            relu(q + 1, 0, j * 4 + e * 2 + 2)
                    if not last:
                        copy_turns(i * T, T_H1, at, at_ready, i * 8 + 4)
                    q = i * X0 + X0 - 2
                    relu(q, 1, 2 * X0 - 4)
                    if not last:
                        roots(0, i + 1)
                    relu(q + 1, 0, 2 * X0 - 2)
                    copy_gate(i, i * T, T_W_LAST if last else T_W)
                    relu(q + 1, 1, 2 * X0 - 2)
                    if not last:
                        copy_turns(i * T, T_X1, xt, xt_ready, (i + 1) * 4)
                        relu(q + 2, 0, 0, range(2))
                    roots(1, i)
                    if not last:
                        relu(q + 2, 0, 0, range(2, 4))
                    copy_turns(i * T, T_Z_LAST if last else T_Z, at, at_ready, i * 8 + (4 if last else 8))
                    if not last:
                        exponentials(i + 1)
                    copy_rows(i, i * S, C_P_LAST if last else C_P)

                copy_turns(0, T_H, at, at_ready, 0)
                roots(0, 0)
                copy_turns(0, T_X, xt, xt_ready, 0)
                relu(0, 0, 0)
                exponentials(0)
                with act.Fori(0, NSB - 1) as i:
                    super_block(i)
                super_block(NSB - 1, last=True)

            @block.vector
            def _(dve):
                seq = Tally(order)

                def then(instruction):
                    seq.done(instruction)
                    dve.wait_ge(order, seq.now)

                dve.sem_inc(h2_low, 4)
                dve.sem_inc(sums_read, 1)
                for n in range(2):
                    dve.sem_inc(turn_free[n], 1)
                then(dve.memset(eps[:, :], 1e-5))
                then(dve.memset(a2_top[:, :], -3e38))

                def node(i, b):
                    return bass.ds(i * SB + b, 1)

                def add_sum(i, b, half, c, tile):
                    x = keep.x[:, node(i, b), :]
                    dve.wait_ge(sums_full, full(half, c))
                    dve.tensor_tensor(x, sums[tile][:, 0:D].rearrange("p (b d) -> p b d", b=1), x, ALU.add)\
                       .then_inc(sums_read, 1)

                def norm_stats(nth, i, half, c):
                    for b in range(SB):
                        dve.wait_ge(sums_read, 2 * half + c + b + 2)
                        dve.sem_inc(pause, 1)
                        seq.done(dve.bn_stats(stats[nth][:, b, :], keep.x[:, node(i, b), :]))
                    dve.wait_ge(order, seq.now)
                    dve.sem_inc(pause, 1)
                    for b in range(SB):
                        last = dve.bn_aggr(aggr[nth][:, b, :], stats[nth][:, b, :])
                    last.then_inc(aggr_ready[nth], 1)

                def normalize(nth, i):
                    dve.wait_ge(std_ready[nth], i + 1)
                    then(dve.reciprocal(rstd[nth][:, :], std[nth][:, :]))
                    for b in range(SB):
                        dve.tensor_scalar(normed[nth][:, b, :], keep.x[:, node(i, b), :], aggr[nth][:, b, 0:1], rstd[nth][:, b:b + 1],
                                          ALU.subtract, ALU.mult).then_inc(normed_ready[nth], 1)

                def high(part, whole):
                    return dve.tensor_copy(part.bitcast(F32R), whole)

                def split_weights(q, n, slot):
                    dve.wait_ge(weights_in[n], q * 16 + 16)
                    dve.sem_inc(pause, 1)
                    high(weights_parts[0][:, slot, n, :, :], weights[:, n, :, :]).then_inc(weights_high, 1)

                def split_next_weights(q, e):
                    split_weights(q + 1, 1, 1 - e)
                    split_weights(q + 1, 2, 1 - e)
                    split_weights(q + 2, 0, e)

                def split_h1(q, tiles=range(4)):
                    for part in range(2):
                        for k in range(KD):
                            if part * 2 + k not in tiles:
                                continue
                            cols = slice(part * HALF, (part + 1) * HALF)
                            dve.wait_ge(h1_ready, q * 4 + part * 2 + k + 1)
                            dve.sem_inc(pause, 1)
                            high(h1_parts[0][:, k, cols], hidden[:, k, cols]).then_inc(h1_high, 1)

                def split_h2(q):
                    for part in range(2):
                        cols = slice(part * HALF, (part + 1) * HALF)
                        for k in range(KD):
                            dve.wait_ge(h2_ready, q * 4 + part * 2 + k + 1 + 4)
                            dve.sem_inc(pause, 1)
                            high(h2_parts[0][:, k, cols], hidden[:, k, cols]).then_inc(h2_high, 1)
                        for k in range(KD):
                            dve.wait_ge(h2_high, q * 4 + part * 2 + k + 1)
                            dve.tensor_tensor(h2_parts[1][:, k, cols].bitcast(F32R), hidden[:, k, cols], h2_parts[0][:, k, cols], ALU.subtract).then_inc(h2_low, 1)

                def split_input(n):
                    for j in range(4):
                        cols = slice(2 * j * P, 2 * j * P + len(turn_blocks(j)) * P)
                        dve.wait_ge(xt_ready, n * 4 + j + 1)
                        dve.sem_inc(pause, 1)
                        high(xt_parts[0][:, :, cols], xt[:, :, cols]).then_inc(xt_high, 1)

                def gin(i, half, c):
                    for b in range(SB):
                        add_sum(i, b, half, c + b, b % 3)
                    norm_stats(0, i, half, c)

                every = [P, SB, X0]
                wide_col = lambda ap: spread(ap.rearrange("p (b e) -> p b e", e=1), every)

                def gate_shifted(i, half, t0):
                    for part, (b0, b1) in enumerate(((0, 4), (4, SB))):
                        t = t0 + part
                        dve.wait_ge(turn_full, full(half, t))
                        dve.tensor_tensor(logits[:, b0:b1, :], turn[t % 2][:, b0 * X0:b1 * X0].rearrange("p (b e) -> p b e", e=X0),
                                          spread(keep.br[:, :].rearrange("p (b e) -> p b e", b=1), [P, b1 - b0, X0]),
                                          ALU.add).then_inc(turn_free[t % 2], 1)
                    for part in range(2):
                        dve.wait_ge(turn_free[(t0 + part) % 2], used(half, t0 + part))
                    then(dve.tensor_reduce(top[:, :], logits[:, :, :], AX.X, ALU.max))
                    dve.tensor_tensor(logits[:, :, :], logits[:, :, :], wide_col(top[:, :]), ALU.subtract).then_inc(exp_in, 1)

                def gate_softmax(i):
                    dve.wait_ge(exp_out, i + 1)
                    then(dve.tensor_reduce(top[:, :], gate[:, :, :], AX.X, ALU.add))
                    then(dve.reciprocal(top[:, :], top[:, :]))
                    dve.tensor_tensor(gate[:, :, :], gate[:, :, :], wide_col(top[:, :]), ALU.mult).then_inc(gate_ready, 1)
                    dve.wait_ge(gate_ready, i + 1)
                    dve.sem_inc(pause, 1)

                def add_expert(i, j, e, half, c0, blocks=range(SB)):
                    for b in blocks:
                        c = c0 + b
                        x = keep.x[:, node(i, b), :]
                        dve.wait_ge(sums_full, full(half, c))
                        dve.scalar_tensor_tensor(x, sums[b % 3][:, 0:D].rearrange("p (b d) -> p b d", b=1),
                                                 gate[:, b, bass.ds(j * 2 + e, 1)], x, ALU.mult, ALU.add).then_inc(sums_read, 1)

                def take_a(i):
                    dve.wait_ge(rows_ready, (i + 1) * 2 * SB)
                    then(dve.tensor_reduce(a2_new[:, :], rows[:, :, D:ROW].rearrange("p b h -> p h b"), AX.X, ALU.max))
                    then(dve.tensor_tensor(a2_top[:, :], a2_top[:, :], a2_new[:, :], ALU.max))
                    dve.sem_inc(pause, 1)
                    dve.tensor_copy(keep.node[:, bass.ds(i * SB, SB), 0:HEADS], residual[:, :, 0:HEADS]).then_inc(a1_taken, 1)

                def super_block(i, last=False):
                    dve.sem_inc(pause, 1)
                    with dve.Fori(0, X0 // 2 - 1) as j:
                        for e in range(2):
                            q = i * X0 + j * 2 + e
                            split_h2(q)
                            split_next_weights(q, e)
                            split_h1(q + 1, range(3))
                            add_expert(i, j, e, i * S + j * SB, C_E + e * SB, range(1))
                            split_h1(q + 1, range(3, 4))
                            add_expert(i, j, e, i * S + j * SB, C_E + e * SB, range(1, SB))
                    if not last:
                        gin(i + 1, i * S, C_G1)
                    j, q = X0 // 2 - 1, i * X0 + X0 - 2
                    split_h2(q)
                    if last:
                        for n in (1, 2):
                            split_weights(q + 1, n, 1)
                    else:
                        split_next_weights(q, 0)
                    c = C_E6_LAST if last else C_E6
                    split_h1(q + 1, range(3))
                    add_expert(i, j, 0, i * S, c, range(1))
                    split_h1(q + 1, range(3, 4))
                    add_expert(i, j, 0, i * S, c, range(1, SB))
                    c = C_BO_LAST if last else C_BO
                    for b in range(SB):
                        add_sum(i, b, i * S, c + b, (b + SB) % 3)
                    if not last:
                        normalize(0, i + 1)
                    split_h2(q + 1)
                    if not last:
                        split_input(i + 1)
                        split_next_weights(q + 1, 1)
                    c = C_E7_LAST if last else C_E7
                    add_expert(i, j, 1, i * S, c)
                    norm_stats(1, i, i * S, c)
                    normalize(1, i)
                    if not last:
                        gate_shifted(i + 1, i * T, T_R1)
                        split_h1((i + 1) * X0)
                        gate_softmax(i + 1)
                    take_a(i)

                gin(0, 0, C_G)
                for n in range(3):
                    split_weights(0, n, 0)
                split_weights(1, 0, 1)
                normalize(0, 0)
                split_input(0)
                gate_shifted(0, 0, T_R)
                split_h1(0)
                gate_softmax(0)
                with dve.Fori(0, NSB - 1) as i:
                    seq.enter(i, DVE_MIX)
                    super_block(i)
                    seq.leave(NSB - 1)
                super_block(NSB - 1, last=True)
                dve.wait_ge(a1_taken, NSB + 1)
                dve.wait_ge(node_ready, 1)
                a1, low = keep.node[:, :, 0:HEADS], keep.node[:, :, HEADS:2 * HEADS]
                then(dve.tensor_tensor(shift[:, :, :], a1, spread(keep.a2_bound[:, :].rearrange("p (b h) -> p b h", b=1), [P, NB, HEADS]), ALU.add))
                then(dve.scalar_tensor_tensor(shift[:, :, :], shift[:, :, :], SLOPE, shift[:, :, :], ALU.mult, ALU.max))
                then(dve.scalar_tensor_tensor(low, a1, SLOPE, shift[:, :, :], ALU.mult, ALU.subtract))
                then(dve.tensor_tensor(a1, a1, shift[:, :, :], ALU.subtract))


def pipeline(eng, stages, registers_of=None):
    def run(i, us, first=False, last=False):
        for u in us:
            for stage, lag in stages:
                if (u - lag >= 0 or not first) and (u - lag < 0 or not last):
                    stage(i, u - lag)

    if registers_of:
        registers_of(0)
    run(0, range(ASLOTS), first=True)
    with eng.Fori(1, AROUNDS) as i:
        if registers_of:
            registers_of(i)
        run(i, range(ASLOTS))
    if registers_of:
        registers_of(AROUNDS)
    run(AROUNDS, range(max(lag for _, lag in stages)), last=True)


def attend(nc, io, keep):
    with ExitStack() as ctx:
        s = Scope(nc, ctx, "att")
        cols = s.sb("cols", [P, ASLOTS, G, 2], I32)
        rows = s.sb("rows", [P, MASKS, STEP], I32)
        dst_in = s.sb("dst_in", [P, ASLOTS, G])
        is_dst = s.sb("is_dst", [P, MASKS, G, P])
        to_edge = s.sb("to_edge", [P, MASKS, G, P])
        gathered = s.sb("gathered", [P, ASLOTS, G, GROW])
        terms = s.sb("terms", [P, ASLOTS, G, 2, HEADS])
        scores = s.sb("scores", [P, ASLOTS, G, HEADS])
        warmed = s.sb("warmed", [P, 1])
        node_ps = [s.ps(f"node_ps{u}", [P, 512]) for u in range(TILES)]
        sums_ps = [s.ps(f"sums_ps{u}", [P, 512]) for u in range(TILES)]
        acc = keep.xn

        cols_in = s.sems("cols_in", ASLOTS)
        rows_in = s.sems("rows_in", MASKS)
        row_in = s.sems("row_in", ASLOTS)
        masks_ready = s.sem("masks_ready")
        node_ready = s.sem("node_ready")
        terms_ready = s.sem("terms_ready")
        scores_ready = s.sem("scores_ready")
        p_ready = s.sem("p_ready")
        lot0_ready = s.sem("lot0_ready")
        lot1_ready = s.sem("lot1_ready")
        summed = s.sem("summed")
        added = s.sem("added")
        zeroed = s.sem("zeroed")
        order = s.sem("order")
        turn = s.sem("turn")

        def upto(i, u):
            return i * ASLOTS + u + 1

        def slot_use(i, u, slots=ASLOTS):
            return i * (ASLOTS // slots) + u // slots + 1

        class Blocks:

            def __init__(self, eng, name, back):
                self.eng, self.back = eng, back
                self.regs = registers(eng, name, ASLOTS + back)

            def load(self, i):
                back, n = self.back, len(self.regs)
                if isinstance(i, int):
                    first, n = (0, ASLOTS) if i == 0 else (i * ASLOTS - back, back)
                    entries, regs = keep.step_block[:, first:first + n], self.regs[back:] if i == 0 else self.regs[:back]
                else:
                    entries, regs = keep.step_block[:, bass.ds(i * ASLOTS - back, n)], self.regs
                if not regs:
                    return
                self.eng.load(regs, entries)
                values = [self.eng.snap(r, min_val=0, max_val=NB - 1) for r in regs]
                self.of = {u: v for u, v in zip(range(0 if isinstance(i, int) and i == 0 else -back, ASLOTS), values)}

            def __getitem__(self, u):
                return bass.ds(self.of[u], 1)

        with nc.Block() as block:

            @block.sync
            def _(sp):
                regs = registers(sp, "att_first", ASLOTS)
                with sp.Fori(0, AROUNDS) as i:
                    firsts = step_values(sp, regs, keep.step_edge, i, E)
                    for u, first in enumerate(firsts):
                        sp.wait_ge(terms_ready, upto(i, u + ASLOTS - MASKS))
                        sp.sem_inc(turn, 1)
                        sp.dma_start(cols[:, u, :, :].rearrange("p g t -> p (g t)"),
                                     keep.pair_list[bass.ds(first, STEP), :].rearrange("(p g) t -> p (g t)", g=G)
                                     ).then_inc(cols_in[u], 16)
                        sp.dma_start(rows[:, u % MASKS, :], keep.dst_list[bass.ds(first, STEP)].partition_broadcast(P)
                                     ).then_inc(rows_in[u % MASKS], 16)

            @block.gpsimd
            def _(pool):
                with pool.Fori(0, AROUNDS) as i:
                    for u in range(ASLOTS):
                        pool.wait_ge(cols_in[u], i * 16 + 16)
                        pool.wait_ge(summed, upto(i, u))
                        pool.sem_inc(turn, 1)
                        for g in range(G):
                            pool.indirect_dma_start(
                                out=gathered[:, u, g, :], out_offset=None, in_=keep.rows_dram[:, :],
                                in_offset=bass.IndirectOffsetOnAxis(ap=cols[:, u, g, 0:1], axis=0)).then_inc(row_in[u], 16)
                for u in range(ASLOTS):
                    pool.wait_ge(row_in[u], 32 * AROUNDS)

            @block.vector
            def _(dve):
                every = [P, G, P]
                dve.sem_inc(added, TILES)
                dve.memset(acc[:, :, :], 0.0).then_inc(zeroed, 1)
                dve.wait_ge(zeroed, 1)
                blocks = Blocks(dve, "att_dve", 5)

                def make_masks(i, u):
                    m = u % MASKS
                    dve.wait_ge(cols_in[u], slot_use(i, u) * 16)
                    dve.tensor_scalar(dst_in[:, u, :], cols[:, u, :, 1], keep.block_base[:, blocks[u]],
                                      None, ALU.subtract).then_inc(order, 1)
                    dve.wait_ge(rows_in[m], slot_use(i, u, MASKS) * 16)
                    dve.wait_ge(summed, upto(i, u + ASLOTS - MASKS))
                    dve.tensor_scalar(to_edge[:, m, :, :], rows[:, m, :].rearrange("p (q g) -> p g q", g=G),
                                      keep.node_id[:, blocks[u]], None, ALU.is_equal).then_inc(masks_ready, 1)
                    dve.wait_ge(order, upto(i, u))
                    dve.tensor_tensor(is_dst[:, m, :, :], spread(keep.lane[:, :].rearrange("p (g n) -> p g n", g=1), every),
                                      spread(dst_in[:, u, :].rearrange("p (g n) -> p g n", n=1), every),
                                      ALU.is_equal).then_inc(masks_ready, 1)

                def make_terms(i, u):
                    at = u % ASLOTS
                    dve.wait_ge(node_ready, upto(i, u))
                    dve.wait_ge(row_in[at], slot_use(i, u) * 32)
                    dve.tensor_tensor(terms[:, at, :, :, :].rearrange("p g t h -> p g (t h)"),
                                      node_ps[u % TILES][:, 0:G * 2 * HEADS].rearrange("p (g c) -> p g c", g=G),
                                      gathered[:, at, :, D:GROW], ALU.add).then_inc(terms_ready, 1)

                def make_scores(i, u):
                    at = u % ASLOTS
                    dve.wait_ge(terms_ready, upto(i, u) + ASLOTS)
                    dve.scalar_tensor_tensor(scores[:, at, :, :], terms[:, at, :, 0, :], 0.0, terms[:, at, :, 1, :],
                                             ALU.min, ALU.max).then_inc(scores_ready, 1)

                def weigh(i, u):
                    at = u % ASLOTS
                    dve.wait_ge(p_ready, upto(i, u))
                    row = gathered[:, at, 0, 0:D].rearrange("p (h o) -> p h o", h=HEADS)
                    dve.tensor_tensor(row, row, spread(gathered[:, at, 0, D:ROW].rearrange("p (h o) -> p h o", o=1), [P, HEADS, DO]),
                                      ALU.mult).then_inc(lot0_ready, 1)

                def add(i, u):
                    dve.wait_ge(summed, upto(i, u) + ASLOTS)
                    dve.wait_ge(added, upto(i, u) - 1 + TILES)
                    here = acc[:, blocks[u], :]
                    dve.tensor_tensor(here, sums_ps[u % TILES][:, 0:ROW].rearrange("p (b d) -> p b d", b=1), here,
                                      ALU.add).then_inc(added, 1)

                pipeline(dve, ((make_masks, 0), (make_terms, 2), (weigh, 3), (make_scores, 2), (add, 5)), blocks.load)
                dve.wait_ge(added, AROUNDS * ASLOTS + TILES)

            @block.scalar
            def _(act):
                act.activation(warmed[:, :], keep.ones[:, 0:1], ACT.Exp).then_inc(turn, 1)

                def exponentials(i, u):
                    at = u % ASLOTS
                    act.wait_ge(scores_ready, upto(i, u))
                    act.activation(gathered[:, at, :, D:ROW], scores[:, at, :, :], ACT.Exp).then_inc(p_ready, 1)

                def weigh(i, u):
                    at = u % ASLOTS
                    act.wait_ge(p_ready, upto(i, u))
                    for h in range(HEADS):
                        row = gathered[:, at, 1, h * DO:(h + 1) * DO]
                        last = act.activation(row, row, ACT.Copy, scale=gathered[:, at, 1, D + h:D + h + 1])
                    last.then_inc(lot1_ready, 1)

                pipeline(act, ((exponentials, 0), (weigh, 1)))

            @block.tensor
            def _(pe):
                pe.sem_inc(summed, ASLOTS)
                pe.sem_inc(terms_ready, ASLOTS)
                blocks = Blocks(pe, "att_pe", 0)

                def expand(i, u):
                    pe.wait_ge(masks_ready, 2 * upto(i, u) - 1)
                    pe.wait_ge(terms_ready, upto(i, u) - TILES + ASLOTS)
                    for g in range(G):
                        last = pe.matmul(node_ps[u % TILES][:, g * 2 * HEADS:(g + 1) * 2 * HEADS], to_edge[:, u % MASKS, g, :],
                                         keep.node[:, blocks[u], :].rearrange("p b c -> p (b c)"), start=True, stop=True)
                    last.then_inc(node_ready, 1)

                def total(i, u):
                    pe.wait_ge(masks_ready, 2 * upto(i, u))
                    pe.wait_ge(lot0_ready, upto(i, u))
                    pe.wait_ge(lot1_ready, upto(i, u))
                    pe.wait_ge(added, upto(i, u))
                    for g in range(G):
                        last = pe.matmul(sums_ps[u % TILES][:, 0:ROW], is_dst[:, u % MASKS, g, :], gathered[:, u % ASLOTS, g, 0:ROW],
                                         start=(g == 0), stop=(g == G - 1))
                    last.then_inc(summed, 1)

                pipeline(pe, ((expand, 0), (total, 3)), blocks.load)


SHARE = 3


def finish_attention(nc, io, keep):
    with ExitStack() as ctx:
        s = Scope(nc, ctx, "fin")
        residual = s.sb("residual", [P, 2, SB, D])
        den = s.sb("den", [P, NB, HEADS])
        stats = s.sb("stats", [P, SB, 6])
        aggr = s.sb("aggr", [P, SB, 2])
        std = s.sb("std", [P, SB])
        rstd = s.sb("rstd", [P, SB])
        offset = s.sb("offset", [P, SB])
        eps = s.sb("eps", [P, 1])
        acc, xn = keep.xn, keep.xn
        total = s.ps("total", [P, D])

        residual_in = s.sems("residual_in", 2)
        den_ready = s.sem("den_ready")
        divided = s.sem("divided")
        pool_divided = s.sem("pool_divided")
        outs_ready = s.sem("outs_ready")
        aggr_ready = s.sem("aggr_ready")
        std_ready = s.sem("std_ready")
        scales_ready = s.sem("scales_ready")
        normed = s.sem("normed")
        summed = s.sem("summed")
        order = s.sem("order")
        pause = s.sem("pause")

        def divide(eng, b):
            row = acc[:, bass.ds(b, 1), 0:D].rearrange("p b (h o) -> p (b h) o", h=HEADS)
            by = den[:, bass.ds(b, 1), :].rearrange("p b (h o) -> p (b h) o", o=1)
            return eng.tensor_tensor(row, row, spread(by, [P, HEADS, DO]), ALU.mult)

        with nc.Block() as block:

            @block.sync
            def _(sp):
                for i in range(NSB):
                    if i >= 2:
                        sp.wait_ge(outs_ready, i - 1)
                    sp.dma_start(residual[:, i % 2, :, :], keep.residual_dram[i * TOK:(i + 1) * TOK, :].rearrange("(b p) d -> p b d", p=P)
                                 ).then_inc(residual_in[i % 2], 16)

            @block.gpsimd
            def _(pool):
                pool.wait_ge(den_ready, 1)
                for i in range(NSB):
                    for b in range(i * SB + SHARE, (i + 1) * SB):
                        last = divide(pool, b)
                    last.then_inc(pool_divided, 1)
                    pool.wait_ge(pool_divided, i + 1)
                    pool.wait_ge(divided, i + 1)
                    pool.wait_ge(residual_in[i % 2], i // 2 * 16 + 16)
                    here = slice(i * SB, (i + 1) * SB)
                    pool.tensor_tensor(acc[:, here, 0:D], acc[:, here, 0:D], residual[:, i % 2, :, :], ALU.add).then_inc(outs_ready, 1)

            @block.vector
            def _(dve):
                seq = Tally(order)

                def then(instruction):
                    seq.done(instruction)
                    dve.wait_ge(order, seq.now)

                def share(i):
                    for b in range(SHARE):
                        last = divide(dve, i * SB + b)
                    last.then_inc(divided, 1)

                def super_block(i, more):
                    here = bass.ds(i * SB, SB)
                    dve.wait_ge(outs_ready, i + 1)
                    then(dve.scalar_tensor_tensor(keep.x[:, here, :], acc[:, here, 0:D], 0.0, keep.x[:, here, :], ALU.max, ALU.add))
                    dve.sem_inc(pause, 1)
                    for b in range(SB):
                        last = dve.bn_stats(stats[:, b, :], keep.x[:, bass.ds(i * SB + b, 1), :])
                    then(last)
                    dve.wait_ge(normed, i + 1)
                    dve.sem_inc(pause, 1)
                    for b in range(SB):
                        last = dve.bn_aggr(aggr[:, b, :], stats[:, b, :])
                    last.then_inc(aggr_ready, 1)
                    if more:
                        share(i + 2)
                    dve.wait_ge(std_ready, i + 1)
                    then(dve.reciprocal(rstd[:, :], std[:, :]))
                    dve.scalar_tensor_tensor(offset[:, :], aggr[:, :, 0], -1.0, rstd[:, :], ALU.mult, ALU.mult)\
                       .then_inc(scales_ready, 1)

                seq.done(dve.memset(eps[:, :], 1e-5))
                then(dve.tensor_scalar(den[:, :, :], acc[:, :, D:ROW], TINY, None, ALU.max))
                dve.reciprocal(den[:, :, :], den[:, :, :]).then_inc(den_ready, 1)
                dve.wait_ge(den_ready, 1)
                share(0)
                share(1)
                with dve.Fori(0, NSB - 2) as i:
                    seq.enter(i, 3)
                    super_block(i, more=True)
                    seq.leave(NSB - 2)
                for i in range(NSB - 2, NSB):
                    super_block(i, more=False)
                dve.wait_ge(summed, 1)
                then(dve.tensor_copy(keep.node_sum[:, :], total[:, :]))

            @block.scalar
            def _(act):
                act.sem_inc(normed, 1)
                with act.Fori(0, NSB) as i:
                    act.wait_ge(aggr_ready, i + 1)
                    act.sem_inc(pause, 1)
                    act.activation(std[:, :], aggr[:, :, 1], ACT.Sqrt, bias=eps[:, 0:1]).then_inc(std_ready, 1)
                    act.wait_ge(scales_ready, i + 1)
                    act.sem_inc(pause, 1)
                    for b in range(SB):
                        here = bass.ds(i * SB + b, 1)
                        last = act.activation(xn[:, here, 0:D], keep.x[:, here, :], ACT.Identity, bias=offset[:, b:b + 1],
                                              scale=rstd[:, b:b + 1])
                    last.then_inc(normed, 1)

            @block.tensor
            def _(pe):
                def super_block(i, first=False, last=False):
                    pe.wait_ge(normed, i + 2)
                    for b in range(SB):
                        end = last and b == SB - 1
                        rows = LAST if end else P
                        mm = pe.matmul(total[:, :], keep.ones[0:rows, :],
                                       xn[0:rows, bass.ds(i * SB + b, 1), 0:D].rearrange("p b d -> p (b d)"),
                                       start=(first and b == 0), stop=end)
                    return mm

                super_block(0, first=True)
                with pe.Fori(1, NSB - 1) as i:
                    super_block(i)
                super_block(NSB - 1, last=True).then_inc(summed, 1)


def route(nc, io, keep):
    with ExitStack() as ctx:
        s = Scope(nc, ctx, "route")
        wr = s.sb("wr", [P, KD, X1])
        br = s.sb("br", [P, X1])
        turned = s.sb("turned", [P, KD, P])
        p = s.sb("p", [P, X1])
        load = s.sb("load", [P, X1])
        scale = s.sb("scale", [P, X1])
        over = s.sb("over", [P, X1])
        left = s.sb("left", [P, X1])
        first = s.sb("first", [P, X1])
        peak = s.sb("peak", [P, TOP])
        low = s.sb("low", [P, 1])
        one = s.sb("one", [P, 1])
        gate = s.sb("gate", [P, TOP])
        chosen = s.sb("chosen", [P, TOP], I32)
        b2 = s.sb("b2", [P, TOP, D])
        ew1 = s.sb("ew1", [P, TOP, KD, F1])
        ew2 = s.sb("ew2", [P, TOP, F1 // P, D])
        turned_ps = s.ps("turned_ps", [P, KD, P])
        logits_ps = s.ps("logits_ps", [P, X1])

        params_in = s.sem("params_in")
        turned_over = s.sem("turned_over")
        turned_ready = s.sem("turned_ready")
        logits_ready = s.sem("logits_ready")
        exp_in = s.sem("exp_in")
        exp_out = s.sem("exp_out")
        chosen_ready = s.sem("chosen_ready")
        w1_in = s.sem("w1_in")
        w2_in = s.sem("w2_in")
        w1_high = s.sem("w1_high")
        w1_low = s.sem("w1_low")
        order = s.sem("order")

        with nc.Block() as block:

            @block.sync
            def _(sp):
                sp.dma_start(wr[:, :, :], io["L1_ffn_Wr"].rearrange("(k p) e -> p k e", p=P)).then_inc(params_in, 16)
                sp.dma_start(br[:, :], io["L1_ffn_br"].partition_broadcast(P)).then_inc(params_in, 16)
                sp.dma_start(keep.gamma[:, :], io["L1_ffn_gamma"].partition_broadcast(P)).then_inc(params_in, 16)
                sp.dma_start(keep.beta[:, :], io["L1_ffn_beta"].partition_broadcast(P)).then_inc(params_in, 16)
                sp.wait_ge(chosen_ready, TOP)
                regs = registers(sp, "route_expert", TOP)
                sp.load(regs, chosen[0:1, 0:TOP])
                for j, r in enumerate(regs):
                    expert = bass.ds(sp.snap(r, min_val=0, max_val=X1 - 1), 1)
                    sp.dma_start(ew1[:, j, :, :], io["L1_ffn_W1"][expert, :, :].rearrange("e (k p) f -> p (e k) f", p=P)).then_inc(w1_in, 16)
                    with nc.allow_non_contiguous_dma(reason="512 words"):
                        sp.dma_start(keep.eb1[:, j, :], io["L1_ffn_b1"][expert, :].rearrange("e (c p) -> p (e c)", p=P)).then_inc(w1_in, 16)
                    sp.dma_start(ew2[:, j, :, :], io["L1_ffn_W2"][expert, :, :].rearrange("e (c p) d -> p (e c) d", p=P)).then_inc(w2_in, 16)
                    sp.dma_start(b2[:, j, :], io["L1_ffn_b2"][expert, :].rearrange("e d -> (e d)").partition_broadcast(P)).then_inc(w2_in, 16)
                sp.wait_ge(w1_in, 32 * TOP)
                sp.wait_ge(params_in, 64)

            @block.tensor
            def _(pe):
                for k in range(KD):
                    last = pe.transpose(turned_ps[:, k, :], keep.node_sum[:, k * P:(k + 1) * P], keep.ident[:, :])
                last.then_inc(turned_over, 1)
                pe.wait_ge(turned_ready, 1)
                pe.wait_ge(params_in, 64)
                for k in range(KD):
                    last = pe.matmul(logits_ps[:, :], turned[:, k, :], wr[:, k, :], start=(k == 0), stop=(k == KD - 1))
                last.then_inc(logits_ready, 1)

            @block.gpsimd
            def _(pool):
                pool.wait_ge(w1_high, 1)
                pool.tensor_tensor(keep.ew1_parts[1][:, :, :, :].bitcast(F32R), ew1[:, :, :, :], keep.ew1_parts[0][:, :, :, :],
                                   ALU.subtract).then_inc(w1_low, 1)
                pool.wait_ge(w1_low, 1)

            @block.scalar
            def _(act):
                act.wait_ge(exp_in, 1)
                act.activation(p[:, :], left[:, :], ACT.Exp).then_inc(exp_out, 1)
                act.wait_ge(exp_in, 2)
                act.activation(p[:, :], left[:, :], ACT.Exp).then_inc(exp_out, 1)
                act.wait_ge(exp_in, 3)
                act.activation(gate[:, :], peak[:, :], ACT.Exp).then_inc(exp_out, 1)

            @block.vector
            def _(dve):
                seq = Tally(order)

                def then(instruction):
                    seq.done(instruction)
                    dve.wait_ge(order, seq.now)

                def softmax(out, x, shifted, nth):
                    then(dve.tensor_reduce(low[:, :], x, AX.X, ALU.max))
                    dve.tensor_scalar(shifted, x, low[:, 0:1], None, ALU.subtract).then_inc(exp_in, 1)
                    dve.wait_ge(exp_out, nth)
                    then(dve.tensor_reduce(low[:, :], out, AX.X, ALU.add))
                    then(dve.reciprocal(low[:, :], low[:, :]))
                    then(dve.tensor_scalar(out, out, low[:, 0:1], None, ALU.mult))

                dve.wait_ge(turned_over, 1)
                dve.tensor_scalar(turned[:, :, :], turned_ps[:, :, :], 1.0 / N, None, ALU.mult).then_inc(turned_ready, 1)
                dve.wait_ge(logits_ready, 1)
                dve.wait_ge(params_in, 64)
                then(dve.tensor_tensor(left[:, :], logits_ps[:, :], br[:, :], ALU.add))
                softmax(p[:, :], left[:, :], left[:, :], 1)
                then(dve.tensor_scalar(load[:, :], p[:, :], float(N), None, ALU.mult))
                then(dve.reciprocal(scale[:, :], load[:, :]))
                then(dve.tensor_scalar(scale[:, :], scale[:, :], CAPACITY, 1.0, ALU.mult, ALU.subtract))
                then(dve.tensor_scalar(over[:, :], load[:, :], CAPACITY, None, ALU.is_gt))
                then(dve.tensor_tensor(scale[:, :], scale[:, :], over[:, :], ALU.mult))
                then(dve.scalar_tensor_tensor(left[:, :], scale[:, :], 1.0, p[:, :], ALU.add, ALU.mult))
                softmax(p[:, :], left[:, :], left[:, :], 2)
                lanes = keep.lane[:, 0:X1]
                for j in range(TOP):
                    then(dve.tensor_reduce(peak[:, j:j + 1], p[:, :], AX.X, ALU.max))
                    then(dve.tensor_scalar(over[:, :], p[:, :], peak[:, j:j + 1], None, ALU.is_ge))
                    then(dve.scalar_tensor_tensor(first[:, :], lanes, float(X1), over[:, :], ALU.subtract, ALU.mult))
                    then(dve.tensor_reduce(one[:, :], first[:, :], AX.X, ALU.min))
                    dve.tensor_scalar(chosen[:, j:j + 1], one[:, :], float(X1), None, ALU.add).then_inc(chosen_ready, 1)
                    if j + 1 < TOP:
                        then(dve.tensor_scalar(first[:, :], first[:, :], one[:, 0:1], None, ALU.is_equal))
                        then(dve.scalar_tensor_tensor(p[:, :], first[:, :], -2.0, p[:, :], ALU.mult, ALU.add))
                softmax(gate[:, :], peak[:, :], peak[:, :], 3)
                dve.wait_ge(w1_in, 32 * TOP)
                dve.tensor_copy(keep.ew1_parts[0][:, :, :, :].bitcast(F32R), ew1[:, :, :, :]).then_inc(w1_high, 1)
                dve.wait_ge(w2_in, 32 * TOP)
                for j in range(TOP):
                    high_part, low_part, whole = keep.ew2_parts[0][:, j, :, :], keep.ew2_parts[1][:, j, :, :], ew2[:, j, :, :]
                    then(dve.tensor_scalar(whole, whole, gate[:, j:j + 1], None, ALU.mult))
                    then(dve.tensor_copy(high_part.bitcast(F32R), whole))
                    seq.done(dve.tensor_tensor(low_part.bitcast(F32R), whole, high_part, ALU.subtract))
                    seq.done(dve.tensor_scalar(b2[:, j, :], b2[:, j, :], gate[:, j:j + 1], None, ALU.mult))
                dve.wait_ge(order, seq.now)
                then(dve.tensor_tensor(keep.eb2[:, :], b2[:, 0, :], b2[:, 1, :], ALU.add))


CH = F1 // P
WIDE1 = 2 * CH


def experts(nc, io, keep):
    with ExitStack() as ctx:
        s = Scope(nc, ctx, "ex")
        tokens = s.sb("tokens", [P, SB, D])
        xt = s.sb("xt", [P, KD, TOK])
        xt_parts = [s.sb(f"xt_{n}", [P, KD, TOK]) for n in ("high", "low")]
        hidden = s.sb("hidden", [P, CH, HALF])
        h_parts = [s.sb(f"h_{n}", [P, CH, TOK]) for n in ("high", "low")]
        stats = keep.node[:, 0:SB, 0:6]
        aggr = s.sb("aggr", [P, SB, 2])
        std = s.sb("std", [P, SB])
        rstd = s.sb("rstd", [P, SB])
        eps = s.sb("eps", [P, 1])
        turn = [s.ps(f"turn{n}", [P, KD, 2 * P]) for n in range(2)]
        wide = [s.ps(f"wide{n}", [P, 512]) for n in range(CH)]
        sums = [s.ps(f"sums{n}", [P, 512]) for n in range(2)]
        xn = keep.xn

        tokens_ready = s.sem("tokens_ready")
        turned = s.sem("turned")
        xt_ready = s.sem("xt_ready")
        xt_high = s.sem("xt_high")
        xt_low = s.sem("xt_low")
        wide_full = s.sem("wide_full")
        h_ready = s.sem("h_ready")
        h_high = s.sem("h_high")
        h_low = s.sems("h_low", 2)
        sums_full = s.sem("sums_full")
        z_ready = s.sem("z_ready")
        with_bias = s.sem("with_bias")
        with_beta = s.sem("with_beta")
        aggr_ready = s.sem("aggr_ready")
        std_ready = s.sem("std_ready")
        z_normed = s.sem("z_normed")
        scaled = s.sem("scaled")
        out_ready = s.sem("out_ready")
        stored = s.sem("stored")
        order = s.sem("order")
        pause = s.sem("pause")

        def loop(eng, body):
            body(0, True, False)
            with eng.Fori(1, NSB - 1) as i:
                body(i, False, False)
            body(NSB - 1, False, True)

        def turn_cols(j):
            return slice(2 * j * P, 2 * j * P + len(turn_blocks(j)) * P)

        def half_cols(half):
            return slice(half * HALF, (half + 1) * HALF)

        with nc.Block() as block:

            @block.sync
            def _(sp):
                def body(i, first, last):
                    sp.wait_ge(out_ready, i + 1)
                    if not first and not last:
                        sp.sem_inc(pause, 1)
                    blocks = SB - 1 if last else SB
                    sp.dma_start(io["out"][bass.ds(i * TOK, blocks * P), :].rearrange("(b p) d -> p b d", p=P),
                                 keep.x[:, bass.ds(i * SB, blocks), :]).then_inc(stored, 16)

                loop(sp, body)
                sp.dma_start(io["out"][(NB - 1) * P:N, :], keep.x[0:LAST, NB - 1, :]).then_inc(stored, 16)
                sp.wait_ge(stored, 16 * (NSB + 1))

            @block.tensor
            def _(pe):
                pe.sem_inc(xt_ready, 2)
                pe.sem_inc(h_ready, CH)
                pe.sem_inc(z_ready, 2)

                def product(out, left, right, slices):
                    terms = [(l, r, k) for k in range(slices) for l, r in ((0, 0), (0, 1), (1, 0))]
                    for n, (l, r, k) in enumerate(terms):
                        last = pe.matmul(out, left(l, k).bitcast(F32R), right(r, k).bitcast(F32R),
                                         start=(n == 0), stop=(n == len(terms) - 1))
                    return last

                def turn_over(i):
                    pe.wait_ge(tokens_ready, i + 1)
                    for j in range(4):
                        pe.wait_ge(xt_ready, i * 4 + j + 1)
                        for b in turn_blocks(j):
                            for k in range(KD):
                                at0 = (b - 2 * j) * P
                                last = pe.transpose(turn[j % 2][:, k, at0:at0 + P],
                                                    tokens[:, b, k * P:(k + 1) * P], keep.ident[:, :])
                        last.then_inc(turned, 1)

                def body(i, first, last):
                    pe.wait_ge(xt_low, i * 4 + 4)
                    for e in range(TOP):
                        q = i * TOP + e
                        for half in range(2):
                            for c in range(CH):
                                pe.wait_ge(h_ready, q * WIDE1 + half * CH + c + 1)
                                product(wide[c][:, 0:HALF], lambda l, k: keep.ew1_parts[l][:, e, k, c * P:(c + 1) * P],
                                        lambda r, k: xt_parts[r][:, k, half_cols(half)], KD).then_inc(wide_full, 1)
                        if e == TOP - 1 and not last:
                            turn_over(i + 1)
                        for b in range(SB):
                            if b * P < HALF:
                                pe.wait_ge(h_low[0], (q + 1) * CH)
                            if (b + 1) * P > HALF:
                                pe.wait_ge(h_low[1], (q + 2) * CH)
                            pe.wait_ge(z_ready, q * SB + b + 1)
                            product(sums[(e * SB + b) % 2][:, 0:D], lambda l, c: h_parts[l][:, c, b * P:(b + 1) * P],
                                    lambda r, c: keep.ew2_parts[r][:, e, c, :], CH).then_inc(sums_full, 1)

                turn_over(0)
                loop(pe, body)

            @block.scalar
            def _(act):
                act.sem_inc(h_low[1], CH)

                def copy_turns(i):
                    for j in range(4):
                        act.wait_ge(turned, i * 4 + j + 1)
                        act.copy(xt[:, :, turn_cols(j)], turn[j % 2][:, :, 0:len(turn_blocks(j)) * P]).then_inc(xt_ready, 1)

                def copy_tokens(i):
                    act.sem_inc(pause, 1)
                    act.copy(tokens[:, :, :], xn[:, bass.ds(i * SB, SB), 0:D]).then_inc(tokens_ready, 1)

                def body(i, first, last):
                    if not last:
                        act.wait_ge(turned, i * 4 + 4)
                        copy_tokens(i + 1)
                    for e in range(TOP):
                        q = i * TOP + e
                        for half in range(2):
                            for c in range(CH):
                                act.wait_ge(h_low[1 - half], q * CH + c + 1)
                                act.wait_ge(wide_full, q * WIDE1 + half * CH + c + 1)
                                act.activation(hidden[:, c, :], wide[c][:, 0:HALF], ACT.Gelu,
                                               bias=keep.eb1[:, e, c:c + 1]).then_inc(h_ready, 1)
                    if not last:
                        copy_turns(i + 1)
                    act.wait_ge(aggr_ready, i + 1)
                    act.activation(std[:, :], aggr[:, :, 1], ACT.Sqrt, bias=eps[:, 0:1]).then_inc(std_ready, 1)

                copy_tokens(0)
                copy_turns(0)
                loop(act, body)

            @block.gpsimd
            def _(pool):
                wide_row = lambda ap: spread(ap.rearrange("p (b d) -> p b d", b=1), [P, SB, D])

                def super_row(tile, i):
                    return tile[:, bass.ds(i * SB, SB), 0:D]

                def split_input(i):
                    for j in range(4):
                        cols = turn_cols(j)
                        pool.wait_ge(xt_high, i * 4 + j + 1)
                        pool.tensor_tensor(xt_parts[1][:, :, cols].bitcast(F32R), xt[:, :, cols], xt_parts[0][:, :, cols],
                                           ALU.subtract).then_inc(xt_low, 1)

                def split_first_half(q):
                    for c in range(CH):
                        pool.wait_ge(h_high, q * WIDE1 + c + 1)
                        pool.tensor_tensor(h_parts[1][:, c, half_cols(0)].bitcast(F32R), hidden[:, c, :], h_parts[0][:, c, half_cols(0)],
                                           ALU.subtract).then_inc(h_low[0], 1)

                def finish(i):
                    z, x = super_row(xn, i), super_row(keep.x, i)
                    pool.wait_ge(z_normed, i + 1)
                    pool.sem_inc(pause, 1)
                    pool.tensor_tensor(z, z, wide_row(keep.gamma[:, :]), ALU.mult).then_inc(scaled, 1)
                    pool.wait_ge(scaled, i + 1)
                    pool.wait_ge(with_beta, i + 1)
                    pool.sem_inc(pause, 1)
                    pool.tensor_tensor(x, x, z, ALU.add).then_inc(out_ready, 1)

                def body(i, first, last):
                    split_first_half(i * TOP)
                    pool.wait_ge(tokens_ready, i + 1)
                    pool.sem_inc(pause, 1)
                    pool.tensor_tensor(super_row(xn, i), super_row(xn, i), wide_row(keep.eb2[:, :]), ALU.add).then_inc(with_bias, 1)
                    if not first:
                        finish(i - 1)
                    split_first_half(i * TOP + 1)
                    pool.sem_inc(pause, 1)
                    pool.tensor_tensor(super_row(keep.x, i), super_row(keep.x, i), wide_row(keep.beta[:, :]), ALU.add).then_inc(with_beta, 1)
                    if not last:
                        split_input(i + 1)

                split_input(0)
                loop(pool, body)
                finish(NSB - 1)

            @block.vector
            def _(dve):
                seq = Tally(order)

                def then(instruction):
                    seq.done(instruction)
                    dve.wait_ge(order, seq.now)

                def high(part, whole):
                    dve.sem_inc(pause, 1)
                    return dve.tensor_copy(part.bitcast(F32R), whole)

                def split_input(i):
                    for j in range(4):
                        dve.wait_ge(xt_ready, i * 4 + j + 1 + 2)
                        high(xt_parts[0][:, :, turn_cols(j)], xt[:, :, turn_cols(j)]).then_inc(xt_high, 1)

                def split_hidden(q):
                    for half in range(2):
                        cols = half_cols(half)
                        for c in range(CH):
                            t = half * CH + c
                            dve.wait_ge(h_ready, q * WIDE1 + t + 1 + CH)
                            high(h_parts[0][:, c, cols], hidden[:, c, :]).then_inc(h_high, 1)
                            if half:
                                dve.wait_ge(h_high, q * WIDE1 + t + 1)
                                dve.tensor_tensor(h_parts[1][:, c, cols].bitcast(F32R), hidden[:, c, :], h_parts[0][:, c, cols],
                                                  ALU.subtract).then_inc(h_low[1], 1)

                def body(i, first, last):
                    one = lambda b: xn[:, bass.ds(i * SB + b, 1), 0:D]

                    def z_stats(b):
                        dve.wait_ge(z_ready, (i * TOP + 1) * SB + b + 1 + 2)
                        dve.sem_inc(pause, 1)
                        seq.done(dve.bn_stats(stats[:, b, :], one(b)))

                    for e in range(TOP):
                        q = i * TOP + e
                        split_hidden(q)
                        if e == 0:
                            dve.wait_ge(with_bias, i + 1)
                        elif not last:
                            split_input(i + 1)
                        for b in range(SB):
                            dve.wait_ge(sums_full, q * SB + b + 1)
                            dve.tensor_tensor(one(b), sums[(e * SB + b) % 2][:, 0:D].rearrange("p (b d) -> p b d", b=1), one(b),
                                              ALU.add).then_inc(z_ready, 1)
                            if e == TOP - 1 and b:
                                z_stats(b - 1)
                    z_stats(SB - 1)
                    dve.wait_ge(order, seq.now)
                    dve.sem_inc(pause, 1)
                    for b in range(SB):
                        end = dve.bn_aggr(aggr[:, b, :], stats[:, b, :])
                    end.then_inc(aggr_ready, 1)
                    dve.wait_ge(std_ready, i + 1)
                    then(dve.reciprocal(rstd[:, :], std[:, :]))
                    for b in range(SB):
                        end = dve.tensor_scalar(one(b), one(b), aggr[:, b, 0:1], rstd[:, b:b + 1], ALU.subtract, ALU.mult)
                    end.then_inc(z_normed, 1)

                then(dve.memset(eps[:, :], 1e-5))
                split_input(0)
                body(0, True, False)
                with dve.Fori(1, NSB - 1) as i:
                    seq.enter(i - 1, SB + 1)
                    body(i, False, False)
                    seq.leave(NSB - 2)
                body(NSB - 1, False, True)


def program(nc, io):
    with ExitStack() as ctx:
        s = Scope(nc, ctx, "keep")
        keep = Kept()
        keep.x = s.sb("x", [P, NB, D])
        keep.step_edge = s.sb("step_edge", [1, TABLE * P], I32)
        keep.step_block = s.sb("step_block", [1, TABLE * P], I32)
        keep.lane = s.sb("lane", [P, P])
        keep.ident = s.sb("ident", [P, P])
        keep.below = s.sb("below", [P, P], BF16)
        keep.ones = s.sb("ones", [P, P])
        keep.node_id = s.sb("node_id", [P, NB])
        keep.block_base = s.sb("block_base", [P, NB])
        keep.spare_row = s.sb("spare_row", [P, 1])
        keep.node = s.sb("node", [P, NB, 2 * HEADS])
        keep.a2_bound = s.sb("a2_bound", [P, HEADS])
        keep.added = s.sems("added", LOTS)
        keep.rows_dram = nc.dram_tensor("rows_dram", [NP, GROW], F32, kind="Internal").ap()
        keep.residual_dram = nc.dram_tensor("residual_dram", [NP, D], F32, kind="Internal").ap()
        keep.src_list = nc.dram_tensor("src_list", [E + STEP], I32, kind="Internal").ap()
        keep.dst_list = nc.dram_tensor("dst_list", [E + STEP], I32, kind="Internal").ap()
        keep.pair_list = nc.dram_tensor("pair_list", [E + STEP, 2], I32, kind="Internal").ap()
        keep.table_dram = nc.dram_tensor("table_dram", [2, TABLE * P], I32, kind="Internal").ap()
        keep.partial = [nc.dram_tensor(f"partial{k}", [NP + P, D], F32, kind="Internal").ap() for k in range(SUMS)]
        with ExitStack() as ctx2:
            w = Scope(nc, ctx2, "w")
            keep.w12 = w.sb("w12", [P, KD, D])
            keep.b12 = w.sb("b12", [P, D])
            keep.wr = w.sb("wr", [P, KD, X0])
            keep.br = w.sb("br", [P, X0])
            keep.bo = w.sb("bo", [X0, D])
            keep.bn = w.sb("bn", [P, 4, 2 * X0])
            keep.proj = w.sb("proj", [P, KD, PROJ])
            with ExitStack() as ctx1:
                keep.xn = Scope(nc, ctx1, "first").sb("xn", [P, NB, ROW])
                load_and_index(nc, io, keep)
                scatter_sums(nc, io, keep)
            mixture(nc, io, keep)
        keep.xn = s.sb("acc", [P, NB, ROW])
        attend(nc, io, keep)
        with ExitStack() as ctx3:
            w = Scope(nc, ctx3, "last")
            keep.ew1_parts = [w.sb(f"ew1_{n}", [P, TOP, KD, F1]) for n in ("high", "low")]
            keep.eb1 = w.sb("eb1", [P, TOP, F1 // P])
            keep.ew2_parts = [w.sb(f"ew2_{n}", [P, TOP, F1 // P, D]) for n in ("high", "low")]
            keep.eb2 = w.sb("eb2", [P, D])
            keep.gamma = w.sb("gamma", [P, D])
            keep.beta = w.sb("beta", [P, D])
            with ExitStack() as ctx4:
                keep.node_sum = Scope(nc, ctx4, "mean").sb("node_sum", [P, D])
                finish_attention(nc, io, keep)
                route(nc, io, keep)
            experts(nc, io, keep)


def kernel(**inputs):
    import numpy as np
    import concourse.bacc as bacc
    from concourse.bass_utils import run_bass_kernel_spmd

    nc = bacc.Bacc("TRN2", target_bir_lowering=False, num_devices=1)
    io, arrays = {}, {}
    for name, value in inputs.items():
        arrays["in_" + name] = np.ascontiguousarray(value)
        io[name] = nc.dram_tensor("in_" + name, value.shape, mybir.dt.from_np(arrays["in_" + name].dtype),
                                           kind="ExternalInput").ap()
    io["out"] = nc.dram_tensor("out", [N, D], F32, kind="ExternalOutput").ap()
    program(nc, io)
    return run_bass_kernel_spmd(nc, [arrays], core_ids=[0]).results[0]["out"]
```
